# Optimizing a Trainium2 kernel written in Bass

```python
import numpy as np
import jax
import jax.numpy as jnp

def _softmax(x, axis=-1):
    return jax.nn.softmax(x, axis=axis)

def _gelu(x):
    return jax.nn.gelu(x, approximate=True)

def _silu(x):
    return jax.nn.silu(x)

def _sigmoid(x):
    return jax.nn.sigmoid(x)

def _layernorm(x, axis=-1, eps=1e-05):
    m = jnp.mean(x, axis=axis, keepdims=True)
    v = jnp.var(x, axis=axis, keepdims=True)
    return (x - m) / jnp.sqrt(v + eps)

def _scatter_add(tgt, idx, src, axis=0):
    return tgt.at[idx].add(src)

def _segment_sum(src, seg, n):
    return jax.ops.segment_sum(src, seg, n)
kernel_name = 'mk_conv_attn_hybrid_d4_conv_nchw256_r4_0a10c4'

def setup_inputs(seed: int=0):
    np.random.seed(seed)
    _w = jnp.asarray

    def _rec_inputs():
        import jax
        import jax.numpy as jnp
        _gk = jax.random.key(seed)
        x = 7.22e-05 + 1 * jax.random.normal(jax.random.fold_in(_gk, 1), (8, 64, 16, 16), jnp.float32)
        return x
    x = _rec_inputs()

    def _L0_conv_setup():
        import jax, jax.numpy as jnp
        import numpy as np
        K = 3
        STRIDE = 1
        PAD = 1
        DIL = 1
        DG = 1

        def _conv(x, w, b):
            y = jax.lax.conv_general_dilated(x, w, (STRIDE, STRIDE), [(PAD, PAD), (PAD, PAD)], dimension_numbers=('NCHW', 'OIHW', 'NCHW'))
            return y + b[None, :, None, None]

        def _dcnv2(x, offset, mask, w, b):
            B, C, H, W = x.shape
            Ho, Wo = (offset.shape[2], offset.shape[3])
            KK = K * K
            Cdg = C // DG
            off = offset.reshape(B, DG, KK, 2, Ho, Wo)
            off_y, off_x = (off[:, :, :, 0], off[:, :, :, 1])
            m = mask.reshape(B, DG, KK, Ho, Wo)
            ky = jnp.arange(KK) // K * DIL
            kx = jnp.arange(KK) % K * DIL
            base_y = jnp.arange(Ho) * STRIDE - PAD
            base_x = jnp.arange(Wo) * STRIDE - PAD
            py = (base_y[None, :, None] + ky[:, None, None]).astype(x.dtype)
            px = (base_x[None, None, :] + kx[:, None, None]).astype(x.dtype)
            sy = py[None, None] + off_y
            sx = px[None, None] + off_x
            y0 = jnp.floor(sy)
            x0 = jnp.floor(sx)
            wy = sy - y0
            wx = sx - x0
            feat = x.reshape(B, DG, Cdg, H * W)

            def corner(iy, ix):
                valid = (iy >= 0) & (iy <= H - 1) & (ix >= 0) & (ix <= W - 1)
                iyc = jnp.clip(iy, 0, H - 1).astype(jnp.int32)
                ixc = jnp.clip(ix, 0, W - 1).astype(jnp.int32)
                idx = (iyc * W + ixc).reshape(B, DG, KK * Ho * Wo)
                g = jax.vmap(jax.vmap(lambda f, i: f[:, i]))(feat, idx)
                g = g.reshape(B, DG, Cdg, KK, Ho, Wo)
                return g * valid[:, :, None].astype(x.dtype)
            one = jnp.asarray(1.0, x.dtype)
            v = corner(y0, x0) * ((one - wy) * (one - wx))[:, :, None] + corner(y0, x0 + 1) * ((one - wy) * wx)[:, :, None] + corner(y0 + 1, x0) * (wy * (one - wx))[:, :, None] + corner(y0 + 1, x0 + 1) * (wy * wx)[:, :, None]
            v = v * m[:, :, None]
            wg = w.reshape(w.shape[0], DG, Cdg, KK)
            out = jnp.einsum('bgckhw,ogck->bohw', v, wg) + b[None, :, None, None]
            return out
        key = jax.random.key(seed)
        k1, k2, k3 = jax.random.split(key, 3)
        B, C, H, W, Cout = (8, 64, 16, 16, 64)
        x = jax.random.normal(k1, (B, C, H, W), jnp.float32)
        w_off = jax.random.normal(k2, (DG * 3 * K * K, C, K, K), jnp.float32) * 0.01
        b_off = jnp.zeros((DG * 3 * K * K,), jnp.float32)
        w_dcn = jax.random.normal(k3, (Cout, C, K, K), jnp.float32) * 0.02
        b_dcn = jnp.zeros((Cout,), jnp.float32)
        return {'x': x, 'w_off': w_off, 'b_off': b_off, 'w_dcn': w_dcn, 'b_dcn': b_dcn}
    _L0_conv_all = _L0_conv_setup()
    _L0_conv_in = {k: v for k, v in _L0_conv_all.items() if k in ('w_off', 'b_off', 'w_dcn', 'b_dcn')}
    del _L0_conv_all

    def _L1_conv_setup():
        import jax, jax.numpy as jnp
        import numpy as np
        N_STREAMS = 4

        def sinkhorn_knopp(H_tilde, t_max=20):
            M = jnp.exp(H_tilde)
            for _ in range(t_max):
                M = M / jnp.sum(M, axis=-1, keepdims=True)
                M = M / jnp.sum(M, axis=-2, keepdims=True)
            return M
        key = jax.random.key(seed)
        ks = jax.random.split(key, 8)
        B, C, H, W = (32, 64, 56, 56)
        n = N_STREAMS
        nC = n * C
        n_out = 2 * n + n * n
        x = jax.random.normal(ks[0], (B, C, H, W), dtype=jnp.float32)
        phi_w = jax.random.normal(ks[1], (n_out, nC), dtype=jnp.float32) * (1.0 / np.sqrt(nC))
        phi_b = jax.random.normal(ks[2], (n_out,), dtype=jnp.float32) * 0.01
        rms_w = jnp.ones((nC,), dtype=jnp.float32)
        alpha_pre = jnp.full((1,), 0.01, dtype=jnp.float32)
        alpha_post = jnp.full((1,), 0.01, dtype=jnp.float32)
        alpha_res = jnp.full((1,), 0.01, dtype=jnp.float32)
        conv_w = jax.random.normal(ks[3], (C, C, 3, 3), dtype=jnp.float32) * (1.0 / np.sqrt(C * 9))
        conv_b = jax.random.normal(ks[4], (C,), dtype=jnp.float32) * 0.01
        return {'x': x, 'phi_w': phi_w, 'phi_b': phi_b, 'rms_w': rms_w, 'alpha_pre': alpha_pre, 'alpha_post': alpha_post, 'alpha_res': alpha_res, 'conv_w': conv_w, 'conv_b': conv_b}
    _L1_conv_all = _L1_conv_setup()
    _L1_conv_in = {k: v for k, v in _L1_conv_all.items() if k in ('phi_w', 'phi_b', 'rms_w', 'alpha_pre', 'alpha_post', 'alpha_res', 'conv_w', 'conv_b')}
    del _L1_conv_all

    def _L2_attn_setup():
        import jax, jax.numpy as jnp
        import numpy as np
        B, N, C, H = (4, 512, 64, 8)
        SCALE = C ** (-0.5)
        key = jax.random.key(seed)
        k1, k2, k3 = jax.random.split(key, 3)
        x = jax.random.normal(k1, (B, N, C), dtype=jnp.float32)
        w_qkv = jax.random.normal(k2, (C, 3 * H * C), dtype=jnp.float32) * C ** (-0.5)
        w_proj = jax.random.normal(k3, (H * C, C), dtype=jnp.float32) * (H * C) ** (-0.5)
        b_proj = jnp.zeros((C,), dtype=jnp.float32)
        return {'x': x, 'w_qkv': w_qkv, 'w_proj': w_proj, 'b_proj': b_proj}
    _L2_attn_all = _L2_attn_setup()
    _L2_attn_in = {k: v for k, v in _L2_attn_all.items() if k in ('w_qkv', 'w_proj', 'b_proj')}
    del _L2_attn_all

    def _L2_ffn_setup():
        import jax, jax.numpy as jnp
        import numpy as np
        TOP_K = 2
        key = jax.random.key(seed)
        ks = jax.random.split(key, 4)
        B, L, D, H, E = (8, 1024, 64, 256, 8)
        s = 0.02
        return {'x': jax.random.normal(ks[0], (B, L, D), jnp.float32), 'Wg': jax.random.normal(ks[1], (D, E), jnp.float32) * s, 'bg': jnp.zeros((E,), jnp.float32), 'W1': jax.random.normal(ks[2], (E, D, H), jnp.float32) * s, 'b1': jnp.zeros((E, H), jnp.float32), 'W2': jax.random.normal(ks[3], (E, H, D), jnp.float32) * s, 'b2': jnp.zeros((E, D), jnp.float32)}
    _L2_ffn_all = _L2_ffn_setup()
    _L2_ffn_in = {k: v for k, v in _L2_ffn_all.items() if k in ('Wg', 'bg', 'W1', 'b1', 'W2', 'b2')}
    del _L2_ffn_all

    def _L3_attn_setup():
        import jax, jax.numpy as jnp
        import numpy as np
        ATTWSIZE = 16

        def _windowed_sum(v, w):
            cs = jnp.cumsum(v, axis=1)
            T = v.shape[1]
            shifted = jnp.pad(cs, ((0, 0), (w, 0), (0, 0)))[:, :T, :]
            return cs - shifted
        key = jax.random.key(seed)
        k1, k2, k3 = jax.random.split(key, 3)
        B, T, D, A = (32, 1024, 64, 32)
        x = jax.random.normal(k1, (B, T, D), dtype=jnp.float32)
        Wp = jax.random.normal(k2, (A, D), dtype=jnp.float32) / np.sqrt(D).astype(np.float32)
        bp = jnp.zeros((A,), dtype=jnp.float32)
        Wg = jax.random.normal(k3, (1, A), dtype=jnp.float32) / np.sqrt(A).astype(np.float32)
        return {'x': x, 'Wp': Wp, 'bp': bp, 'Wg': Wg}
    _L3_attn_all = _L3_attn_setup()
    _L3_attn_in = {k: v for k, v in _L3_attn_all.items() if k in ('Wp', 'bp', 'Wg')}
    del _L3_attn_all

    def _L3_ffn_setup():
        import jax, jax.numpy as jnp
        import numpy as np
        D_MODEL = 64
        N_EXPERTS = 16
        HIDDEN = 128
        SCALE = 0.02
        key = jax.random.key(seed)
        ks = jax.random.split(key, 5)
        x = jax.random.normal(ks[0], (4, 2048, D_MODEL), dtype=jnp.float32)
        gate_w = jax.random.normal(ks[1], (D_MODEL, N_EXPERTS), dtype=jnp.float32) * SCALE
        gate_b = jnp.zeros((N_EXPERTS,), dtype=jnp.float32)
        w1 = jax.random.normal(ks[2], (N_EXPERTS, D_MODEL, HIDDEN), dtype=jnp.float32) * SCALE
        w2 = jax.random.normal(ks[3], (N_EXPERTS, D_MODEL, HIDDEN), dtype=jnp.float32) * SCALE
        w3 = jax.random.normal(ks[4], (N_EXPERTS, HIDDEN, D_MODEL), dtype=jnp.float32) * SCALE
        return {'x': x, 'gate_w': gate_w, 'gate_b': gate_b, 'w1': w1, 'w2': w2, 'w3': w3}
    _L3_ffn_all = _L3_ffn_setup()
    _L3_ffn_in = {k: v for k, v in _L3_ffn_all.items() if k in ('gate_w', 'gate_b', 'w1', 'w2', 'w3')}
    del _L3_ffn_all
    return {'x': x, 'L0_conv_w_off': _L0_conv_in['w_off'], 'L0_conv_b_off': _L0_conv_in['b_off'], 'L0_conv_w_dcn': _L0_conv_in['w_dcn'], 'L0_conv_b_dcn': _L0_conv_in['b_dcn'], 'L1_conv_phi_w': _L1_conv_in['phi_w'], 'L1_conv_phi_b': _L1_conv_in['phi_b'], 'L1_conv_rms_w': _L1_conv_in['rms_w'], 'L1_conv_alpha_pre': _L1_conv_in['alpha_pre'], 'L1_conv_alpha_post': _L1_conv_in['alpha_post'], 'L1_conv_alpha_res': _L1_conv_in['alpha_res'], 'L1_conv_conv_w': _L1_conv_in['conv_w'], 'L1_conv_conv_b': _L1_conv_in['conv_b'], 'L2_attn_w_qkv': _L2_attn_in['w_qkv'], 'L2_attn_w_proj': _L2_attn_in['w_proj'], 'L2_attn_b_proj': _L2_attn_in['b_proj'], 'L2_ffn_Wg': _L2_ffn_in['Wg'], 'L2_ffn_bg': _L2_ffn_in['bg'], 'L2_ffn_W1': _L2_ffn_in['W1'], 'L2_ffn_b1': _L2_ffn_in['b1'], 'L2_ffn_W2': _L2_ffn_in['W2'], 'L2_ffn_b2': _L2_ffn_in['b2'], 'L3_attn_Wp': _L3_attn_in['Wp'], 'L3_attn_bp': _L3_attn_in['bp'], 'L3_attn_Wg': _L3_attn_in['Wg'], 'L3_ffn_gate_w': _L3_ffn_in['gate_w'], 'L3_ffn_gate_b': _L3_ffn_in['gate_b'], 'L3_ffn_w1': _L3_ffn_in['w1'], 'L3_ffn_w2': _L3_ffn_in['w2'], 'L3_ffn_w3': _L3_ffn_in['w3']}

def reference(x, L0_conv_w_off, L0_conv_b_off, L0_conv_w_dcn, L0_conv_b_dcn, L1_conv_phi_w, L1_conv_phi_b, L1_conv_rms_w, L1_conv_alpha_pre, L1_conv_alpha_post, L1_conv_alpha_res, L1_conv_conv_w, L1_conv_conv_b, L2_attn_w_qkv, L2_attn_w_proj, L2_attn_b_proj, L2_ffn_Wg, L2_ffn_bg, L2_ffn_W1, L2_ffn_b1, L2_ffn_W2, L2_ffn_b2, L3_attn_Wp, L3_attn_bp, L3_attn_Wg, L3_ffn_gate_w, L3_ffn_gate_b, L3_ffn_w1, L3_ffn_w2, L3_ffn_w3):
    import jax
    import jax.numpy as jnp

    def _L0_conv_ref(x, w_off, b_off, w_dcn, b_dcn):
        import jax, jax.numpy as jnp
        import numpy as np
        K = 3
        STRIDE = 1
        PAD = 1
        DIL = 1
        DG = 1

        def _conv(x, w, b):
            y = jax.lax.conv_general_dilated(x, w, (STRIDE, STRIDE), [(PAD, PAD), (PAD, PAD)], dimension_numbers=('NCHW', 'OIHW', 'NCHW'))
            return y + b[None, :, None, None]

        def _dcnv2(x, offset, mask, w, b):
            B, C, H, W = x.shape
            Ho, Wo = (offset.shape[2], offset.shape[3])
            KK = K * K
            Cdg = C // DG
            off = offset.reshape(B, DG, KK, 2, Ho, Wo)
            off_y, off_x = (off[:, :, :, 0], off[:, :, :, 1])
            m = mask.reshape(B, DG, KK, Ho, Wo)
            ky = jnp.arange(KK) // K * DIL
            kx = jnp.arange(KK) % K * DIL
            base_y = jnp.arange(Ho) * STRIDE - PAD
            base_x = jnp.arange(Wo) * STRIDE - PAD
            py = (base_y[None, :, None] + ky[:, None, None]).astype(x.dtype)
            px = (base_x[None, None, :] + kx[:, None, None]).astype(x.dtype)
            sy = py[None, None] + off_y
            sx = px[None, None] + off_x
            y0 = jnp.floor(sy)
            x0 = jnp.floor(sx)
            wy = sy - y0
            wx = sx - x0
            feat = x.reshape(B, DG, Cdg, H * W)

            def corner(iy, ix):
                valid = (iy >= 0) & (iy <= H - 1) & (ix >= 0) & (ix <= W - 1)
                iyc = jnp.clip(iy, 0, H - 1).astype(jnp.int32)
                ixc = jnp.clip(ix, 0, W - 1).astype(jnp.int32)
                idx = (iyc * W + ixc).reshape(B, DG, KK * Ho * Wo)
                g = jax.vmap(jax.vmap(lambda f, i: f[:, i]))(feat, idx)
                g = g.reshape(B, DG, Cdg, KK, Ho, Wo)
                return g * valid[:, :, None].astype(x.dtype)
            one = jnp.asarray(1.0, x.dtype)
            v = corner(y0, x0) * ((one - wy) * (one - wx))[:, :, None] + corner(y0, x0 + 1) * ((one - wy) * wx)[:, :, None] + corner(y0 + 1, x0) * (wy * (one - wx))[:, :, None] + corner(y0 + 1, x0 + 1) * (wy * wx)[:, :, None]
            v = v * m[:, :, None]
            wg = w.reshape(w.shape[0], DG, Cdg, KK)
            out = jnp.einsum('bgckhw,ogck->bohw', v, wg) + b[None, :, None, None]
            return out
        om = _conv(x, w_off, b_off)
        o1, o2, mask = jnp.split(om, 3, axis=1)
        offset = jnp.concatenate([o1, o2], axis=1)
        mask = jax.nn.sigmoid(mask)
        return _dcnv2(x, offset, mask, w_dcn, b_dcn)

    def _L1_conv_ref(x, phi_w, phi_b, rms_w, alpha_pre, alpha_post, alpha_res, conv_w, conv_b):
        import jax, jax.numpy as jnp
        import numpy as np
        N_STREAMS = 4

        def sinkhorn_knopp(H_tilde, t_max=20):
            M = jnp.exp(H_tilde)
            for _ in range(t_max):
                M = M / jnp.sum(M, axis=-1, keepdims=True)
                M = M / jnp.sum(M, axis=-2, keepdims=True)
            return M
        n = N_STREAMS
        B, C, H, W = x.shape
        nC = n * C
        x_l = jnp.broadcast_to(x[:, None], (B, n, C, H, W))
        x_pooled = jnp.mean(x_l.reshape(B, nC, H, W), axis=(2, 3))
        x_norm = x_pooled * jax.lax.rsqrt(jnp.mean(x_pooled * x_pooled, axis=-1, keepdims=True) + 1e-20) * rms_w
        coeffs = x_norm @ phi_w.T + phi_b
        H_pre = jax.nn.sigmoid(alpha_pre * coeffs[:, :n])
        H_post = 2.0 * jax.nn.sigmoid(alpha_post * coeffs[:, n:2 * n])
        H_res = sinkhorn_knopp(alpha_res * coeffs[:, 2 * n:].reshape(B, n, n))
        h_in = jnp.einsum('bn,bnchw->bchw', H_pre, x_l)
        h_out = jax.lax.conv_general_dilated(h_in, conv_w, (1, 1), 'SAME', dimension_numbers=('NCHW', 'OIHW', 'NCHW'))
        h_out = h_out + conv_b[None, :, None, None]
        post_part = jnp.einsum('bn,bchw->bnchw', H_post, h_out)
        res_part = jnp.einsum('bnn,bnchw->bnchw', H_res, x_l)
        return jnp.mean(res_part + post_part, axis=1)

    def _L2_attn_ref(x, w_qkv, w_proj, b_proj):
        import jax, jax.numpy as jnp
        import numpy as np
        B, N, C, H = (4, 512, 64, 8)
        SCALE = C ** (-0.5)
        b, n, c = x.shape
        qkv = (x @ w_qkv).reshape(b, n, 3, H, c)
        qkv = jnp.transpose(qkv, (2, 0, 3, 1, 4))
        q, k, v = (qkv[0], qkv[1], qkv[2])
        attn = jnp.einsum('bhqc,bhkc->bhqk', q, k) * SCALE
        causal_mask = jnp.triu(jnp.ones((n, n), dtype=bool), k=1)
        attn = jnp.where(causal_mask, -jnp.inf, attn)
        attn = jax.nn.softmax(attn, axis=-1)
        out = jnp.einsum('bhqk,bhkc->bhqc', attn, v)
        out = jnp.transpose(out, (0, 2, 1, 3)).reshape(b, n, H * c)
        return out @ w_proj + b_proj

    def _L2_ffn_ref(x, Wg, bg, W1, b1, W2, b2):
        import jax, jax.numpy as jnp
        import numpy as np
        TOP_K = 2
        B, L, D = x.shape
        E = W1.shape[0]
        xf = x.reshape(-1, D)
        gate_logits = xf @ Wg + bg
        top_w, top_i = jax.lax.top_k(gate_logits, TOP_K)
        top_w = jax.nn.softmax(top_w, axis=-1)
        w_dense = jnp.sum(jax.nn.one_hot(top_i, E, dtype=xf.dtype) * top_w[..., None], axis=1)
        out = jnp.zeros_like(xf)
        for e in range(E):
            h = jax.nn.gelu(xf @ W1[e] + b1[e], approximate=False)
            out = out + w_dense[:, e:e + 1] * (h @ W2[e] + b2[e])
        return out.reshape(B, L, D)

    def _L3_attn_ref(x, Wp, bp, Wg):
        import jax, jax.numpy as jnp
        import numpy as np
        ATTWSIZE = 16

        def _windowed_sum(v, w):
            cs = jnp.cumsum(v, axis=1)
            T = v.shape[1]
            shifted = jnp.pad(cs, ((0, 0), (w, 0), (0, 0)))[:, :T, :]
            return cs - shifted
        proj = jnp.tanh(jnp.einsum('btd,ad->bta', x, Wp) + bp)
        g = jax.nn.sigmoid(jnp.einsum('bta,oa->bto', proj, Wg))
        wx = g * x
        num = _windowed_sum(wx, ATTWSIZE)
        den = _windowed_sum(g, ATTWSIZE)
        return num / den

    def _L3_ffn_ref(x, gate_w, gate_b, w1, w2, w3):
        import jax, jax.numpy as jnp
        import numpy as np
        D_MODEL = 64
        N_EXPERTS = 16
        HIDDEN = 128
        SCALE = 0.02
        n_experts = w1.shape[0]
        logits = jnp.einsum('bsd,de->bse', x, gate_w) + gate_b
        probs = jax.nn.softmax(logits, axis=-1)
        top_probs, top_idx = jax.lax.top_k(probs, 2)
        top_probs = top_probs / jnp.sum(top_probs, axis=-1, keepdims=True)
        dispatch = jnp.sum(jax.nn.one_hot(top_idx, n_experts, dtype=x.dtype) * top_probs[..., None], axis=-2)
        h1 = jnp.einsum('bsd,edh->bseh', x, w1)
        h2 = jnp.einsum('bsd,edh->bseh', x, w2)
        hidden = jax.nn.silu(h1) * h2
        expert_out = jnp.einsum('bseh,eho->bseo', hidden, w3)
        return jnp.einsum('bseo,bse->bso', expert_out, dispatch)

    def _gn(v, G=32, eps=1e-05):
        B_, C_, H_, W_ = v.shape
        g = v.reshape(B_, G, C_ // G, H_, W_)
        m = jnp.mean(g, axis=(2, 3, 4), keepdims=True)
        s = jnp.var(g, axis=(2, 3, 4), keepdims=True)
        return ((g - m) / jnp.sqrt(s + eps)).reshape(v.shape)

    def _ln_c(v, eps=1e-06):
        m = jnp.mean(v, axis=1, keepdims=True)
        s = jnp.var(v, axis=1, keepdims=True)
        return (v - m) / jnp.sqrt(s + eps)

    def _ln_t(v, eps=1e-05):
        m = jnp.mean(v, axis=-1, keepdims=True)
        s = jnp.var(v, axis=-1, keepdims=True)
        return (v - m) / jnp.sqrt(s + eps)

    def _to_tokens(v):
        B_, C_, H_, W_ = v.shape
        return v.reshape(B_, C_, H_ * W_).transpose(0, 2, 1)

    def _from_tokens(t, like):
        B_, C_, H_, W_ = like.shape
        return t.transpose(0, 2, 1).reshape(B_, C_, H_, W_)
    x = x + _L0_conv_ref(_gn(x), L0_conv_w_off, L0_conv_b_off, L0_conv_w_dcn, L0_conv_b_dcn)
    x = x + _L1_conv_ref(_gn(x), L1_conv_phi_w, L1_conv_phi_b, L1_conv_rms_w, L1_conv_alpha_pre, L1_conv_alpha_post, L1_conv_alpha_res, L1_conv_conv_w, L1_conv_conv_b)
    t = _to_tokens(x)
    t = t + _L2_attn_ref(_ln_t(t), L2_attn_w_qkv, L2_attn_w_proj, L2_attn_b_proj)
    t = t + _L2_ffn_ref(_ln_t(t), L2_ffn_Wg, L2_ffn_bg, L2_ffn_W1, L2_ffn_b1, L2_ffn_W2, L2_ffn_b2)
    t = t + _L3_attn_ref(_ln_t(t), L3_attn_Wp, L3_attn_bp, L3_attn_Wg)
    t = t + _L3_ffn_ref(_ln_t(t), L3_ffn_gate_w, L3_ffn_gate_b, L3_ffn_w1, L3_ffn_w2, L3_ffn_w3)
    x = _from_tokens(t, x)
    return x

_drawn_inputs = setup_inputs


def setup_inputs(seed=0):
    import zlib

    import numpy as np

    out = dict(_drawn_inputs(seed))
    spreads = {'L0_conv_b_off': (0.0, 0.294),
     'L0_conv_b_dcn': (0.0, 0.1),
     'L1_conv_rms_w': (1.0, 0.6),
     'L2_attn_b_proj': (0.0, 0.1),
     'L2_ffn_bg': (0.0, 0.1),
     'L2_ffn_b1': (0.0, 0.8),
     'L2_ffn_b2': (0.0, 0.1),
     'L3_attn_bp': (0.0, 0.8),
     'L3_ffn_gate_b': (0.0, 0.8)}
    factors = {'L1_conv_phi_w': 8.0,
     'L1_conv_phi_b': 8.0,
     'L1_conv_conv_b': 8.0,
     'L2_ffn_W1': 7.2,
     'L2_ffn_W2': 5.82,
     'L3_ffn_gate_w': 8.0,
     'L3_ffn_w1': 8.0,
     'L3_ffn_w2': 8.0,
     'L3_ffn_w3': 8.0}
    for name, (base, spread) in spreads.items():
        noise = np.random.default_rng([zlib.crc32(name.encode()), seed]).standard_normal(out[name].shape)
        drawn = base * np.exp(spread * noise) if base else spread * noise
        out[name] = jnp.asarray(drawn.astype(out[name].dtype))
    for name, factor in factors.items():
        out[name] = (out[name] * factor).astype(out[name].dtype)
    return out
```

```python
from contextlib import ExitStack

import numpy as np

import concourse.bass as bass
from concourse import mybir

ALU = mybir.AluOpType
ACT = mybir.ActivationFunctionType
AX = mybir.AxisListType
F32 = mybir.dt.float32

B, C, HH, WW = 8, 64, 16, 16
S = HH * WW
P = 128
J = B // 2
PT = S // P
NP = J * PT
NT = 2 * NP
TAPS = 9
NOFF = 3 * TAPS
PADW = WW + 2
STREAMS = 4
NPHI = 2 * STREAMS + STREAMS * STREAMS
SINKHORN = 20
HEADS = 8
HPAIRS = HEADS // 2
SCALE = float(C) ** -0.5
E2, HID2 = 8, 256
E3, HID3 = 16, 128
A3 = 32
WINDOW = 16
NEG = -1e30
EPS5 = 1e-5


def layout(*fields):
    at, where = 0, {}
    for name, width in fields:
        where[name] = slice(at, at + width)
        at += width
    return where, at


CONST, NCONST = layout(("ident", P), ("pair_mean", P), ("half_mean", P), ("base", PT * 2 * TAPS), ("grid", WW),
                       ("causal", 2 * P), ("band", P), ("band_prev", P), ("sel_half", P), ("sel_image", J),
                       ("desc", E3), ("tile_rows", NT))
W64, NW64 = layout(("w_off", TAPS * NOFF), ("w_conv", TAPS * C), ("w_dcn", TAPS * C), ("conv_b", 1), ("b_dcn", 1), ("phi", STREAMS * NPHI),
                   ("rms", STREAMS), ("qkv", 3 * HEADS * C), ("wg2", E2), ("wp", A3), ("wg3", E3),
                   ("w1_2", E2 * HID2), ("w1_3", E3 * HID3), ("w2_3", E3 * HID3))
W128, NW128 = layout(("proj", 4 * C), ("b1", 2 * E2), ("w2_2", 2 * E2 * C), ("w3", E3 * C))
ROWS, NROWS = layout(("b_off", NOFF), ("b_proj", C), ("bg2", E2), ("bp", A3), ("wg", A3), ("bg3", E3),
                     ("phi_b", NPHI), ("alpha", 3))


def shape_constants():
    c = np.zeros((P, NCONST), np.float32)
    p = np.arange(P)
    c[:, CONST["ident"]] = np.eye(P)
    c[:, CONST["pair_mean"]] = (p[:, None] // 2 == p[None] // 2) * 0.5
    c[:, CONST["half_mean"]] = (p[:, None] // C == p[None] // C) / C
    base = np.zeros((P, PT, TAPS, 2), np.float32)
    for pt in range(PT):
        s = pt * P + p
        for k in range(TAPS):
            base[:, pt, k, 0] = s // WW - 1 + k // 3
            base[:, pt, k, 1] = s % WW - 1 + k % 3
    c[:, CONST["base"]] = base.reshape(P, -1)
    c[:, CONST["grid"]] = np.arange(WW)
    c[:, CONST["causal"]] = np.concatenate([np.zeros((P, P)), np.where(p[None] <= p[:, None], 0.0, NEG)], 1)
    c[:, CONST["band"]] = (p[:, None] <= p[None]) & (p[:, None] > p[None] - WINDOW)
    c[:, CONST["band_prev"]] = p[:, None] - P > p[None] - WINDOW
    c[:B, CONST["sel_half"]] = np.arange(B)[:, None] // J == p[None] // C
    c[:B, CONST["sel_image"]] = np.arange(B)[:, None] % J == np.arange(J)[None]
    c[:, CONST["desc"]] = E3 - np.arange(E3)
    c[:, CONST["tile_rows"]] = p[:, None] // E2 == np.arange(NT)[None]
    return c


def hybrid_kernel(nc, x, w64, w128, rows, b2, consts, out):
    with ExitStack() as ctx:
        def sb(name, *shape):
            return ctx.enter_context(nc.sbuf_tensor(name, [P, *shape], F32))

        def sem(name):
            return ctx.enter_context(nc.semaphore(name))

        PS = ctx.enter_context(nc.psum_tensor("PS", [P, 8, 512], F32))

        cst = sb("cst", NCONST)
        wc = sb("wc", NW64)
        wk = sb("wk", NW128)
        rw = sb("rw", NROWS)
        b2rep = sb("b2rep", C)
        b2blk = sb("b2blk", NT, C)
        arena = sb("arena", 24576)
        score_arena = sb("score_arena", 3 * 4 * 384)
        w_off = score_arena[:, 2592:3078].rearrange("p (k n) -> p k n", k=TAPS)
        w_conv = score_arena[:, 3078:4230].rearrange("p (k n) -> p k n", k=TAPS)
        X = sb("X", J, S)
        X1 = sb("X1", J, S)
        G = arena[:, 18432:18432 + 3 * J * PADW * WW].rearrange("p (k j y x) -> p k j y x", k=3, j=J, y=PADW)
        G2 = score_arena[:, 1296:2592].rearrange("p (j y x) -> p j y x", j=J, y=PADW)
        stat = sb("stat", J, 6)
        mv = sb("mv", 2, J, 2)
        gmv = sb("gmv", J, 2)
        small = sb("small", 64)
        T = sb("T", NT, C)
        Y = sb("Y", NT, C)
        Z = sb("Z", NT, C)
        YT = sb("YT", NP, P)
        lnst = sb("lnst", 4, NT)
        coord = sb("coord", NT, 2 * TAPS)
        mask = sb("mask", NT, TAPS)
        hats = arena[:, 0:4608].rearrange("p (t k q) -> p t k q", t=NT, k=2 * TAPS)
        U = arena[:, 4608:4608 + NT * TAPS * C].rearrange("p (t n) -> p t n", t=NT)
        prod = arena[:, 13824:13824 + 2304].rearrange("p (k q) -> p k q", k=TAPS)
        prod2 = arena[:, 16128:16128 + 2304].rearrange("p (k q) -> p k q", k=TAPS)
        prods = [prod, prod2]
        ST = [arena[:, o:o + 2304].rearrange("p (k q) -> p k q", q=P) for o in (18432, 20736)]
        D = sb("D", 2, P)
        weff = sb("weff", NPHI)
        phr = sb("phr", STREAMS, NPHI)
        PB = sb("PB", B)
        cf = sb("cf", NPHI)
        M = sb("M", STREAMS, STREAMS)
        mn = sb("mn", STREAMS)
        V = sb("V", 4)
        V3 = sb("V3", J, 3)
        CB = sb("CB", J, 3)
        bb = sb("bb", J)
        QK = arena[:, 0:B * HPAIRS * 2 * S].rearrange("p (b h n) -> p b h n", b=B, h=HPAIRS)
        VV = arena[:, 16384:24576].rearrange("p (t n) -> p t n", t=NT)
        MS, PR, PTs = (score_arena[:, o * 1536:(o + 1) * 1536].rearrange("p (u n) -> p u n", u=4) for o in range(3))
        nmx = sb("nmx", 4, 2)
        rsum = sb("rsum", 2, PT, HEADS)
        rinv = sb("rinv", 2, PT, HEADS)
        ON = sb("ON", PT, HEADS * C)
        OT = sb("OT", PT, HEADS * C)
        moe_at = [0]

        def later(*shape):
            n = int(np.prod(shape))
            moe_at[0] += n
            piece = arena[:, moe_at[0] - n:moe_at[0]]
            names = " ".join("abc"[:len(shape)])
            return piece if len(shape) == 1 else piece.rearrange(f"p ({names}) -> p {names}", **dict(zip("abc", shape)))

        tg = later(8, NT * E3)
        gate = sb("gate", NT, E3)
        gateT = later(P)
        hid = later(3, 2, 256)
        sil = later(2, 2, 256)
        pr8 = later(2, E2 * C)
        part = later(2, C)
        PJ = later(NT, A3)
        WX = later(NT, C + 1)

        def c_(name):
            return cst[:, CONST[name]]

        def w_(name, h=None):
            return wc[:, W64[name]] if h is None else wc[h * C:(h + 1) * C, W64[name]]

        ident = c_("ident")

        def img(t):
            return t[:].rearrange("p j (y x) -> p j y x", y=HH)

        x_loaded = sem("x_loaded")
        const_loaded = sem("const_loaded")
        rows_loaded = sem("rows_loaded")
        w_early_loaded = sem("w_early_loaded")
        w_late_loaded = sem("w_late_loaded")
        block_zeroed = sem("block_zeroed")
        off_block_loaded = sem("off_block_loaded")
        conv_block_loaded = sem("conv_block_loaded")
        b2_loaded = sem("b2_loaded")
        pads_zeroed = sem("pads_zeroed")
        b2blk_ready = sem("b2blk_ready")
        dve_step = sem("dve_step")
        act_step = sem("act_step")
        moments_ready = sem("moments_ready")
        group_moments_ready = sem("group_moments_ready")
        var_ready = sem("var_ready")
        sd_ready = sem("sd_ready")
        norm_ready = sem("norm_ready")
        g_ready = sem("g_ready")
        g_shifted_ready = sem("g_shifted_ready")
        offsets_ready = sem("offsets_ready")
        mask_logits_ready = sem("mask_logits_ready")
        mask_ready = sem("mask_ready")
        hat_diff_ready = sem("hat_diff_ready")
        hat_ready = sem("hat_ready")
        u_ready = sem("u_ready")
        u_copied = sem("u_copied")
        prod_ready = sem("prod_ready")
        st_ready = sem("st_ready")
        st_copied = sem("st_copied")
        d_ready = sem("d_ready")
        d_copied = sem("d_copied")
        dT_ready = sem("dT_ready")
        x1_tile_ready = sem("x1_tile_ready")
        sq_ready = sem("sq_ready")
        q_ready = sem("q_ready")
        qe_ready = sem("qe_ready")
        qs_ready = sem("qs_ready")
        pb_ready = sem("pb_ready")
        coef_ready = sem("coef_ready")
        logits_ready = sem("logits_ready")
        gates_ready = sem("gates_ready")
        v3_ready = sem("v3_ready")
        cb_ready = sem("cb_ready")
        conv_ready = sem("conv_ready")
        x2_ready = sem("x2_ready")
        t_ready = sem("t_ready")
        y_ready = sem("y_ready")
        yT_ready = sem("yT_ready")
        yT_copied_act = sem("yT_copied_act")
        yT_copied_dve = sem("yT_copied_dve")
        qkv_ready = sem("qkv_ready")
        qkv_copied_act = sem("qkv_copied_act")
        qkv_copied_dve = sem("qkv_copied_dve")
        scores_ready = sem("scores_ready")
        masked_ready = sem("masked_ready")
        probs_ready = sem("probs_ready")
        bank4_filled = sem("bank4_filled")
        bank4_free = sem("bank4_free")
        bank5_filled = sem("bank5_filled")
        bank5_free = sem("bank5_free")
        pv_done = sem("pv_done")
        heads_normed = sem("heads_normed")
        gate_logits_ready = sem("gate_logits_ready")
        gate_exp_ready = sem("gate_exp_ready")
        gate_diff_ready = sem("gate_diff_ready")
        gate_ready = sem("gate_ready")
        gateT_ready = sem("gateT_ready")
        gateT_copied = sem("gateT_copied")
        b2_term_ready = sem("b2_term_ready")
        hid2_ready = sem("hid2_ready")
        gelu_done = sem("gelu_done")
        out2_done = sem("out2_done")
        acc2_free = sem("acc2_free")
        proj_ready = sem("proj_ready")
        pj_ready = sem("pj_ready")
        tanh_done = sem("tanh_done")
        glogit_ready = sem("glogit_ready")
        g3_ready = sem("g3_ready")
        wx_ready = sem("wx_ready")
        window_ready = sem("window_ready")
        hid3_ready = sem("hid3_ready")
        silu_done = sem("silu_done")
        prod3_done = sem("prod3_done")
        out3_done = sem("out3_done")
        acc3_free = sem("acc3_free")
        final_ready = sem("final_ready")
        finalT_ready = sem("finalT_ready")
        o_lower_ready = sem("o_lower_ready")
        o_upper_ready = sem("o_upper_ready")
        stored = sem("stored")

        LATE = slice(W64["phi"].start, NW64)
        EARLY = slice(0, W64["phi"].start)
        STG = (4, 4, 4, 4, 2)
        NG = len(STG)
        NS = B * HPAIRS

        def n4_probs(v):
            return v + 1 + max(0, (v - 2) // 4)

        def n4_heads(b):
            return min(4 * b + 6, NS) + b + 1

        def n5_probs(v):
            return v + 1 + max(0, (v - 2) // 4) + max(0, (v - 3) // 4)

        def n5_heads(b):
            return min(4 * b + 6, NS) + 2 * b + 1

        def n5_proj(b):
            return min(4 * b + 7, NS) + 2 * b + 2

        block = ctx.enter_context(nc.Block())

        @block.sync
        def _(sp):
            for h in range(2):
                sp.dma_start(X[h * C:(h + 1) * C], x[h * J:(h + 1) * J].rearrange("j c s -> c j s")).then_inc(x_loaded, 16)
            sp.dma_start(cst[:], consts).then_inc(const_loaded, 16)
            for h in range(2):
                sp.dma_start(wc[h * C:(h + 1) * C, EARLY], w64[:, EARLY]).then_inc(w_early_loaded, 16)
            for h in range(2):
                sp.dma_start(wc[h * C:(h + 1) * C, LATE], w64[:, LATE]).then_inc(w_late_loaded, 16)
            sp.dma_start(wk[:], w128).then_inc(w_late_loaded, 16)
            for t in range(NT):
                sp.dma_start(b2rep[t * E2:(t + 1) * E2, :], b2).then_inc(b2_loaded, 16)
            for n in range(2):
                sp.wait_ge((o_lower_ready, o_upper_ready)[n], 1)
                for h in range(2):
                    sp.dma_start(out[h * J + 2 * n:h * J + 2 * n + 2].rearrange("j c s -> c j s"),
                                 X[h * C:(h + 1) * C, 2 * n:2 * n + 2, :]).then_inc(stored, 16)
            sp.wait_ge(stored, 64)

        @block.gpsimd
        def _(pool):
            nc.gpsimd.memset(w_off, 0.0).then_inc(block_zeroed, 1)
            nc.gpsimd.memset(G, 0.0).then_inc(pads_zeroed, 1)
            pool.wait_ge(block_zeroed, 1)
            for h in range(2):
                pool.dma_start(w_off[h * C:(h + 1) * C, :, h * NOFF:(h + 1) * NOFF],
                               w64[:, W64["w_off"]].rearrange("c (t o) -> c t o", t=TAPS)).then_inc(off_block_loaded, 16)
            nc.gpsimd.memset(w_conv, 0.0).then_inc(block_zeroed, 1)
            nc.gpsimd.memset(G2, 0.0).then_inc(pads_zeroed, 1)
            nc.gpsimd.memset(PB[:], 0.0).then_inc(pads_zeroed, 1)
            pool.wait_ge(block_zeroed, 2)
            for h in range(2):
                pool.dma_start(w_conv[h * C:(h + 1) * C, :, h * C:(h + 1) * C],
                               w64[:, W64["w_conv"]].rearrange("c (t o) -> c t o", t=TAPS)).then_inc(conv_block_loaded, 16)
            pool.wait_ge(b2_loaded, 16 * NT)
            pool.wait_ge(const_loaded, 16)
            nc.gpsimd.tensor_tensor(b2blk[:], b2rep[:].unsqueeze(1).to_broadcast([P, NT, C]),
                                    c_("tile_rows").unsqueeze(2).to_broadcast([P, NT, C]), ALU.mult).then_inc(b2blk_ready, 1)

        @block.scalar
        def _(act):
            act.dma_start(rw[:], rows.to_broadcast([P, NROWS])).then_inc(rows_loaded, 16)

            def sqrt(n, ap):
                act.wait_ge(var_ready, n)
                nc.scalar.activation(ap, ap, ACT.Sqrt).then_inc(sd_ready, 1)

            sqrt(1, small[:, 0:J])
            act.wait_ge(norm_ready, 1)
            act.wait_ge(pads_zeroed, 1)
            for j in range(J):
                for k, to, frm in ((0, slice(1, WW), slice(0, WW - 1)), (2, slice(0, WW - 1), slice(1, WW))):
                    nc.scalar.activation(G[:, k, j, 1:HH + 1, to], img(X)[:, j, :, frm], ACT.Identity, bias=small[:, 12 + j:13 + j],
                                         scale=small[:, 4 + j:5 + j]).then_inc(g_shifted_ready, 1)
            act.wait_ge(mask_logits_ready, 4)
            nc.scalar.activation(mask[:], mask[:], ACT.Sigmoid).then_inc(mask_ready, 1)
            for j in range(J):
                act.wait_ge(hat_diff_ready, j + 1)
                hj = hats[:, 4 * j:4 * j + 4].rearrange("p t k q -> p (t k q)")
                nc.scalar.activation(hj, hj, ACT.Abs).then_inc(act_step, 1)
                act.wait_ge(act_step, j + 1)
                nc.scalar.activation(hj, hj, ACT.Relu, bias=1.0, scale=-1.0).then_inc(hat_ready, 1)
            for n in range(NT):
                act.wait_ge(u_ready, n // 2 + 1)
                slot = 1 + 2 * (n % 3)
                nc.scalar.activation(U[:, n, :].rearrange("p (a n) -> p a n", a=2), PS[:, slot:slot + 2, 0:288],
                                     ACT.Copy).then_inc(u_copied, 1)
            for n in range(NT):
                if n >= 2:
                    act.wait_ge(d_ready, n - 1)
                for g in range(NG):
                    m = n * NG + g
                    act.wait_ge(st_ready, m + 1)
                    nc.scalar.activation(ST[n % 2][:, 4 * g:4 * g + STG[g], :],
                                         PS[:, 1 + m % 4, 0:STG[g] * P].rearrange("p (a n) -> p a n", n=P),
                                         ACT.Copy).then_inc(st_copied, 1)
            sqrt(2, small[:, 0:J])
            act.wait_ge(qe_ready, 1)
            nc.scalar.activation(small[:, 8:8 + J], small[:, 8:8 + J], ACT.Sqrt).then_inc(qs_ready, 1)
            act.wait_ge(logits_ready, 1)
            nc.scalar.activation(cf[0:B, 0:2 * STREAMS], cf[0:B, 0:2 * STREAMS], ACT.Sigmoid).then_inc(gates_ready, 1)
            nc.scalar.activation(M[0:B].rearrange("p a b -> p (a b)"), cf[0:B, 2 * STREAMS:NPHI], ACT.Exp).then_inc(gates_ready, 1)

            def copy_yT(k):
                act.wait_ge(yT_ready, 2 * k + 1)
                nc.scalar.activation(YT[:, 0:4, :].rearrange("p a b -> p (a b)"), PS[:, 0, :], ACT.Copy).then_inc(yT_copied_act, 1)

            sqrt(3, lnst[:, 2, :])
            copy_yT(0)
            for n in range(0, 48, 2):
                act.wait_ge(qkv_ready, n // 2 + 1)
                j, r = divmod(n, 12)
                if r < 8:
                    dst = QK[:, j, r // 2, :]
                else:
                    dst = VV[:, 2 * j + (r - 8) // 2, :]
                nc.scalar.activation(dst, PS[:, n % 8, :], ACT.Copy).then_inc(qkv_copied_act, 1)
            for s in range(NS + 4):
                if s < NS:
                    b, hp = divmod(s, HPAIRS)
                    if s >= 2:
                        act.wait_ge(bank4_filled, n4_probs(s - 2))
                        act.wait_ge(bank5_filled, n5_probs(s - 2))
                    if hp == 0 and b >= 2:
                        act.wait_ge(heads_normed, 2 * (b - 1))
                    for e in range(2):
                        act.wait_ge(masked_ready, 2 * s + e + 1)
                        u = 2 * (s % 2) + e
                        for qt in range(PT):
                            cols = slice(0, P) if qt == 0 else slice(P, 3 * P)
                            ins = nc.scalar.activation(PR[:, u, cols], MS[:, u, cols], ACT.Exp, bias=nmx[:, u, qt:qt + 1],
                                                       scale=-1.0, accum_out=rsum[:, b % 2, qt, 2 * hp + e:2 * hp + e + 1])
                        ins.then_inc(probs_ready, 1)
                if 1 <= s <= NS:
                    act.wait_ge(bank4_filled, n4_probs(s - 1))
                    if s >= 3:
                        act.wait_ge(pv_done, s - 2)
                    nc.scalar.activation(PTs[:, 2 * ((s - 1) % 2), :], PS[:, 4, 0:384], ACT.Copy).then_inc(bank4_free, 1)
                if s >= 6 and s % 4 == 2:
                    act.wait_ge(bank4_filled, n4_heads((s - 6) // 4))
                    nc.scalar.activation(OT[:, 0, :], PS[:, 4, :], ACT.Copy).then_inc(bank4_free, 1)

            sqrt(4, lnst[:, 2, :])
            copy_yT(1)
            act.wait_ge(gate_diff_ready, 1)
            nc.scalar.activation(tg[:, 5, 0:NT], tg[:, 4, 0:NT], ACT.Exp).then_inc(gate_exp_ready, 1)
            for n in range(4 * E2 * 2):
                e2 = n % (2 * E2)
                act.wait_ge(hid2_ready, n + 1)
                if n >= 3:
                    act.wait_ge(out2_done, n - 2)
                nc.scalar.activation(hid[:, n % 3], PS[:, 2 * (n % 2):2 * (n % 2) + 2, 0:256], ACT.Gelu,
                                     bias=wk[:, W128["b1"]][:, e2:e2 + 1]).then_inc(gelu_done, 1)

            sqrt(5, lnst[:, 2, :])
            copy_yT(2)
            act.wait_ge(pj_ready, 1)
            nc.scalar.activation(PJ, PJ, ACT.Tanh).then_inc(tanh_done, 1)
            act.wait_ge(glogit_ready, 1)
            nc.scalar.activation(tg[:, 0, 0:NT], tg[:, 1, 0:NT], ACT.Sigmoid).then_inc(g3_ready, 1)

            sqrt(6, lnst[:, 2, :])
            copy_yT(3)
            act.wait_ge(gate_diff_ready, 2)
            nc.scalar.activation(tg[:, 5, 0:NT], tg[:, 4, 0:NT], ACT.Exp).then_inc(gate_exp_ready, 1)
            for n in range(4 * E3):
                act.wait_ge(hid3_ready, n + 1)
                if n >= 2:
                    act.wait_ge(prod3_done, n - 1)
                nc.scalar.activation(sil[:, n % 2], PS[:, 2 * (n % 2):2 * (n % 2) + 2, 0:256], ACT.Silu).then_inc(silu_done, 1)
            act.wait_ge(finalT_ready, 1)
            nc.scalar.activation(X[:, 0:2, :].rearrange("p a b -> p (a b)"), PS[:, 0, :], ACT.Copy).then_inc(o_lower_ready, 1)

        @block.vector
        def _(dve):
            steps = [0]

            def step(ins):
                ins.then_inc(dve_step, 1)
                steps[0] += 1

            def settle():
                dve.wait_ge(dve_step, steps[0])

            def group_norm(n, src, dst):
                for j in range(J):
                    step(nc.vector.bn_stats(stat[:, j, :], src[:, j, :]))
                settle()
                for j in range(J):
                    step(nc.vector.bn_aggr(mv[:, n, j, :], stat[:, j, :]))
                settle()
                mean, var = mv[:, n, :, 0], mv[:, n, :, 1]
                step(nc.vector.tensor_tensor(small[:, 0:J], mean, mean, ALU.mult))
                settle()
                nc.vector.tensor_tensor(var, var, small[:, 0:J], ALU.add).then_inc(moments_ready, 1)
                dve.wait_ge(group_moments_ready, n + 1)
                step(nc.vector.tensor_copy(gmv[:].rearrange("p j m -> p (j m)"), PS[:, 7, 0:2 * J]))
                settle()
                step(nc.vector.tensor_tensor(small[:, 4:4 + J], gmv[:, :, 0], gmv[:, :, 0], ALU.mult))
                settle()
                step(nc.vector.tensor_tensor(small[:, 0:J], gmv[:, :, 1], small[:, 4:4 + J], ALU.subtract))
                settle()
                nc.vector.tensor_scalar(small[:, 0:J], small[:, 0:J], EPS5, None, ALU.add).then_inc(var_ready, 1)
                dve.wait_ge(sd_ready, n + 1)
                step(nc.vector.reciprocal(small[:, 4:4 + J], small[:, 0:J]))
                settle()
                nc.vector.scalar_tensor_tensor(small[:, 12:12 + J], gmv[:, :, 0], -1.0, small[:, 4:4 + J], ALU.mult,
                                               ALU.mult).then_inc(norm_ready, 1)
                dve.wait_ge(norm_ready, n + 1)
                dve.wait_ge(pads_zeroed, n + 1)
                for j in range(J):
                    nc.vector.tensor_scalar(dst[:, j], img(src)[:, j], small[:, 4 + j:5 + j],
                                            small[:, 12 + j:13 + j], ALU.mult, ALU.add).then_inc(g_ready, 1)

            dve.wait_ge(x_loaded, 32)
            group_norm(0, X, G[:, 1, :, 1:HH + 1, :])

            dve.wait_ge(w_late_loaded, 48)
            dve.wait_ge(rows_loaded, 16)
            dve.wait_ge(const_loaded, 16)
            step(nc.vector.tensor_tensor(phr[:], w_("phi").rearrange("p (n o) -> p n o", n=STREAMS),
                                         w_("rms").unsqueeze(2).to_broadcast([P, STREAMS, NPHI]), ALU.mult))
            step(nc.vector.tensor_tensor(c_("base").rearrange("p (a k) -> p a k", a=PT), c_("base").rearrange("p (a k) -> p a k", a=PT),
                                         rw[:, ROWS["b_off"]][:, 0:2 * TAPS].unsqueeze(1).to_broadcast([P, PT, 2 * TAPS]), ALU.add))
            settle()
            step(nc.vector.tensor_reduce(weff[:], phr[:].rearrange("p n o -> p o n"), AX.X, ALU.add))

            dve.wait_ge(offsets_ready, 1)
            om = PS[:, 0, 0:NP * 2 * NOFF].rearrange("p (j t h o) -> p t h j o", j=J, t=PT, h=2)
            co = coord[:].rearrange("p (j t h) k -> p t h j k", h=2, j=J)
            mo = mask[:].rearrange("p (j t h) k -> p t h j k", h=2, j=J)
            for t in range(PT):
                for h in range(2):
                    nc.vector.tensor_tensor(mo[:, t, h], om[:, t, h, :, 2 * TAPS:NOFF],
                                            rw[:, ROWS["b_off"]][:, 2 * TAPS:NOFF].unsqueeze(1).to_broadcast([P, J, TAPS]),
                                            ALU.add).then_inc(mask_logits_ready, 1)
            for t in range(PT):
                for h in range(2):
                    step(nc.vector.tensor_tensor(co[:, t, h], om[:, t, h, :, 0:2 * TAPS],
                                                 c_("base").rearrange("p (a k) -> p a k", a=PT)[:, t].unsqueeze(1).to_broadcast([P, J, 2 * TAPS]), ALU.add))
            settle()
            def chunk(j):
                return hats[:, 4 * j:4 * j + 4].rearrange("p t k q -> p (t k) q")

            for j in range(J):
                nc.vector.tensor_tensor(chunk(j), coord[:, 4 * j:4 * j + 4].rearrange("p t k -> p (t k)").unsqueeze(2).to_broadcast([P, 8 * TAPS, WW]),
                                        c_("grid").unsqueeze(1).to_broadcast([P, 8 * TAPS, WW]), ALU.subtract).then_inc(hat_diff_ready, 1)

            def x1_tile(ip):
                j, pt = divmod(ip, PT)
                dve.wait_ge(dT_ready, ip + 1)
                nc.vector.scalar_tensor_tensor(X1[:, j, pt * P:(pt + 1) * P], PS[:, 7 * (ip % 2), 0:P], w_("b_dcn"),
                                               X[:, j, pt * P:(pt + 1) * P], ALU.add, ALU.add).then_inc(x1_tile_ready, 1)

            def d_copy(ip):
                dve.wait_ge(d_ready, 2 * ip + 2)
                if ip >= 2:
                    dve.wait_ge(dT_ready, ip - 1)
                nc.vector.tensor_copy(D[:, ip % 2, :], PS[:, 5 + ip % 2, 0:P]).then_inc(d_copied, 1)

            for n in range(NT):
                if n % 4 == 0:
                    dve.wait_ge(hat_ready, n // 4 + 1)
                    dve.wait_ge(mask_ready, 1)
                    hx = chunk(n // 4).rearrange("p (k c) q -> p c k q", c=2)[:, 1]
                    step(nc.vector.tensor_tensor(hx, hx, mask[:, n:n + 4].rearrange("p t k -> p (t k)").unsqueeze(2).to_broadcast([P, 4 * TAPS, WW]),
                                                 ALU.mult))
                    settle()
                if n >= 2:
                    dve.wait_ge(st_ready, NG * (n - 1))
                hk = hats[:, n].rearrange("p (k c) q -> p c k q", c=2)
                nc.vector.tensor_tensor(prods[n % 2].rearrange("p k (a b) -> p k a b", a=HH),
                                        hk[:, 0].unsqueeze(3).to_broadcast([P, TAPS, HH, WW]),
                                        hk[:, 1].unsqueeze(2).to_broadcast([P, TAPS, HH, WW]), ALU.mult).then_inc(prod_ready, 1)
                if n >= 4 and n % 2 == 0:
                    d_copy(n // 2 - 2)
                if n >= 5 and n % 2 == 1:
                    x1_tile(n // 2 - 2)
            for ip in range(NP - 2, NP):
                d_copy(ip)
                x1_tile(ip)
            dve.wait_ge(x1_tile_ready, NP)

            group_norm(1, X1, G2[:, :, 1:HH + 1, 1:WW + 1])
            pooled = small[:, 16:16 + J]
            step(nc.vector.tensor_tensor(pooled, mv[:, 1, :, 0], gmv[:, :, 0], ALU.subtract))
            settle()
            step(nc.vector.tensor_tensor(pooled, pooled, small[:, 4:4 + J], ALU.mult))
            settle()
            nc.vector.tensor_tensor(small[:, 20:20 + J], pooled, pooled, ALU.mult).then_inc(sq_ready, 1)
            dve.wait_ge(q_ready, 1)
            nc.vector.tensor_scalar(small[:, 8:8 + J], PS[:, 3, 0:J], 1e-20, None, ALU.add).then_inc(qe_ready, 1)
            dve.wait_ge(qs_ready, 1)
            step(nc.vector.reciprocal(small[:, 24:24 + J], small[:, 8:8 + J]))
            settle()
            dve.wait_ge(pads_zeroed, 3)
            for h in range(2):
                hs = slice(h * C, (h + 1) * C)
                nc.vector.tensor_tensor(PB[hs, h * J:(h + 1) * J], pooled[hs], small[hs, 24:24 + J], ALU.mult).then_inc(pb_ready, 1)
            dve.wait_ge(coef_ready, 1)
            step(nc.vector.tensor_tensor(cf[0:B], PS[0:B, 3, 0:NPHI], rw[0:B, ROWS["phi_b"]], ALU.add))
            settle()
            al = rw[0:B, ROWS["alpha"]]
            step(nc.vector.tensor_scalar(cf[0:B, 0:4], cf[0:B, 0:4], al[:, 0:1], None, ALU.mult))
            step(nc.vector.tensor_scalar(cf[0:B, 4:8], cf[0:B, 4:8], al[:, 1:2], None, ALU.mult))
            step(nc.vector.tensor_scalar(cf[0:B, 8:NPHI], cf[0:B, 8:NPHI], al[:, 2:3], None, ALU.mult))
            settle()
            nc.vector.tensor_copy(V[0:B, 3:4], cf[0:B, 0:1]).then_inc(logits_ready, 1)
            dve.wait_ge(gates_ready, 2)
            MM = M[0:B]
            for _ in range(SINKHORN):
                for view in (MM, MM.rearrange("p a b -> p b a")):
                    step(nc.vector.tensor_reduce(mn[0:B], view, AX.X, ALU.add))
                    settle()
                    step(nc.vector.reciprocal(mn[0:B], mn[0:B]))
                    settle()
                    step(nc.vector.tensor_tensor(view, view, mn[0:B].unsqueeze(2).to_broadcast([B, STREAMS, STREAMS]), ALU.mult))
                    settle()
            step(nc.vector.tensor_reduce(V[0:B, 0:1], MM.rearrange("p a b -> p (a b)")[:, 0:16:5], AX.X, ALU.add))
            step(nc.vector.tensor_reduce(V[0:B, 1:2], cf[0:B, 0:4], AX.X, ALU.add))
            step(nc.vector.tensor_reduce(V[0:B, 2:3], cf[0:B, 4:8], AX.X, ALU.add))
            settle()
            step(nc.vector.tensor_scalar(V[0:B, 0:1], V[0:B, 0:1], 0.25, None, ALU.mult))
            step(nc.vector.tensor_scalar(V[0:B, 2:3], V[0:B, 2:3], 0.5, None, ALU.mult))
            settle()
            step(nc.vector.tensor_tensor(V[0:B, 1:2], V[0:B, 1:2], V[0:B, 2:3], ALU.mult))
            settle()
            nc.vector.tensor_tensor(V3[0:B], V[0:B, 0:3].unsqueeze(1).to_broadcast([B, J, 3]),
                                    cst[0:B, CONST["sel_image"]].unsqueeze(2).to_broadcast([B, J, 3]), ALU.mult).then_inc(v3_ready, 1)
            dve.wait_ge(cb_ready, 1)
            step(nc.vector.tensor_copy(CB[:].rearrange("p a b -> p (a b)"), PS[:, 3, 0:3 * J]))
            settle()
            step(nc.vector.tensor_scalar(bb[:], CB[:, :, 2], w_("conv_b"), None, ALU.mult))
            settle()
            for j in range(J):
                step(nc.vector.tensor_scalar(X1[:, j], X1[:, j], bb[:, j:j + 1], None, ALU.add))
            settle()
            for j in range(J):
                step(nc.vector.scalar_tensor_tensor(img(X1)[:, j], G2[:, j, 1:HH + 1, 1:WW + 1], CB[:, j, 0:1],
                                                    img(X1)[:, j], ALU.mult, ALU.add))
            settle()
            for j in range(J):
                dve.wait_ge(conv_ready, j // 2 + 1)
                nc.vector.scalar_tensor_tensor(X1[:, j], PS[:, 1 + j // 2, (j % 2) * S:(j % 2 + 1) * S], CB[:, j, 1:2],
                                               X1[:, j], ALU.mult, ALU.add).then_inc(x2_ready, 1)
            for m in range(2):
                dve.wait_ge(t_ready, m + 1)
                step(nc.vector.tensor_copy(T[:, 8 * m:8 * m + 8, :].rearrange("p t c -> p (t c)"), PS[:, 5 + m, :]))
            settle()

            def layer_norm(k):
                mean, var, sd, inv = (lnst[:, r, :] for r in range(4))
                var = lnst[:, 2, :]
                step(nc.vector.tensor_reduce(mean, T[:], AX.X, ALU.add))
                settle()
                step(nc.vector.tensor_scalar(mean, mean, 1.0 / C, None, ALU.mult))
                settle()
                step(nc.vector.tensor_tensor(Y[:], T[:], mean.unsqueeze(2).to_broadcast([P, NT, C]), ALU.subtract))
                settle()
                step(nc.vector.tensor_tensor(Z[:], Y[:], Y[:], ALU.mult))
                settle()
                step(nc.vector.tensor_reduce(var, Z[:], AX.X, ALU.add))
                settle()
                nc.vector.tensor_scalar(var, var, 1.0 / C, EPS5, ALU.mult, ALU.add).then_inc(var_ready, 1)
                dve.wait_ge(sd_ready, 3 + k)
                step(nc.vector.reciprocal(inv, var))
                settle()
                nc.vector.tensor_tensor(Y[:], Y[:], inv.unsqueeze(2).to_broadcast([P, NT, C]), ALU.mult).then_inc(y_ready, 1)
                dve.wait_ge(yT_ready, 2 * k + 2)
                nc.vector.tensor_copy(YT[:, 4:8, :].rearrange("p a b -> p (a b)"), PS[:, 1, :]).then_inc(yT_copied_dve, 1)

            layer_norm(0)
            step(nc.vector.tensor_tensor(T[:], T[:], rw[:, ROWS["b_proj"]].unsqueeze(1).to_broadcast([P, NT, C]), ALU.add))
            settle()
            for n in range(1, 48, 2):
                dve.wait_ge(qkv_ready, n // 2 + 1)
                j, r = divmod(n, 12)
                if r < 8:
                    dst = QK[:, J + j, r // 2, :]
                else:
                    dst = VV[:, NP + 2 * j + (r - 8) // 2, :]
                nc.vector.tensor_copy(dst, PS[:, n % 8, :]).then_inc(qkv_copied_dve, 1)
            for s in range(NS + 4):
                if s < NS:
                    dve.wait_ge(scores_ready, s + 1)
                    if s >= 2:
                        dve.wait_ge(probs_ready, 2 * (s - 1))
                    for e in range(2):
                        u = 2 * (s % 2) + e
                        nc.vector.tensor_tensor_reduce(MS[:, u, 0:P], PS[:, u, 0:P], c_("causal")[:, P:2 * P], -SCALE, 1e30,
                                                       ALU.add, ALU.min, nmx[:, u, 0:1])
                        nc.vector.tensor_tensor_reduce(MS[:, u, P:3 * P], PS[:, u, P:3 * P], c_("causal"), -SCALE, 1e30,
                                                       ALU.add, ALU.min, nmx[:, u, 1:2]).then_inc(masked_ready, 1)
                if 1 <= s <= NS:
                    dve.wait_ge(bank5_filled, n5_probs(s - 1))
                    if s >= 3:
                        dve.wait_ge(pv_done, s - 2)
                    nc.vector.tensor_copy(PTs[:, 2 * ((s - 1) % 2) + 1, :], PS[:, 5, 0:384]).then_inc(bank5_free, 1)
                if s >= 5 and s % 4 == 1:
                    b = (s - 5) // 4
                    dve.wait_ge(probs_ready, 8 * (b + 1))
                    step(nc.vector.reciprocal(rinv[:, b % 2], rsum[:, b % 2]))
                    settle()
                    dve.wait_ge(pv_done, 4 * (b + 1))
                    for qt in range(PT):
                        nc.vector.tensor_tensor(ON[:, qt, :].rearrange("p (h c) -> p h c", h=HEADS),
                                                PS[:, 6 + qt, :].rearrange("p (h c) -> p h c", h=HEADS),
                                                rinv[:, b % 2, qt, :].unsqueeze(2).to_broadcast([P, HEADS, C]),
                                                ALU.mult).then_inc(heads_normed, 1)
                if s >= 6 and s % 4 == 2:
                    dve.wait_ge(bank5_filled, n5_heads((s - 6) // 4))
                    nc.vector.tensor_copy(OT[:, 1, :], PS[:, 5, :]).then_inc(bank5_free, 1)
                if s >= 7 and s % 4 == 3:
                    b = (s - 7) // 4
                    dve.wait_ge(bank5_filled, n5_proj(b))
                    h, j = divmod(b, J)
                    tt = T[:].rearrange("p (j t h) c -> p j h t c", t=PT, h=2)[:, j, h]
                    nc.vector.tensor_tensor(tt, PS[:, 5, 0:2 * C].rearrange("p (t c) -> p t c", t=PT), tt, ALU.add).then_inc(bank5_free, 1)
            dve.wait_ge(bank5_free, NS + 2 * B)

            def top2(k, logits_cols, bias, E):
                n = NT * E
                lg, key, h1, l2 = (tg[:, r, 0:n].rearrange("p (t e) -> p t e", e=E) for r in range(4))
                m1, m2, mk, df, w1 = (tg[:, 4, 16 * r:16 * r + NT] for r in (1, 2, 3, 0, 4))
                ex = tg[:, 5, 0:NT]
                desc = c_("desc")[:, E3 - E:E3].unsqueeze(1).to_broadcast([P, NT, E])

                def wide(v):
                    return v.unsqueeze(2).to_broadcast([P, NT, E])

                dve.wait_ge(gate_logits_ready, k + 1)
                for h in range(2):
                    step(nc.vector.tensor_tensor(lg[:, h:NT:2], PS[:, 2 + h, 0:NP * E].rearrange("p (t e) -> p t e", e=E),
                                                 bias.unsqueeze(1).to_broadcast([P, NP, E]), ALU.add))
                settle()

                def first_max(src, m, hot):
                    step(nc.vector.tensor_reduce(m, src, AX.X, ALU.max))
                    settle()
                    step(nc.vector.tensor_tensor(key, src, wide(m), ALU.is_equal))
                    settle()
                    step(nc.vector.tensor_tensor(key, key, desc, ALU.mult))
                    settle()
                    step(nc.vector.tensor_reduce(mk, key, AX.X, ALU.max))
                    settle()
                    step(nc.vector.tensor_tensor(hot, key, wide(mk), ALU.is_equal))
                    settle()

                first_max(lg, m1, h1)
                step(nc.vector.scalar_tensor_tensor(l2, h1, NEG, lg, ALU.mult, ALU.add))
                settle()
                first_max(l2, m2, l2)
                nc.vector.tensor_tensor(df, m2, m1, ALU.subtract).then_inc(gate_diff_ready, 1)
                dve.wait_ge(gate_exp_ready, k + 1)
                step(nc.vector.tensor_scalar(w1, ex, 1.0, None, ALU.add))
                settle()
                step(nc.vector.reciprocal(w1, w1))
                settle()
                step(nc.vector.tensor_tensor(mk, ex, w1, ALU.mult))
                settle()
                step(nc.vector.tensor_tensor(h1, h1, wide(w1), ALU.mult))
                step(nc.vector.tensor_tensor(l2, l2, wide(mk), ALU.mult))
                settle()
                nc.vector.tensor_tensor(gate[:].rearrange("p t e -> p (t e)")[:, 0:n].rearrange("p (t e) -> p t e", e=E),
                                        h1, l2, ALU.add).then_inc(gate_ready, 1)
                dve.wait_ge(gate_ready, k + 1)

            def combine(bank, tile, g, gates, free):
                step(nc.vector.tensor_tensor(pr8[:, bank % 2].rearrange("p (e c) -> p e c", c=C), PS[:, bank].rearrange("p (e c) -> p e c", c=C),
                                             gates.unsqueeze(2).to_broadcast([P, E2, C]), ALU.mult))
                settle()
                nc.vector.tensor_reduce(part[:, bank % 2], pr8[:, bank % 2].rearrange("p (e c) -> p c e", c=C), AX.X,
                                        ALU.add).then_inc(free, 1)

            layer_norm(1)
            top2(0, None, rw[:, ROWS["bg2"]], E2)
            g2v = gate[:].rearrange("p t e -> p (t e)")[:, 0:NT * E2].rearrange("p (t e) -> p t e", e=E2)
            dve.wait_ge(gateT_ready, 1)
            nc.vector.tensor_copy(gateT, PS[:, 2, 0:P]).then_inc(gateT_copied, 1)
            dve.wait_ge(b2_term_ready, 1)
            step(nc.vector.tensor_tensor(T[:].rearrange("p (a t) c -> p a (t c)", a=2), PS[:, 4:6, :],
                                         T[:].rearrange("p (a t) c -> p a (t c)", a=2), ALU.add))
            settle()
            nc.vector.tensor_copy(part[:, 0, 0:1], T[:, 0, 0:1]).then_inc(acc2_free, 1)
            count = 1
            for c in range(4):
                dve.wait_ge(out2_done, 2 * E2 * (c + 1))
                for q in range(4):
                    h, t = divmod(q, 2)
                    tile = 2 * (2 * c + t) + h
                    combine(4 + q, tile, 0, g2v[:, tile], acc2_free)
                    count += 1
                    dve.wait_ge(acc2_free, count)
                    step(nc.vector.tensor_tensor(T[:, tile], T[:, tile], part[:, q % 2], ALU.add))
            settle()

            layer_norm(2)
            dve.wait_ge(proj_ready, 1)
            nc.vector.tensor_tensor(PJ.rearrange("p (t h) a -> p h t a", h=2),
                                    PS[:, 2:4, 0:NP * A3].rearrange("p h (t a) -> p h t a", a=A3),
                                    rw[:, ROWS["bp"]].unsqueeze(1).unsqueeze(1).to_broadcast([P, 2, NP, A3]), ALU.add).then_inc(pj_ready, 1)
            dve.wait_ge(tanh_done, 1)
            step(nc.vector.tensor_tensor(PJ, PJ, rw[:, ROWS["wg"]].unsqueeze(1).to_broadcast([P, NT, A3]), ALU.mult))
            settle()
            nc.vector.tensor_reduce(tg[:, 1, 0:NT], PJ, AX.X, ALU.add).then_inc(glogit_ready, 1)
            dve.wait_ge(g3_ready, 1)
            step(nc.vector.tensor_copy(WX[:, :, C], tg[:, 0, 0:NT]))
            nc.vector.tensor_tensor(WX[:, :, 0:C], Y[:], tg[:, 0, 0:NT].unsqueeze(2).to_broadcast([P, NT, C]), ALU.mult).then_inc(wx_ready, 1)
            for q in range(4):
                h, pt = divmod(q, 2)
                bank = PS[:, 4 + q, 0:J * (C + 1)].rearrange("p (j c) -> p j c", c=C + 1)
                dve.wait_ge(window_ready, q + 1)
                step(nc.vector.reciprocal(tg[:, 6, 4 * q:4 * q + 4], bank[:, :, C]))
                settle()
                zv = Z[:].rearrange("p (j t h) c -> p h t j c", h=2, t=PT)[:, h, pt]
                tv = T[:].rearrange("p (j t h) c -> p h t j c", h=2, t=PT)[:, h, pt]
                step(nc.vector.tensor_tensor(zv, bank[:, :, 0:C], tg[:, 6, 4 * q:4 * q + 4].unsqueeze(2).to_broadcast([P, J, C]), ALU.mult))
                settle()
                step(nc.vector.tensor_tensor(tv, tv, zv, ALU.add))
            settle()

            layer_norm(3)
            top2(1, None, rw[:, ROWS["bg3"]], E3)
            count = 0

            def combine3(u):
                nonlocal count
                c, g = divmod(u, 2)
                dve.wait_ge(out3_done, E2 * (u + 1))
                for q in range(4):
                    h, t = divmod(q, 2)
                    tile = 2 * (2 * c + t) + h
                    combine(4 + q, tile, g, gate[:, tile, g * E2:(g + 1) * E2], acc3_free)
                    count += 1
                    dve.wait_ge(acc3_free, count)
                    step(nc.vector.tensor_tensor(T[:, tile], T[:, tile], part[:, q % 2], ALU.add))

            for n in range(4 * E3):
                dve.wait_ge(silu_done, n + 1)
                if n >= 3:
                    dve.wait_ge(out3_done, n - 2)
                nc.vector.tensor_tensor(hid[:, n % 3], sil[:, n % 2], PS[:, 2 * (n % 2):2 * (n % 2) + 2, 256:512],
                                        ALU.mult).then_inc(prod3_done, 1)
                if n % E2 == 1 and n > E2:
                    combine3(n // E2 - 1)
            combine3(2 * 4 - 1)
            settle()
            nc.vector.tensor_copy(part[:, 0, 0:1], T[:, 0, 0:1]).then_inc(final_ready, 1)
            dve.wait_ge(finalT_ready, 2)
            nc.vector.tensor_copy(X[:, 2:4, :].rearrange("p a b -> p (a b)"), PS[:, 1, :]).then_inc(o_upper_ready, 1)

        @block.tensor
        def _(pe):
            mm = nc.tensor.matmul

            pe.wait_ge(const_loaded, 16)
            pe.wait_ge(moments_ready, 1)
            mm(PS[:, 7, 0:2 * J], c_("pair_mean"), mv[:, 0].rearrange("p j m -> p (j m)"), start=True, stop=True).then_inc(group_moments_ready, 1)
            pe.wait_ge(off_block_loaded, 32)
            for ip in range(NP):
                j, pt = divmod(ip, PT)
                pe.wait_ge(g_ready, j + 1)
                pe.wait_ge(g_shifted_ready, 2 * j + 2)
                for k in range(TAPS):
                    ky, kx = divmod(k, 3)
                    ins = mm(PS[:, 0, ip * 2 * NOFF:(ip + 1) * 2 * NOFF], G[:, kx, j, 8 * pt + ky:8 * pt + ky + 8, :],
                             w_off[:, k, :], start=(k == 0), stop=(k == TAPS - 1))
            ins.then_inc(offsets_ready, 1)
            pe.wait_ge(w_early_loaded, 32)
            for ip in range(NP):
                j, pt = divmod(ip, PT)
                if 2 * ip + 1 >= 3:
                    pe.wait_ge(u_copied, 2 * ip + 1 - 2)
                for a in range(2):
                    for h in range(2):
                        n = 2 * ip + h
                        hs = slice(h * C, (h + 1) * C)
                        ins = mm(PS[:, 1 + 2 * (n % 3) + a, 0:288], G[hs, 1, j, 8 * pt + 1:8 * pt + 9, :],
                                 w_("w_dcn", h)[:, a * 288:(a + 1) * 288], start=True, stop=True)
                ins.then_inc(u_ready, 1)

            def dT(ip):
                pe.wait_ge(d_copied, ip + 1)
                if ip >= 2:
                    pe.wait_ge(x1_tile_ready, ip - 1)
                nc.tensor.transpose(PS[:, 7 * (ip % 2), 0:P], D[:, ip % 2, :], ident).then_inc(dT_ready, 1)

            pe.wait_ge(u_copied, NT)
            for n in range(NT + 1):
                for g in range(NG):
                    if n < NT:
                        m = n * NG + g
                        if g == 0:
                            pe.wait_ge(prod_ready, n + 1)
                        if m >= 4:
                            pe.wait_ge(st_copied, m - 3)
                        for a in range(STG[g]):
                            k, qt = divmod(4 * g + a, 2)
                            ins = nc.tensor.transpose(PS[:, 1 + m % 4, a * P:(a + 1) * P], prods[n % 2][:, k, qt * P:(qt + 1) * P], ident)
                        ins.then_inc(st_ready, 1)
                    if n >= 1:
                        v = n - 1
                        ip, h = divmod(v, 2)
                        b = h * J + ip // 2
                        pe.wait_ge(st_copied, v * NG + g + 1)
                        if h == 0 and ip >= 2 and g == 0:
                            pe.wait_ge(d_copied, ip - 1)
                        for a in range(STG[g]):
                            k, qt = divmod(4 * g + a, 2)
                            ins = mm(PS[:, 5 + ip % 2, h * C:(h + 1) * C], ST[v % 2][:, 4 * g + a, :],
                                     U[:, 2 * (2 * (ip // 2) + qt) + h, k * C:(k + 1) * C],
                                     start=(g + a == 0), stop=(4 * g + a == 2 * TAPS - 1))
                        if g == NG - 1:
                            ins.then_inc(d_ready, 1)
                if n >= 4 and n % 2 == 0 and n // 2 - 2 < NP:
                    dT(n // 2 - 2)
            for ip in range(NP - 1, NP):
                dT(ip)

            pe.wait_ge(x1_tile_ready, NP)
            pe.wait_ge(moments_ready, 2)
            mm(PS[:, 7, 0:2 * J], c_("pair_mean"), mv[:, 1].rearrange("p j m -> p (j m)"), start=True, stop=True).then_inc(group_moments_ready, 1)
            pe.wait_ge(sq_ready, 1)
            mm(PS[:, 3, 0:J], c_("half_mean"), small[:, 20:20 + J], start=True, stop=True).then_inc(q_ready, 1)
            pe.wait_ge(conv_block_loaded, 32)

            def conv(r):
                pe.wait_ge(g_ready, J + 2 * r + 2)
                for k in range(TAPS):
                    ky, kx = divmod(k, 3)
                    ins = mm(PS[:, 1 + r, :], w_conv[:, k, :], G2[:, 2 * r:2 * r + 2, ky:ky + HH, kx:kx + WW],
                             start=(k == 0), stop=(k == TAPS - 1))
                ins.then_inc(conv_ready, 1)

            conv(0)
            pe.wait_ge(pb_ready, 2)
            mm(PS[0:B, 3, 0:NPHI], PB[:], weff[:], start=True, stop=True).then_inc(coef_ready, 1)
            conv(1)
            pe.wait_ge(v3_ready, 1)
            mm(PS[:, 3, 0:3 * J], cst[0:B, CONST["sel_half"]], V3[0:B].rearrange("p a b -> p (a b)"), start=True, stop=True).then_inc(cb_ready, 1)
            for m in range(2):
                pe.wait_ge(x2_ready, 2 * m + 2)
                for a in range(4):
                    j, pt = divmod(4 * m + a, PT)
                    ins = nc.tensor.transpose(PS[:, 5 + m, a * P:(a + 1) * P], X1[:, j, pt * P:(pt + 1) * P], ident)
                ins.then_inc(t_ready, 1)

            def transpose_y(k):
                pe.wait_ge(y_ready, k + 1)
                for m in range(2):
                    for a in range(4):
                        ins = nc.tensor.transpose(PS[:, m, a * P:(a + 1) * P],
                                                  Y[:, 2 * (4 * m + a):2 * (4 * m + a) + 2, :].rearrange("p h c -> p (h c)"), ident)
                    ins.then_inc(yT_ready, 1)
                pe.wait_ge(yT_copied_act, k + 1)
                pe.wait_ge(yT_copied_dve, k + 1)

            transpose_y(0)
            yt = YT[:].rearrange("p t q -> p (t q)")
            for n in range(0, 48, 2):
                j, r = divmod(n, 12)
                if n >= 8:
                    pe.wait_ge(qkv_copied_act, (n - 8) // 2 + 1)
                    pe.wait_ge(qkv_copied_dve, (n - 8) // 2 + 1)
                if r < 8:
                    hp = r // 2
                    for kq in range(2):
                        for h in range(2):
                            o = kq * HEADS * C + hp * P
                            ins = mm(PS[:, (n + h) % 8, kq * S:(kq + 1) * S], w_("qkv", h)[:, o:o + P],
                                     yt[h * C:(h + 1) * C, j * S:(j + 1) * S], start=True, stop=True)
                else:
                    t = 2 * j + (r - 8) // 2
                    for h in range(2):
                        ins = mm(PS[:, (n + h) % 8, :], YT[h * C:(h + 1) * C, t, :], w_("qkv", h)[:, 2 * HEADS * C:3 * HEADS * C],
                                 start=True, stop=True)
                ins.then_inc(qkv_ready, 1)
            pe.wait_ge(qkv_copied_act, 24)
            pe.wait_ge(qkv_copied_dve, 24)
            for s in range(NS + 4):
                if s < NS:
                    b, hp = divmod(s, HPAIRS)
                    if s >= 2:
                        pe.wait_ge(masked_ready, 2 * (s - 1))
                    for qt in range(PT):
                        for e in range(2):
                            es = slice(e * C, (e + 1) * C)
                            cols = slice(0, P) if qt == 0 else slice(P, 3 * P)
                            ins = mm(PS[:, 2 * (s % 2) + e, cols], QK[es, b, hp, qt * P:(qt + 1) * P],
                                     QK[es, b, hp, S:S + (qt + 1) * P], start=True, stop=True)
                    ins.then_inc(scores_ready, 1)
                if 1 <= s <= NS:
                    for e in range(2):
                        u = 2 * ((s - 1) % 2) + e
                        pe.wait_ge(probs_ready, 2 * (s - 1) + e + 1)
                        if s >= 2:
                            pe.wait_ge((bank4_free, bank5_free)[e], (n4_probs, n5_probs)[e](s - 1) - 1)
                        for a in range(3):
                            ins = nc.tensor.transpose(PS[:, 4 + e, a * P:(a + 1) * P], PR[:, u, a * P:(a + 1) * P], ident)
                        ins.then_inc((bank4_filled, bank5_filled)[e], 1)
                if 2 <= s <= NS + 1:
                    v = s - 2
                    b, hp = divmod(v, HPAIRS)
                    if hp == 0 and b >= 1:
                        pe.wait_ge(heads_normed, 2 * b)
                    pe.wait_ge(bank4_free, n4_probs(v))
                    pe.wait_ge(bank5_free, n5_probs(v))
                    for e in range(2):
                        hd = 2 * hp + e
                        pt_ = PTs[:, 2 * (v % 2) + e, :]
                        vh = slice(hd * C, (hd + 1) * C)
                        mm(PS[:, 6, vh], pt_[:, 0:P], VV[:, 2 * b, vh], start=True, stop=True)
                        mm(PS[:, 7, vh], pt_[:, P:2 * P], VV[:, 2 * b, vh], start=True, stop=False)
                        ins = mm(PS[:, 7, vh], pt_[:, 2 * P:3 * P], VV[:, 2 * b + 1, vh], start=False, stop=True)
                    ins.then_inc(pv_done, 1)
                if s >= 6 and s % 4 == 2:
                    b = (s - 6) // 4
                    for qt in range(PT):
                        pe.wait_ge(heads_normed, 2 * b + qt + 1)
                        pe.wait_ge((bank4_free, bank5_free)[qt], (n4_heads, n5_heads)[qt](b) - 1)
                        for a in range(4):
                            ins = nc.tensor.transpose(PS[:, 4 + qt, a * P:(a + 1) * P], ON[:, qt, a * P:(a + 1) * P], ident)
                        ins.then_inc((bank4_filled, bank5_filled)[qt], 1)
                if s >= 7 and s % 4 == 3:
                    b = (s - 7) // 4
                    pe.wait_ge(bank4_free, n4_heads(b))
                    pe.wait_ge(bank5_free, n5_proj(b) - 1)
                    for qt in range(PT):
                        for a in range(4):
                            ins = mm(PS[:, 5, qt * C:(qt + 1) * C], OT[:, qt, a * P:(a + 1) * P],
                                     wk[:, W128["proj"]][:, a * C:(a + 1) * C], start=(a == 0), stop=(a == 3))
                    ins.then_inc(bank5_filled, 1)

            def gate_logits(name, E):
                for t in range(NP):
                    for h in range(2):
                        ins = mm(PS[:, 2 + h, t * E:(t + 1) * E], YT[h * C:(h + 1) * C, t, :], w_(name, h), start=True, stop=True)
                ins.then_inc(gate_logits_ready, 1)

            transpose_y(1)
            gate_logits("wg2", E2)
            pe.wait_ge(gate_ready, 1)
            nc.tensor.transpose(PS[:, 2, 0:P], gate[:].rearrange("p t e -> p (t e)")[:, 0:NT * E2], ident).then_inc(gateT_ready, 1)
            pe.wait_ge(gateT_copied, 1)
            pe.wait_ge(b2blk_ready, 1)
            for a in range(2):
                ins = mm(PS[:, 4 + a, :], gateT, b2blk[:].rearrange("p (a t) c -> p a (t c)", a=2)[:, a], start=True, stop=True)
            ins.then_inc(b2_term_ready, 1)
            N2 = 4 * E2 * 2
            for n in range(N2 + 1):
                if n < N2:
                    c, r = divmod(n, 2 * E2)
                    if n >= 2:
                        pe.wait_ge(gelu_done, n - 1)
                    for h in range(2):
                        ins = mm(PS[:, 2 * (n % 2) + h, 0:256], w_("w1_2", h)[:, r * P:(r + 1) * P],
                                 yt[h * C:(h + 1) * C, c * 256:(c + 1) * 256], start=True, stop=True)
                    ins.then_inc(hid2_ready, 1)
                if n >= 1:
                    v = n - 1
                    c, r = divmod(v, 2 * E2)
                    e, ht = divmod(r, 2)
                    pe.wait_ge(gelu_done, v + 1)
                    for q in range(4):
                        h, t = divmod(q, 2)
                        if r == 0:
                            pe.wait_ge(acc2_free, 1 + (4 * (c - 1) + q + 1 if c else 0))
                        ins = mm(PS[:, 4 + q, e * C:(e + 1) * C], hid[:, v % 3, h, t * P:(t + 1) * P],
                                 wk[:, W128["w2_2"]][:, r * C:(r + 1) * C], start=(ht == 0), stop=(ht == 1))
                    ins.then_inc(out2_done, 1)

            transpose_y(2)
            for t in range(NP):
                for h in range(2):
                    ins = mm(PS[:, 2 + h, t * A3:(t + 1) * A3], YT[h * C:(h + 1) * C, t, :], w_("wp", h), start=True, stop=True)
            ins.then_inc(proj_ready, 1)
            pe.wait_ge(wx_ready, 1)
            wxv = WX.rearrange("p (j t h) c -> p h t j c", h=2, t=PT)
            for q in range(4):
                h, pt = divmod(q, 2)
                bank = PS[:, 4 + q, 0:J * (C + 1)]
                ins = mm(bank, c_("band"), wxv[:, h, pt], start=True, stop=(pt == 0))
                if pt == 1:
                    ins = mm(bank, c_("band_prev"), wxv[:, h, 0], start=False, stop=True)
                ins.then_inc(window_ready, 1)

            transpose_y(3)
            gate_logits("wg3", E3)
            N3 = 4 * E3
            for n in range(N3 + 1):
                if n < N3:
                    c, e = divmod(n, E3)
                    if n >= 2:
                        pe.wait_ge(prod3_done, n - 1)
                    elif n == 0:
                        pe.wait_ge(gate_ready, 2)
                    for a, name in enumerate(("w1_3", "w2_3")):
                        for h in range(2):
                            ins = mm(PS[:, 2 * (n % 2) + h, a * 256:(a + 1) * 256], w_(name, h)[:, e * P:(e + 1) * P],
                                     yt[h * C:(h + 1) * C, c * 256:(c + 1) * 256], start=True, stop=True)
                    ins.then_inc(hid3_ready, 1)
                if n >= 1:
                    v = n - 1
                    c, e = divmod(v, E3)
                    pe.wait_ge(prod3_done, v + 1)
                    u = v // E2
                    for q in range(4):
                        h, t = divmod(q, 2)
                        if v % E2 == 0 and u >= 1:
                            pe.wait_ge(acc3_free, 4 * (u - 1) + q + 1)
                        ins = mm(PS[:, 4 + q, (e % E2) * C:(e % E2 + 1) * C], hid[:, v % 3, h, t * P:(t + 1) * P],
                                 wk[:, W128["w3"]][:, e * C:(e + 1) * C], start=True, stop=True)
                    ins.then_inc(out3_done, 1)

            pe.wait_ge(final_ready, 1)
            for m in range(2):
                for a in range(4):
                    ins = nc.tensor.transpose(PS[:, m, a * P:(a + 1) * P],
                                              T[:, 2 * (4 * m + a):2 * (4 * m + a) + 2, :].rearrange("p h c -> p (h c)"), ident)
                ins.then_inc(finalT_ready, 1)


def pack(widths, total, parts, height):
    a = np.zeros((height, total), np.float32)
    for name, v in parts.items():
        a[:, widths[name]] = np.asarray(v).reshape(height, -1)
    return a


def kernel(**inputs):
    import concourse.bacc as bacc
    from concourse.bass_utils import run_bass_kernel_spmd

    i = {k: np.asarray(v) for k, v in inputs.items()}

    def taps(w):
        return w.transpose(1, 2, 3, 0).reshape(C, -1)

    arrays = {
        "x": i["x"].reshape(B, C, S),
        "w64": pack(W64, NW64, {
            "w_off": taps(i["L0_conv_w_off"]), "w_dcn": taps(i["L0_conv_w_dcn"]), "w_conv": taps(i["L1_conv_conv_w"]),
            "conv_b": i["L1_conv_conv_b"], "b_dcn": i["L0_conv_b_dcn"],
            "phi": i["L1_conv_phi_w"].reshape(NPHI, STREAMS, C).transpose(2, 1, 0),
            "rms": i["L1_conv_rms_w"].reshape(STREAMS, C).T, "qkv": i["L2_attn_w_qkv"],
            "wg2": i["L2_ffn_Wg"], "wp": i["L3_attn_Wp"].T, "wg3": i["L3_ffn_gate_w"],
            "w1_2": i["L2_ffn_W1"].transpose(1, 0, 2), "w1_3": i["L3_ffn_w1"].transpose(1, 0, 2),
            "w2_3": i["L3_ffn_w2"].transpose(1, 0, 2)}, C),
        "w128": pack(W128, NW128, {
            "proj": i["L2_attn_w_proj"].reshape(4, P, C).transpose(1, 0, 2),
            "b1": i["L2_ffn_b1"].reshape(E2 * 2, P).T,
            "w2_2": i["L2_ffn_W2"].reshape(E2 * 2, P, C).transpose(1, 0, 2),
            "w3": i["L3_ffn_w3"].transpose(1, 0, 2)}, P),
        "rows": pack(ROWS, NROWS, {
            "b_off": i["L0_conv_b_off"], "b_proj": i["L2_attn_b_proj"], "bg2": i["L2_ffn_bg"], "bp": i["L3_attn_bp"],
            "wg": i["L3_attn_Wg"], "bg3": i["L3_ffn_gate_b"], "phi_b": i["L1_conv_phi_b"],
            "alpha": np.concatenate([i["L1_conv_alpha_pre"], i["L1_conv_alpha_post"], i["L1_conv_alpha_res"]])}, 1),
        "b2": i["L2_ffn_b2"],
        "consts": shape_constants(),
    }
    nc = bacc.Bacc("TRN2", target_bir_lowering=False, num_devices=1)
    feeds, args = {}, []
    for name, a in arrays.items():
        feeds[f"in_{name}"] = np.ascontiguousarray(a)
        args.append(nc.dram_tensor(f"in_{name}", list(a.shape), F32, kind="ExternalInput").ap())
    result = nc.dram_tensor("out_0", [B, C, S], F32, kind="ExternalOutput").ap()
    hybrid_kernel(nc, *args, result)
    r = run_bass_kernel_spmd(nc, [feeds], core_ids=[0])
    return r.results[0]["out_0"].reshape(B, C, HH, WW)
```

```python
from contextlib import ExitStack

import numpy as np

import concourse.bass as bass
from concourse import mybir

ALU = mybir.AluOpType
ACT = mybir.ActivationFunctionType
AX = mybir.AxisListType
F32 = mybir.dt.float32
F32R = mybir.dt.float32r

B, C, HH, WW = 8, 64, 16, 16
S = HH * WW
P = 128
J = B // 2
PT = S // P
NP = J * PT
NT = 2 * NP
TAPS = 9
NOFF = 3 * TAPS
PADW = WW + 2
STREAMS = 4
NPHI = 2 * STREAMS + STREAMS * STREAMS
SINKHORN = 20
HEADS = 8
HPAIRS = HEADS // 2
SCALE = float(C) ** -0.5
E2, HID2 = 8, 256
E3, HID3 = 16, 128
A3 = 32
WINDOW = 16
NEG = -1e30
EPS5 = 1e-5


def layout(*fields):
    at, where = 0, {}
    for name, width in fields:
        where[name] = slice(at, at + width)
        at += width
    return where, at


CONST, NCONST = layout(("ident", P), ("pair_mean", P), ("half_mean", P), ("base", PT * 2 * TAPS), ("grid", WW),
                       ("causal", 2 * P), ("band", P), ("band_prev", P), ("sel_half", P), ("sel_image", J),
                       ("desc", E3), ("neg_half", 4), ("euler", 4), ("row0", 1), ("row1", 1))
W64, NW64 = layout(("w_dcn", TAPS * C), ("conv_b", 1), ("b_dcn", 1), ("phi", STREAMS * NPHI), ("rms", STREAMS),
                   ("wg2", E2), ("wp", A3), ("wg3", E3))
WCV, NWCV = layout(("w_off", TAPS * NOFF), ("w_conv", TAPS * C))
WAT, NWAT = layout(("q", HPAIRS * 2 * C), ("k", HPAIRS * C), ("v", HPAIRS * 2 * C), ("p", HPAIRS * C))
W128, NW128 = layout(("b1", 2 * E2), ("w2_2", 2 * E2 * C), ("w3", E3 * C))
ROWS, NROWS = layout(("b_off", NOFF), ("b_proj", C), ("bg2", E2), ("bp", A3), ("wg", A3), ("bg3", E3),
                     ("phi_b", NPHI), ("alpha", 3))
CHUNK = 4
CW = CHUNK * P
NEXP = E2 * HID2


def shape_constants():
    c = np.zeros((P, NCONST), np.float32)
    p = np.arange(P)
    c[:, CONST["ident"]] = np.eye(P)
    c[:, CONST["pair_mean"]] = (p[:, None] // 2 == p[None] // 2) * 0.5
    c[:, CONST["half_mean"]] = (p[:, None] // C == p[None] // C) / C
    base = np.zeros((P, PT, TAPS, 2), np.float32)
    for pt in range(PT):
        s = pt * P + p
        for k in range(TAPS):
            base[:, pt, k, 0] = s // WW - 1 + k // 3
            base[:, pt, k, 1] = s % WW - 1 + k % 3
    c[:, CONST["base"]] = base.reshape(P, -1)
    c[:, CONST["grid"]] = np.arange(WW)
    c[:, CONST["causal"]] = np.concatenate([np.zeros((P, P)), np.where(p[None] <= p[:, None], 0.0, NEG)], 1)
    c[:, CONST["band"]] = (p[:, None] <= p[None]) & (p[:, None] > p[None] - WINDOW)
    c[:, CONST["band_prev"]] = p[:, None] - P > p[None] - WINDOW
    c[:B, CONST["sel_half"]] = np.arange(B)[:, None] // J == p[None] // C
    c[:B, CONST["sel_image"]] = np.arange(B)[:, None] % J == np.arange(J)[None]
    c[:, CONST["desc"]] = E3 - np.arange(E3)
    c[:, CONST["neg_half"]] = -0.5
    c[:, CONST["euler"]] = np.e
    c[:, CONST["row0"]] = p[:, None] == 0
    c[:, CONST["row1"]] = p[:, None] == 1
    return c


IMAGES, STEPS = B, B * HEADS


def projections(a):
    return [("q", a, i) for i in range(HPAIRS)] + [("v", a, i) for i in range(PT)]


def attention_fills(s):
    a, i = divmod(s, HEADS)
    out = []
    if a + 1 < IMAGES and i < 6:
        out.append(projections(a + 1)[i])
    if s in (6, 14):
        out.append(("yA", 2 + s // 8))
    if i == 6 and a >= 3 and a % 2 == 1:
        out.append(("yB", (a - 3) // 2))
    if i == 7 and a >= 3 and a % 2 == 1:
        out.append(("gB", (a - 3) // 2))
    return out


FIRST_FILLS = {10: ("yB", 3), 12: ("gB", 3)}
for _c in range(3):
    for _off, _what in ((12, "yC"), (13, "pC"), (18, "wC"), (24, "yD"), (25, "gD")):
        if 16 * (_c + 1) + _off < 64:
            FIRST_FILLS[16 * (_c + 1) + _off] = (_what, _c)
SECOND_FILLS = {1: ("wC", 2), 6: ("yD", 2), 7: ("gD", 2), 9: ("yC", 3), 10: ("pC", 3), 14: ("wC", 3), 19: ("yD", 3),
                20: ("gD", 3), 27: ("oT", 0), 43: ("oT", 1), 59: ("oT", 2)}
FILLS = [("xT", j) for j in range(J)] + [("yA", 0)] + projections(0) + [("yA", 1)]
for _s in range(STEPS):
    FILLS += attention_fills(_s)
FILLS += [FIRST_FILLS[n] for n in sorted(FIRST_FILLS)] + [SECOND_FILLS[n] for n in sorted(SECOND_FILLS)] + [("oT", 3)]
FILL = {name: n for n, name in enumerate(FILLS)}


def hybrid_kernel(nc, x, w64, wcv, wat, w128, wexp, rows, b2, consts, out):
    with ExitStack() as ctx:
        def sem(name):
            return ctx.enter_context(nc.semaphore(name))

        def tensor(stack, name, *shape, dtype=F32):
            return stack.enter_context(nc.sbuf_tensor(name, [P, *shape], dtype))

        PS = ctx.enter_context(nc.psum_tensor("PS", [P, 8, 512], F32))

        def sb(name, *shape, dtype=F32):
            return tensor(ctx, name, *shape, dtype=dtype)

        cst = sb("cst", NCONST)
        wc = sb("wc", NW64)
        wk = sb("wk", NW128)
        rw = sb("rw", NROWS)
        b2row = sb("b2row", E2 * C)
        b2hi = sb("b2hi", E2 * C)
        b2s = sb("b2s", E2 * C, dtype=F32R)
        ones = sb("ones", P, dtype=F32R)
        score_arena = sb("score_arena", 9 * 384 + 774)
        w_off = score_arena[:, 2592:3078].rearrange("p (k n) -> p k n", k=TAPS)
        w_conv = score_arena[:, 3078:4230].rearrange("p (k n) -> p k n", k=TAPS)
        G2 = score_arena[:, 1296:2592].rearrange("p (j y x) -> p j y x", j=J, y=PADW)
        X = sb("X", J, S)
        X1 = sb("X1", J, S)
        stat = sb("stat", J, 6)
        mv = sb("mv", 2, J, 2)
        gmv = sb("gmv", J, 2)
        small = sb("small", 64)
        T = sb("T", NT, C)
        Y = sb("Y", NT, C)
        Y2 = sb("Y2", NT, 2 * C)
        YTs = sb("YTs", NT * P, dtype=F32R)
        lnst = sb("lnst", 3, NT)
        AVH = sb("AVH", 3 * 512, dtype=F32R)
        AVL = sb("AVL", 3 * 512, dtype=F32R)
        swh = sb("swh", E2 + A3 + E3, dtype=F32R)
        swl = sb("swl", E2 + A3 + E3, dtype=F32R)
        coord = sb("coord", NT, 2 * TAPS)
        mask = sb("mask", NT, TAPS)
        D = sb("D", 2, P)
        weff = sb("weff", NPHI)
        phr = sb("phr", STREAMS, NPHI)
        PB = sb("PB", B)
        cf = sb("cf", NPHI)
        M = sb("M", STREAMS, STREAMS)
        mn = sb("mn", STREAMS)
        V = sb("V", 4)
        V3 = sb("V3", J, 3)
        CB = sb("CB", J, 3)
        bb = sb("bb", J)
        MS, PR, PTs = (score_arena[:, o * 1152:(o + 1) * 1152].rearrange("p (u n) -> p u n", u=3) for o in range(3))
        nmx = sb("nmx", 3, 2)
        rsum = sb("rsum", 2, PT, HEADS)
        rinv = sb("rinv", 2, PT, HEADS)
        tg = sb("tg", 8, CHUNK * E3)
        gate = sb("gate", 2, NT, E3)
        PJ = sb("PJ", CHUNK, A3)
        WX = sb("WX", CHUNK, C + 1)
        wy_t = sb("wy", CHUNK, C)

        with ExitStack() as early:
            hats_t = tensor(early, "hats", NT, 2 * TAPS, WW)
            U = tensor(early, "U", NT, TAPS * C)
            prods = [tensor(early, f"prod{n}", TAPS, S) for n in range(2)]
            st_mem = tensor(early, "st_mem", 4608)
            ST = [st_mem[:, o:o + 2304].rearrange("p (k q) -> p k q", q=P) for o in (0, 2304)]
            G = st_mem[:, 0:3 * J * PADW * WW].rearrange("p (k j y x) -> p k j y x", k=3, j=J, y=PADW)
            GH = tensor(early, "GH", J, S, dtype=F32R)
            GL = tensor(early, "GL", J, S, dtype=F32R)
            DH = tensor(early, "DH", TAPS * C, dtype=F32R)
            DL = tensor(early, "DL", TAPS * C, dtype=F32R)
            wa = tensor(early, "wa", NWAT)
        hats = hats_t[:]
        av = prods[0][:].rearrange("p k q -> p (k q)")[:, 0:3 * 512]
        QH = sb("QH", 2, HEADS, S, dtype=F32R)
        QL = sb("QL", 2, HEADS, S, dtype=F32R)
        VV = sb("VV", 2, PT, HEADS * C)
        pr8 = sb("pr8", CHUNK, E2 * C)
        stage = sb("stage", NEXP)
        WH = sb("WH", 3, NEXP, dtype=F32R)
        WL = sb("WL", 3, NEXP, dtype=F32R)
        hid = sb("hid", 3, CW)
        sil = VV[:, 0]

        def c_(name):
            return cst[:, CONST[name]]

        SW = {"wg2": slice(0, E2), "wp": slice(E2, E2 + A3), "wg3": slice(E2 + A3, E2 + A3 + E3)}
        SMALL64 = slice(W64["wg2"].start, W64["wg3"].stop)

        def w_(name, h=None):
            return wc[:, W64[name]] if h is None else wc[h * C:(h + 1) * C, W64[name]]

        ident = c_("ident")

        def img(t):
            return t[:].rearrange("p j (y x) -> p j y x", y=HH)

        x_loaded = sem("x_loaded")
        const_loaded = sem("const_loaded")
        rows_loaded = sem("rows_loaded")
        w64_loaded = sem("w64_loaded")
        wat_loaded = sem("wat_loaded")
        w128_loaded = sem("w128_loaded")
        b2_loaded = sem("b2_loaded")
        block_zeroed = sem("block_zeroed")
        off_block_loaded = sem("off_block_loaded")
        conv_block_loaded = sem("conv_block_loaded")
        pads_zeroed = sem("pads_zeroed")
        b2s_zeroed = sem("b2s_zeroed")
        b2s_ready = sem("b2s_ready")
        dve_step = sem("dve_step")
        act_step = sem("act_step")
        pool_step = sem("pool_step")
        moments_ready = sem("moments_ready")
        group_moments_ready = sem("group_moments_ready")
        var_ready = sem("var_ready")
        sd_ready = sem("sd_ready")
        norm_ready = sem("norm_ready")
        g_ready = sem("g_ready")
        g_shifted_ready = sem("g_shifted_ready")
        gh_ready = sem("gh_ready")
        gl_ready = sem("gl_ready")
        dh_ready = sem("dh_ready")
        dl_ready = sem("dl_ready")
        swh_ready = sem("swh_ready")
        swl_ready = sem("swl_ready")
        offsets_ready = sem("offsets_ready")
        mask_logits_ready = sem("mask_logits_ready")
        mask_ready = sem("mask_ready")
        hat_diff_ready = sem("hat_diff_ready")
        hat_ready = sem("hat_ready")
        u_ready = sem("u_ready")
        u_copied = sem("u_copied")
        prod_ready = sem("prod_ready")
        st_ready = sem("st_ready")
        st_copied = sem("st_copied")
        d_ready = sem("d_ready")
        d_copied = sem("d_copied")
        dT_ready = sem("dT_ready")
        x1_tile_ready = sem("x1_tile_ready")
        sq_ready = sem("sq_ready")
        q_ready = sem("q_ready")
        qe_ready = sem("qe_ready")
        qs_ready = sem("qs_ready")
        pb_ready = sem("pb_ready")
        coef_ready = sem("coef_ready")
        logits_ready = sem("logits_ready")
        gates_ready = sem("gates_ready")
        v3_ready = sem("v3_ready")
        cb_ready = sem("cb_ready")
        conv_ready = sem("conv_ready")
        x2_ready = sem("x2_ready")
        av_ready = sem("av_ready")
        avh_ready = sem("avh_ready")
        avl_ready = sem("avl_ready")
        stage_loaded = sem("stage_loaded")
        stage_split = sem("stage_split")
        misc_filled = sem("misc_filled")
        misc_free = sem("misc_free")
        lnvar_ready = sem("lnvar_ready")
        lninv_ready = sem("lninv_ready")
        y2_ready = sem("y2_ready")
        centered_ready = sem("centered_ready")
        proj_added = sem("proj_added")
        qh_copied = sem("qh_copied")
        scores_ready = sem("scores_ready")
        masked_ready = sem("masked_ready")
        probs_ready = sem("probs_ready")
        pT_ready = sem("pT_ready")
        pT_copied = sem("pT_copied")
        pv_done = sem("pv_done")
        heads_normed = sem("heads_normed")
        fold_done = sem("fold_done")
        top_diff_ready = sem("top_diff_ready")
        top_exp_ready = sem("top_exp_ready")
        gate_ready = sem("gate_ready")
        hid2_ready = sem("hid2_ready")
        gelu_done = sem("gelu_done")
        out2_done = sem("out2_done")
        acc_free = sem("acc_free")
        tanh_done = sem("tanh_done")
        z_ready = sem("z_ready")
        ez_ready = sem("ez_ready")
        wx_ready = sem("wx_ready")
        hid3_ready = sem("hid3_ready")
        silu_done = sem("silu_done")
        prod3_done = sem("prod3_done")
        out3_done = sem("out3_done")
        stored = sem("stored")

        STG = (4, 4, 4, 4, 2)
        NG = len(STG)

        block = ctx.enter_context(nc.Block())

        @block.sync
        def _(sp):
            for h in range(2):
                sp.dma_start(X[h * C:(h + 1) * C], x[h * J:(h + 1) * J].rearrange("j c s -> c j s")).then_inc(x_loaded, 16)
            sp.dma_start(cst[:], consts).then_inc(const_loaded, 16)
            sp.wait_ge(block_zeroed, 1)
            for h in range(2):
                sp.dma_start(w_off[h * C:(h + 1) * C, :, h * NOFF:(h + 1) * NOFF],
                             wcv[:, WCV["w_off"]].rearrange("c (t o) -> c t o", t=TAPS)).then_inc(off_block_loaded, 16)
            for h in range(2):
                sp.dma_start(wc[h * C:(h + 1) * C, :], w64).then_inc(w64_loaded, 16)
            sp.wait_ge(block_zeroed, 2)
            for h in range(2):
                sp.dma_start(w_conv[h * C:(h + 1) * C, :, h * C:(h + 1) * C],
                             wcv[:, WCV["w_conv"]].rearrange("c (t o) -> c t o", t=TAPS)).then_inc(conv_block_loaded, 16)
            sp.dma_start(wa[:], wat).then_inc(wat_loaded, 16)
            sp.dma_start(wk[:], w128).then_inc(w128_loaded, 16)
            sp.dma_start(b2row[0:2, :], b2.to_broadcast([2, E2 * C])).then_inc(b2_loaded, 16)
            for m in range(3):
                if m == 0:
                    sp.wait_ge(x1_tile_ready, NP)
                    sp.wait_ge(avl_ready, 1)
                else:
                    sp.wait_ge(stage_split, m)
                for h in range(2):
                    sp.dma_start(stage[h * C:(h + 1) * C, :], wexp[m]).then_inc(stage_loaded, 16)
            for c in range(J):
                sp.wait_ge(misc_free, FILL["oT", c] + 1)
                for h in range(2):
                    for pt in range(PT):
                        sp.dma_start(out[h * J + c, :, pt * P:(pt + 1) * P], X[pt * C:(pt + 1) * C, c, h * P:(h + 1) * P]).then_inc(stored, 16)
            sp.wait_ge(stored, 16 * J * 2 * PT)

        @block.gpsimd
        def _(pool):
            steps = [0]

            def step(ins):
                ins.then_inc(pool_step, 1)
                steps[0] += 1

            def settle():
                pool.wait_ge(pool_step, steps[0])

            nc.gpsimd.memset(w_off, 0.0).then_inc(block_zeroed, 1)
            nc.gpsimd.memset(G, 0.0).then_inc(pads_zeroed, 1)
            nc.gpsimd.memset(w_conv, 0.0).then_inc(block_zeroed, 1)
            nc.gpsimd.memset(G2, 0.0).then_inc(pads_zeroed, 1)
            nc.gpsimd.memset(PB[:], 0.0).then_inc(pads_zeroed, 1)
            nc.gpsimd.memset(b2s[:].bitcast(F32), 0.0).then_inc(b2s_zeroed, 1)
            nc.gpsimd.memset(ones[:].bitcast(F32), 1.0).then_inc(b2s_zeroed, 1)
            for j in range(J):
                pool.wait_ge(gh_ready, j + 1)
                pool.wait_ge(g_ready, j + 1)
                nc.gpsimd.tensor_tensor(GL[:, j].rearrange("p (y x) -> p y x", y=HH), G[:, 1, j, 1:HH + 1, :],
                                        GH[:, j].rearrange("p (y x) -> p y x", y=HH).bitcast(F32), ALU.subtract).then_inc(gl_ready, 1)
                if j == 0:
                    pool.wait_ge(dh_ready, 1)
                    pool.wait_ge(w64_loaded, 32)
                    nc.gpsimd.tensor_tensor(DL[:], w_("w_dcn"), DH[:].bitcast(F32), ALU.subtract).then_inc(dl_ready, 1)
            pool.wait_ge(swh_ready, 1)
            nc.gpsimd.tensor_tensor(swl[:], wc[:, SMALL64], swh[:].bitcast(F32), ALU.subtract).then_inc(swl_ready, 1)
            pool.wait_ge(b2_loaded, 16)
            pool.wait_ge(const_loaded, 16)
            pool.wait_ge(b2s_zeroed, 2)
            step(nc.gpsimd.tensor_copy(b2hi[0:2].bitcast(F32R), b2row[0:2]))
            settle()
            step(nc.gpsimd.tensor_tensor(b2row[0:2], b2row[0:2], b2hi[0:2], ALU.subtract))
            step(nc.gpsimd.tensor_scalar(b2hi[0:2], b2hi[0:2], cst[0:2, CONST["row0"]], None, ALU.mult))
            settle()
            step(nc.gpsimd.tensor_scalar(b2row[0:2], b2row[0:2], cst[0:2, CONST["row1"]], None, ALU.mult))
            settle()
            nc.gpsimd.tensor_tensor(b2s[0:2], b2row[0:2], b2hi[0:2], ALU.add).then_inc(b2s_ready, 1)
            pool.wait_ge(avh_ready, 4)
            nc.gpsimd.tensor_tensor(AVL[:], av, AVH[:].bitcast(F32), ALU.subtract).then_inc(avl_ready, 1)

            norms = [0]

            def ln_power(X_, c):
                norms[0] += 1
                pool.wait_ge(lnvar_ready, norms[0])
                cols = slice(4 * c, 4 * c + 4)
                nc.gpsimd.tensor_tensor(lnst[:, 2, cols], lnst[:, 1, cols], c_("neg_half"), ALU.pow).then_inc(lninv_ready, 1)

            tops = [0]

            def top_power():
                tops[0] += 1
                pool.wait_ge(top_diff_ready, tops[0])
                nc.gpsimd.tensor_tensor(tg[:, 5, 0:CHUNK], c_("euler"), tg[:, 4, 0:CHUNK], ALU.pow).then_inc(top_exp_ready, 1)

            zs = [0]

            def z_power():
                zs[0] += 1
                pool.wait_ge(z_ready, zs[0])
                nc.gpsimd.tensor_tensor(tg[:, 6, 16:16 + CHUNK], c_("euler"), tg[:, 6, 0:CHUNK], ALU.pow).then_inc(ez_ready, 1)

            def fold(first, n, tiles):
                buf = pr8[:, first:first + n, :]
                for width in (4 * C, 2 * C, C):
                    step(nc.gpsimd.tensor_tensor(buf[:, :, 0:width], buf[:, :, 0:width], buf[:, :, width:2 * width], ALU.add))
                    settle()
                tt = T[:, tiles, :]
                nc.gpsimd.tensor_tensor(tt, tt, buf[:, :, 0:C], ALU.add).then_inc(fold_done, 1)

            def split_stage(m):
                pool.wait_ge(stage_loaded, 32 * (m + 1))
                step(nc.gpsimd.tensor_copy(WH[:, m], stage[:]))
                settle()
                nc.gpsimd.tensor_tensor(WL[:, m], stage[:], WH[:, m].bitcast(F32), ALU.subtract).then_inc(stage_split, 1)

            pool.wait_ge(rows_loaded, 16)
            for j in range(J):
                ln_power("A", j)
            for j in range(J):
                pool.wait_ge(centered_ready, j + 1)
                tt = T[:, 4 * j:4 * j + 4, :]
                nc.gpsimd.tensor_tensor(tt, tt, rw[:, ROWS["b_proj"]].unsqueeze(1).to_broadcast([P, CHUNK, C]), ALU.add).then_inc(proj_added, 1)
            pool.wait_ge(proj_added, J)
            split_stage(0)
            for s in range(STEPS + 2):
                a, i = divmod(s, HEADS)
                if i == 1 and a >= 1:
                    pool.wait_ge(heads_normed, a)
                    fold(2 * ((a - 1) % 2), PT, slice(2 * (a - 1), 2 * a))
                if s in (12, 20):
                    split_stage(s // 8)
                if i == 2 and a in (4, 6):
                    top_power()
                if i == 7 and a in (2, 4, 6):
                    ln_power("B", (a - 2) // 2)
            top_power()
            ln_power("B", 3)
            top_power()

            for c in range(J):
                pool.wait_ge(acc_free, 4 * (c + 1))
                fold(0, CHUNK, slice(4 * c, 4 * c + 4))
                if c >= 1:
                    ln_power("D", c - 1)
                if c < 3:
                    if c >= 1:
                        top_power()
                    ln_power("C", c)
                    z_power()
            ln_power("C", 3)
            top_power()
            for u in range(8):
                if u == 1:
                    z_power()
                if u == 2:
                    ln_power("D", 3)
                    top_power()
                pool.wait_ge(acc_free, 16 + 4 * (u + 1))
                fold(0, CHUNK, slice(4 * (u // 2), 4 * (u // 2) + 4))

        @block.scalar
        def _(act):
            act.dma_start(rw[:], rows.to_broadcast([P, NROWS])).then_inc(rows_loaded, 16)

            def sqrt(n, ap):
                act.wait_ge(var_ready, n)
                nc.scalar.activation(ap, ap, ACT.Sqrt).then_inc(sd_ready, 1)

            sqrt(1, small[:, 0:J])
            act.wait_ge(norm_ready, 1)
            act.wait_ge(pads_zeroed, 1)
            for j in range(J):
                for k, to, frm in ((0, slice(1, WW), slice(0, WW - 1)), (2, slice(0, WW - 1), slice(1, WW))):
                    nc.scalar.activation(G[:, k, j, 1:HH + 1, to], img(X)[:, j, :, frm], ACT.Identity, bias=small[:, 12 + j:13 + j],
                                         scale=small[:, 4 + j:5 + j]).then_inc(g_shifted_ready, 1)
            for j in range(J):
                act.wait_ge(g_ready, j + 1)
                nc.scalar.activation(GH[:, j].rearrange("p (y x) -> p y x", y=HH), G[:, 1, j, 1:HH + 1, :], ACT.Copy).then_inc(gh_ready, 1)
                if j == 0:
                    act.wait_ge(w64_loaded, 32)
                    nc.scalar.activation(DH[:], w_("w_dcn"), ACT.Copy).then_inc(dh_ready, 1)
            nc.scalar.activation(swh[:], wc[:, SMALL64], ACT.Copy).then_inc(swh_ready, 1)
            act.wait_ge(mask_logits_ready, 4)
            nc.scalar.activation(mask[:], mask[:], ACT.Sigmoid).then_inc(mask_ready, 1)
            for j in range(J):
                act.wait_ge(hat_diff_ready, j + 1)
                hj = hats[:, 4 * j:4 * j + 4].rearrange("p t k q -> p (t k q)")
                nc.scalar.activation(hj, hj, ACT.Abs).then_inc(act_step, 1)
                act.wait_ge(act_step, j + 1)
                nc.scalar.activation(hj, hj, ACT.Relu, bias=1.0, scale=-1.0).then_inc(hat_ready, 1)
            for n in range(NT):
                act.wait_ge(u_ready, n // 2 + 1)
                slot = 1 + 2 * (n % 3)
                nc.scalar.activation(U[:, n, :].rearrange("p (a n) -> p a n", a=2), PS[:, slot:slot + 2, 0:288],
                                     ACT.Copy).then_inc(u_copied, 1)
            for n in range(NT):
                if n >= 2:
                    act.wait_ge(d_ready, n - 1)
                for g in range(NG):
                    m = n * NG + g
                    act.wait_ge(st_ready, m + 1)
                    nc.scalar.activation(ST[n % 2][:, 4 * g:4 * g + STG[g], :],
                                         PS[:, 1 + m % 4, 0:STG[g] * P].rearrange("p (a n) -> p a n", n=P),
                                         ACT.Copy).then_inc(st_copied, 1)
            sqrt(2, small[:, 0:J])
            act.wait_ge(qe_ready, 1)
            nc.scalar.activation(small[:, 8:8 + J], small[:, 8:8 + J], ACT.Sqrt).then_inc(qs_ready, 1)
            act.wait_ge(logits_ready, 1)
            nc.scalar.activation(cf[0:B, 0:2 * STREAMS], cf[0:B, 0:2 * STREAMS], ACT.Sigmoid).then_inc(gates_ready, 1)
            nc.scalar.activation(M[0:B].rearrange("p a b -> p (a b)"), cf[0:B, 2 * STREAMS:NPHI], ACT.Exp).then_inc(gates_ready, 1)
            act.wait_ge(av_ready, 1)
            for to in (AVH[:], av):
                nc.scalar.activation(to[:, 0:1024].rearrange("p (a n) -> p a n", a=2), PS[:, 4:6, :], ACT.Copy).then_inc(avh_ready, 1)
                nc.scalar.activation(to[:, 1024:1536].rearrange("p (a n) -> p a n", a=2), PS[:, 6:8, 0:256], ACT.Copy).then_inc(avh_ready, 1)

            def project(a, i):
                if i < HPAIRS:
                    act.wait_ge(misc_filled, FILL["q", a, i] + 1)
                    nc.scalar.activation(QH[:, a % 2, 2 * i:2 * i + 2, :].rearrange("p g n -> p (g n)"), PS[:, 7, :], ACT.Copy).then_inc(qh_copied, 1)
                else:
                    act.wait_ge(misc_filled, FILL["v", a, i - HPAIRS] + 1)
                    nc.scalar.activation(VV[:, a % 2, i - HPAIRS, :], PS[:, 7, :], ACT.Copy).then_inc(misc_free, 1)

            def copy_probs(v):
                act.wait_ge(pT_ready, v + 1)
                if v >= 3:
                    act.wait_ge(pv_done, v - 2)
                nc.scalar.activation(PTs[:, v % 3, :], PS[:, 3 + v % 2, 0:384], ACT.Copy).then_inc(pT_copied, 1)

            for i in range(6):
                project(0, i)
            for s in range(STEPS + 1):
                if s < STEPS:
                    a, g = divmod(s, HEADS)
                    act.wait_ge(masked_ready, s + 1)
                    if s >= 3:
                        act.wait_ge(pT_ready, s - 2)
                    if g == 0 and a >= 2:
                        act.wait_ge(heads_normed, a - 1)
                    for qt in range(PT):
                        cols = slice(0, P) if qt == 0 else slice(P, 3 * P)
                        ins = nc.scalar.activation(PR[:, s % 3, cols], MS[:, s % 3, cols], ACT.Exp, bias=nmx[:, s % 3, qt:qt + 1],
                                                   scale=-1.0, accum_out=rsum[:, a % 2, qt, g:g + 1])
                    ins.then_inc(probs_ready, 1)
                if s >= 1:
                    copy_probs(s - 1)
                if s < STEPS and a + 1 < IMAGES and g < 6:
                    project(a + 1, g)

            act.wait_ge(w128_loaded, 16)

            def tanh(c):
                act.wait_ge(misc_free, FILL["pC", c] + 1)
                nc.scalar.activation(PJ[:], PJ[:], ACT.Tanh).then_inc(tanh_done, 1)

            for n in range(4 * E2 * 2):
                e2 = n % (2 * E2)
                act.wait_ge(hid2_ready, n + 1)
                if n >= 3:
                    act.wait_ge(out2_done, n - 2)
                nc.scalar.activation(hid[:, n % 3], PS[:, n % 3, :], ACT.Gelu,
                                     bias=wk[:, W128["b1"]][:, e2:e2 + 1]).then_inc(gelu_done, 1)
                if n in (31, 47, 63):
                    tanh(n // 16 - 1)

            for n in range(4 * E3):
                act.wait_ge(hid3_ready, 2 * n + 1)
                if n >= 2:
                    act.wait_ge(prod3_done, n - 1)
                nc.scalar.activation(sil[:, n % 2], PS[:, 2 * n % 3, :], ACT.Silu).then_inc(silu_done, 1)
                if n == 12:
                    tanh(3)

        @block.vector
        def _(dve):
            steps = [0]

            def step(ins):
                ins.then_inc(dve_step, 1)
                steps[0] += 1

            def settle():
                dve.wait_ge(dve_step, steps[0])

            def group_norm(n, src, dst):
                for j in range(J):
                    step(nc.vector.bn_stats(stat[:, j, :], src[:, j, :]))
                settle()
                for j in range(J):
                    step(nc.vector.bn_aggr(mv[:, n, j, :], stat[:, j, :]))
                settle()
                mean, var = mv[:, n, :, 0], mv[:, n, :, 1]
                step(nc.vector.tensor_tensor(small[:, 0:J], mean, mean, ALU.mult))
                settle()
                nc.vector.tensor_tensor(var, var, small[:, 0:J], ALU.add).then_inc(moments_ready, 1)
                dve.wait_ge(group_moments_ready, n + 1)
                step(nc.vector.tensor_copy(gmv[:].rearrange("p j m -> p (j m)"), PS[:, 7, 0:2 * J]))
                settle()
                step(nc.vector.tensor_tensor(small[:, 4:4 + J], gmv[:, :, 0], gmv[:, :, 0], ALU.mult))
                settle()
                step(nc.vector.tensor_tensor(small[:, 0:J], gmv[:, :, 1], small[:, 4:4 + J], ALU.subtract))
                settle()
                nc.vector.tensor_scalar(small[:, 0:J], small[:, 0:J], EPS5, None, ALU.add).then_inc(var_ready, 1)
                dve.wait_ge(sd_ready, n + 1)
                step(nc.vector.reciprocal(small[:, 4:4 + J], small[:, 0:J]))
                settle()
                nc.vector.scalar_tensor_tensor(small[:, 12:12 + J], gmv[:, :, 0], -1.0, small[:, 4:4 + J], ALU.mult,
                                               ALU.mult).then_inc(norm_ready, 1)
                dve.wait_ge(norm_ready, n + 1)
                dve.wait_ge(pads_zeroed, n + 1)
                for j in range(J):
                    nc.vector.tensor_scalar(dst[:, j], img(src)[:, j], small[:, 4 + j:5 + j],
                                            small[:, 12 + j:13 + j], ALU.mult, ALU.add).then_inc(g_ready, 1)

            dve.wait_ge(x_loaded, 32)
            group_norm(0, X, G[:, 1, :, 1:HH + 1, :])

            dve.wait_ge(w64_loaded, 32)
            dve.wait_ge(rows_loaded, 16)
            dve.wait_ge(const_loaded, 16)
            step(nc.vector.tensor_tensor(phr[:], w_("phi").rearrange("p (n o) -> p n o", n=STREAMS),
                                         w_("rms").unsqueeze(2).to_broadcast([P, STREAMS, NPHI]), ALU.mult))
            step(nc.vector.tensor_tensor(c_("base").rearrange("p (a k) -> p a k", a=PT), c_("base").rearrange("p (a k) -> p a k", a=PT),
                                         rw[:, ROWS["b_off"]][:, 0:2 * TAPS].unsqueeze(1).to_broadcast([P, PT, 2 * TAPS]), ALU.add))
            settle()
            step(nc.vector.tensor_reduce(weff[:], phr[:].rearrange("p n o -> p o n"), AX.X, ALU.add))

            dve.wait_ge(offsets_ready, 1)
            om = PS[:, 0, 0:NP * 2 * NOFF].rearrange("p (j t h o) -> p t h j o", j=J, t=PT, h=2)
            co = coord[:].rearrange("p (j t h) k -> p t h j k", h=2, j=J)
            mo = mask[:].rearrange("p (j t h) k -> p t h j k", h=2, j=J)
            for t in range(PT):
                for h in range(2):
                    nc.vector.tensor_tensor(mo[:, t, h], om[:, t, h, :, 2 * TAPS:NOFF],
                                            rw[:, ROWS["b_off"]][:, 2 * TAPS:NOFF].unsqueeze(1).to_broadcast([P, J, TAPS]),
                                            ALU.add).then_inc(mask_logits_ready, 1)
            for t in range(PT):
                for h in range(2):
                    step(nc.vector.tensor_tensor(co[:, t, h], om[:, t, h, :, 0:2 * TAPS],
                                                 c_("base").rearrange("p (a k) -> p a k", a=PT)[:, t].unsqueeze(1).to_broadcast([P, J, 2 * TAPS]), ALU.add))
            settle()
            def chunk(j):
                return hats[:, 4 * j:4 * j + 4].rearrange("p t k q -> p (t k) q")

            for j in range(J):
                nc.vector.tensor_tensor(chunk(j), coord[:, 4 * j:4 * j + 4].rearrange("p t k -> p (t k)").unsqueeze(2).to_broadcast([P, 8 * TAPS, WW]),
                                        c_("grid").unsqueeze(1).to_broadcast([P, 8 * TAPS, WW]), ALU.subtract).then_inc(hat_diff_ready, 1)

            def x1_tile(ip):
                j, pt = divmod(ip, PT)
                dve.wait_ge(dT_ready, ip + 1)
                nc.vector.scalar_tensor_tensor(X1[:, j, pt * P:(pt + 1) * P], PS[:, 7 * (ip % 2), 0:P], w_("b_dcn"),
                                               X[:, j, pt * P:(pt + 1) * P], ALU.add, ALU.add).then_inc(x1_tile_ready, 1)

            def d_copy(ip):
                dve.wait_ge(d_ready, 2 * ip + 2)
                if ip >= 2:
                    dve.wait_ge(dT_ready, ip - 1)
                nc.vector.tensor_copy(D[:, ip % 2, :], PS[:, 5 + ip % 2, 0:P]).then_inc(d_copied, 1)

            for n in range(NT):
                if n % 4 == 0:
                    dve.wait_ge(hat_ready, n // 4 + 1)
                    dve.wait_ge(mask_ready, 1)
                    hx = chunk(n // 4).rearrange("p (k c) q -> p c k q", c=2)[:, 1]
                    step(nc.vector.tensor_tensor(hx, hx, mask[:, n:n + 4].rearrange("p t k -> p (t k)").unsqueeze(2).to_broadcast([P, 4 * TAPS, WW]),
                                                 ALU.mult))
                    settle()
                if n >= 2:
                    dve.wait_ge(st_ready, NG * (n - 1))
                hk = hats[:, n].rearrange("p (k c) q -> p c k q", c=2)
                nc.vector.tensor_tensor(prods[n % 2].rearrange("p k (a b) -> p k a b", a=HH),
                                        hk[:, 0].unsqueeze(3).to_broadcast([P, TAPS, HH, WW]),
                                        hk[:, 1].unsqueeze(2).to_broadcast([P, TAPS, HH, WW]), ALU.mult).then_inc(prod_ready, 1)
                if n >= 4 and n % 2 == 0:
                    d_copy(n // 2 - 2)
                if n >= 5 and n % 2 == 1:
                    x1_tile(n // 2 - 2)
            for ip in range(NP - 2, NP):
                d_copy(ip)
                x1_tile(ip)
            dve.wait_ge(x1_tile_ready, NP)

            group_norm(1, X1, G2[:, :, 1:HH + 1, 1:WW + 1])
            pooled = small[:, 16:16 + J]
            step(nc.vector.tensor_tensor(pooled, mv[:, 1, :, 0], gmv[:, :, 0], ALU.subtract))
            settle()
            step(nc.vector.tensor_tensor(pooled, pooled, small[:, 4:4 + J], ALU.mult))
            settle()
            nc.vector.tensor_tensor(small[:, 20:20 + J], pooled, pooled, ALU.mult).then_inc(sq_ready, 1)
            dve.wait_ge(q_ready, 1)
            nc.vector.tensor_scalar(small[:, 8:8 + J], PS[:, 3, 0:J], 1e-20, None, ALU.add).then_inc(qe_ready, 1)
            dve.wait_ge(qs_ready, 1)
            step(nc.vector.reciprocal(small[:, 24:24 + J], small[:, 8:8 + J]))
            settle()
            dve.wait_ge(pads_zeroed, 3)
            for h in range(2):
                hs = slice(h * C, (h + 1) * C)
                nc.vector.tensor_tensor(PB[hs, h * J:(h + 1) * J], pooled[hs], small[hs, 24:24 + J], ALU.mult).then_inc(pb_ready, 1)
            dve.wait_ge(coef_ready, 1)
            step(nc.vector.tensor_tensor(cf[0:B], PS[0:B, 3, 0:NPHI], rw[0:B, ROWS["phi_b"]], ALU.add))
            settle()
            al = rw[0:B, ROWS["alpha"]]
            step(nc.vector.tensor_scalar(cf[0:B, 0:4], cf[0:B, 0:4], al[:, 0:1], None, ALU.mult))
            step(nc.vector.tensor_scalar(cf[0:B, 4:8], cf[0:B, 4:8], al[:, 1:2], None, ALU.mult))
            step(nc.vector.tensor_scalar(cf[0:B, 8:NPHI], cf[0:B, 8:NPHI], al[:, 2:3], None, ALU.mult))
            settle()
            nc.vector.tensor_copy(V[0:B, 3:4], cf[0:B, 0:1]).then_inc(logits_ready, 1)
            dve.wait_ge(gates_ready, 2)
            MM = M[0:B]
            for _ in range(SINKHORN):
                for view in (MM, MM.rearrange("p a b -> p b a")):
                    step(nc.vector.tensor_reduce(mn[0:B], view, AX.X, ALU.add))
                    settle()
                    step(nc.vector.reciprocal(mn[0:B], mn[0:B]))
                    settle()
                    step(nc.vector.tensor_tensor(view, view, mn[0:B].unsqueeze(2).to_broadcast([B, STREAMS, STREAMS]), ALU.mult))
                    settle()
            step(nc.vector.tensor_reduce(V[0:B, 0:1], MM.rearrange("p a b -> p (a b)")[:, 0:16:5], AX.X, ALU.add))
            step(nc.vector.tensor_reduce(V[0:B, 1:2], cf[0:B, 0:4], AX.X, ALU.add))
            step(nc.vector.tensor_reduce(V[0:B, 2:3], cf[0:B, 4:8], AX.X, ALU.add))
            settle()
            step(nc.vector.tensor_scalar(V[0:B, 0:1], V[0:B, 0:1], 0.25, None, ALU.mult))
            step(nc.vector.tensor_scalar(V[0:B, 2:3], V[0:B, 2:3], 0.5, None, ALU.mult))
            settle()
            step(nc.vector.tensor_tensor(V[0:B, 1:2], V[0:B, 1:2], V[0:B, 2:3], ALU.mult))
            settle()
            nc.vector.tensor_tensor(V3[0:B], V[0:B, 0:3].unsqueeze(1).to_broadcast([B, J, 3]),
                                    cst[0:B, CONST["sel_image"]].unsqueeze(2).to_broadcast([B, J, 3]), ALU.mult).then_inc(v3_ready, 1)
            dve.wait_ge(cb_ready, 1)
            step(nc.vector.tensor_copy(CB[:].rearrange("p a b -> p (a b)"), PS[:, 3, 0:3 * J]))
            settle()
            step(nc.vector.tensor_scalar(bb[:], CB[:, :, 2], w_("conv_b"), None, ALU.mult))
            settle()
            for j in range(J):
                step(nc.vector.tensor_scalar(X1[:, j], X1[:, j], bb[:, j:j + 1], None, ALU.add))
            settle()
            for j in range(J):
                step(nc.vector.scalar_tensor_tensor(img(X1)[:, j], G2[:, j, 1:HH + 1, 1:WW + 1], CB[:, j, 0:1],
                                                    img(X1)[:, j], ALU.mult, ALU.add))
            settle()
            for j in range(J):
                dve.wait_ge(conv_ready, j // 2 + 1)
                nc.vector.scalar_tensor_tensor(X1[:, j], PS[:, 1 + j // 2, (j % 2) * S:(j % 2 + 1) * S], CB[:, j, 1:2],
                                               X1[:, j], ALU.mult, ALU.add).then_inc(x2_ready, 1)
            for j in range(J):
                dve.wait_ge(misc_filled, FILL["xT", j] + 1)
                for h in range(2):
                    ins = nc.vector.tensor_copy(T[:, 4 * j + 2 * h:4 * j + 2 * h + 2, :],
                                                PS[:, 7, 0:2 * P].rearrange("p (t h c) -> p h t c", h=2, c=C)[:, h])
                    if h == 0:
                        step(ins)
                ins.then_inc(misc_free, 1)
                dve.wait_ge(misc_free, FILL["xT", j] + 1)

            norms = [0]

            def ln_stats(c):
                ts = slice(4 * c, 4 * c + 4)
                settle()
                step(nc.vector.tensor_reduce(lnst[:, 0, ts], T[:, ts], AX.X, ALU.add))
                settle()
                step(nc.vector.tensor_scalar(lnst[:, 0, ts], lnst[:, 0, ts], 1.0 / C, None, ALU.mult))
                settle()
                nc.vector.tensor_tensor(Y[:, ts], T[:, ts], lnst[:, 0, ts].unsqueeze(2).to_broadcast([P, CHUNK, C]), ALU.subtract).then_inc(centered_ready, 1)
                norms[0] += 1
                dve.wait_ge(centered_ready, norms[0])
                step(nc.vector.tensor_tensor(Y2[:, ts, 0:C], Y[:, ts], Y[:, ts], ALU.mult))
                settle()
                step(nc.vector.tensor_reduce(lnst[:, 1, ts], Y2[:, ts, 0:C], AX.X, ALU.add))
                settle()
                nc.vector.tensor_scalar(lnst[:, 1, ts], lnst[:, 1, ts], 1.0 / C, EPS5, ALU.mult, ALU.add).then_inc(lnvar_ready, 1)

            outs = [0]

            def ln_out(c):
                ts = slice(4 * c, 4 * c + 4)
                outs[0] += 1
                dve.wait_ge(lninv_ready, outs[0])
                step(nc.vector.tensor_tensor(Y[:, ts], Y[:, ts], lnst[:, 2, ts].unsqueeze(2).to_broadcast([P, CHUNK, C]), ALU.mult))
                settle()
                step(nc.vector.tensor_copy(Y2[:, ts, 0:C].bitcast(F32R), Y[:, ts]))
                settle()
                nc.vector.tensor_tensor(Y2[:, ts, C:2 * C], Y[:, ts], Y2[:, ts, 0:C], ALU.subtract).then_inc(y2_ready, 1)

            def ln_evac(name, c):
                dve.wait_ge(misc_filled, FILL[name, c] + 1)
                nc.vector.tensor_copy(YTs[:, c * CW:(c + 1) * CW], PS[:, 7, :]).then_inc(misc_free, 1)

            for j in range(J):
                ln_stats(j)
                if j >= 1:
                    ln_out(j - 1)
                if j == 1:
                    ln_evac("yA", 0)
            ln_out(J - 1)

            def query_remainders(a, i):
                dve.wait_ge(misc_filled, FILL["q", a, i] + 1)
                dve.wait_ge(qh_copied, HPAIRS * a + i + 1)
                nc.vector.tensor_tensor(QL[:, a % 2, 2 * i:2 * i + 2, :].rearrange("p g n -> p (g n)"), PS[:, 7, :],
                                        QH[:, a % 2, 2 * i:2 * i + 2, :].rearrange("p g n -> p (g n)").bitcast(F32),
                                        ALU.subtract).then_inc(misc_free, 1)

            def normalise(a):
                dve.wait_ge(probs_ready, HEADS * (a + 1))
                step(nc.vector.reciprocal(rinv[:, a % 2], rsum[:, a % 2]))
                settle()
                dve.wait_ge(pv_done, HEADS * (a + 1))
                if a >= 2:
                    dve.wait_ge(fold_done, a - 1)
                for qt in range(PT):
                    ins = nc.vector.tensor_tensor(pr8[:, 2 * (a % 2) + qt, :].rearrange("p (h c) -> p h c", h=HEADS),
                                                  PS[:, 5 + qt, :].rearrange("p (h c) -> p h c", h=HEADS),
                                                  rinv[:, a % 2, qt, :].unsqueeze(2).to_broadcast([P, HEADS, C]), ALU.mult)
                    if qt == 0:
                        step(ins)
                ins.then_inc(heads_normed, 1)

            tops = [0]

            def take_logits(name, c, bias, E):
                n = CHUNK * E
                dve.wait_ge(misc_filled, FILL[name, c] + 1)
                nc.vector.tensor_tensor(tg[:, 0, 0:n].rearrange("p (t e) -> p t e", e=E), PS[:, 7, 0:n].rearrange("p (t e) -> p t e", e=E),
                                        bias.unsqueeze(1).to_broadcast([P, CHUNK, E]), ALU.add).then_inc(misc_free, 1)

            def top2(name, c, bias, E, logits_taken=False):
                n = CHUNK * E
                k = tops[0]
                tops[0] += 1
                lg, key, h1, l2 = (tg[:, r, 0:n].rearrange("p (t e) -> p t e", e=E) for r in range(4))
                df, m1, m2, mk, w1 = (tg[:, 4, 4 * r:4 * r + 4] for r in range(5))
                ex = tg[:, 5, 0:CHUNK]
                desc = c_("desc")[:, E3 - E:E3].unsqueeze(1).to_broadcast([P, CHUNK, E])

                def wide(v):
                    return v.unsqueeze(2).to_broadcast([P, CHUNK, E])

                if not logits_taken:
                    take_logits(name, c, bias, E)
                dve.wait_ge(misc_free, FILL[name, c] + 1)

                def first_max(src, m, hot):
                    step(nc.vector.tensor_reduce(m, src, AX.X, ALU.max))
                    settle()
                    step(nc.vector.tensor_tensor(key, src, wide(m), ALU.is_equal))
                    settle()
                    step(nc.vector.tensor_tensor(key, key, desc, ALU.mult))
                    settle()
                    step(nc.vector.tensor_reduce(mk, key, AX.X, ALU.max))
                    settle()
                    step(nc.vector.tensor_tensor(hot, key, wide(mk), ALU.is_equal))
                    settle()

                first_max(lg, m1, h1)
                step(nc.vector.scalar_tensor_tensor(l2, h1, NEG, lg, ALU.mult, ALU.add))
                settle()
                first_max(l2, m2, l2)
                nc.vector.tensor_tensor(df, m2, m1, ALU.subtract).then_inc(top_diff_ready, 1)
                dve.wait_ge(top_exp_ready, k + 1)
                step(nc.vector.tensor_scalar(w1, ex, 1.0, None, ALU.add))
                settle()
                step(nc.vector.reciprocal(w1, w1))
                settle()
                step(nc.vector.tensor_tensor(mk, ex, w1, ALU.mult))
                settle()
                step(nc.vector.tensor_tensor(h1, h1, wide(w1), ALU.mult))
                step(nc.vector.tensor_tensor(l2, l2, wide(mk), ALU.mult))
                settle()
                step(nc.vector.tensor_tensor(gate[:, 0 if E == E2 else 1, 4 * c:4 * c + 4, 0:E], h1, l2, ALU.add))
                settle()

            for i in range(HPAIRS):
                query_remainders(0, i)
            ln_evac("yA", 1)
            for s in range(STEPS):
                a, g = divmod(s, HEADS)
                dve.wait_ge(scores_ready, s + 1)
                if s >= 3:
                    dve.wait_ge(probs_ready, s - 2)
                nc.vector.tensor_tensor_reduce(MS[:, s % 3, 0:P], PS[:, s % 3, 0:P], c_("causal")[:, P:2 * P], -SCALE, 1e30,
                                               ALU.add, ALU.min, nmx[:, s % 3, 0:1])
                nc.vector.tensor_tensor_reduce(MS[:, s % 3, P:3 * P], PS[:, s % 3, P:3 * P], c_("causal"), -SCALE, 1e30,
                                               ALU.add, ALU.min, nmx[:, s % 3, 1:2]).then_inc(masked_ready, 1)
                if a + 1 < IMAGES and g < HPAIRS:
                    query_remainders(a + 1, g)
                if s in (6, 14):
                    ln_evac("yA", 2 + s // 8)
                if g == 1 and a >= 1:
                    normalise(a - 1)
                if g == 2 and a in (4, 6):
                    top2("gB", a // 2 - 2, rw[:, ROWS["bg2"]], E2, logits_taken=True)
                if g == 7 and a in (3, 5, 7):
                    take_logits("gB", a // 2 - 1, rw[:, ROWS["bg2"]], E2)
                if g == 7 and a in (2, 4, 6):
                    dve.wait_ge(fold_done, a)
                    ln_stats(a // 2 - 1)
                if g == 1 and a in (3, 5, 7):
                    ln_out(a // 2 - 1)
                if g == 6 and a in (3, 5, 7):
                    ln_evac("yB", a // 2 - 1)
            normalise(IMAGES - 1)
            top2("gB", 2, rw[:, ROWS["bg2"]], E2, logits_taken=True)
            dve.wait_ge(fold_done, IMAGES)
            ln_stats(3)
            ln_out(3)
            ln_evac("yB", 3)
            top2("gB", 3, rw[:, ROWS["bg2"]], E2)

            def combine(unit, c, gates):
                dve.wait_ge(fold_done, IMAGES + unit)
                for q in range(CHUNK):
                    nc.vector.tensor_tensor(pr8[:, q].rearrange("p (e c) -> p e c", c=C), PS[:, 3 + q].rearrange("p (e c) -> p e c", c=C),
                                            gates[:, q].unsqueeze(2).to_broadcast([P, E2, C]), ALU.mult).then_inc(acc_free, 1)

            def combine2(c):
                dve.wait_ge(out2_done, 2 * E2 * (c + 1))
                combine(c, c, gate[:, 0, 4 * c:4 * c + 4, 0:E2])

            def combine3(u):
                c, g = divmod(u, 2)
                dve.wait_ge(out3_done, E2 * (u + 1))
                combine(4 + u, c, gate[:, 1, 4 * c:4 * c + 4, g * E2:(g + 1) * E2])

            def window_bias(c):
                dve.wait_ge(misc_filled, FILL["pC", c] + 1)
                nc.vector.tensor_tensor(PJ[:], PS[:, 7, 0:CHUNK * A3].rearrange("p (t a) -> p t a", a=A3),
                                        rw[:, ROWS["bp"]].unsqueeze(1).to_broadcast([P, CHUNK, A3]), ALU.add).then_inc(misc_free, 1)

            def window_logits(c):
                dve.wait_ge(tanh_done, c + 1)
                step(nc.vector.tensor_tensor(PJ[:], PJ[:], rw[:, ROWS["wg"]].unsqueeze(1).to_broadcast([P, CHUNK, A3]), ALU.mult))
                settle()
                nc.vector.tensor_reduce(tg[:, 6, 0:CHUNK], PJ[:], AX.X, ALU.add, negate=True).then_inc(z_ready, 1)

            def window_gate(c):
                gg = tg[:, 6, 32:32 + CHUNK]
                dve.wait_ge(ez_ready, c + 1)
                step(nc.vector.tensor_scalar(gg, tg[:, 6, 16:16 + CHUNK], 1.0, None, ALU.add))
                settle()
                step(nc.vector.reciprocal(gg, gg))
                settle()
                step(nc.vector.tensor_copy(WX[:, :, C], gg))
                nc.vector.tensor_tensor(WX[:, :, 0:C], Y[:, 4 * c:4 * c + 4], gg.unsqueeze(2).to_broadcast([P, CHUNK, C]), ALU.mult).then_inc(wx_ready, 1)

            def window_add(c):
                bank = PS[:, 7, 0:CHUNK * (C + 1)].rearrange("p (t c) -> p t c", c=C + 1)
                rd = tg[:, 7, 0:CHUNK]
                wy = wy_t[:]
                dve.wait_ge(misc_filled, FILL["wC", c] + 1)
                step(nc.vector.reciprocal(rd, bank[:, :, C]))
                settle()
                nc.vector.tensor_tensor(wy, bank[:, :, 0:C], rd.unsqueeze(2).to_broadcast([P, CHUNK, C]), ALU.mult).then_inc(misc_free, 1)
                dve.wait_ge(misc_free, FILL["wC", c] + 1)
                tv = T[:, 4 * c:4 * c + 4, :].rearrange("p (h t) c -> p t h c", t=PT)
                step(nc.vector.tensor_tensor(tv, tv, wy.rearrange("p (t h) c -> p t h c", t=PT), ALU.add))

            combine2(0)
            for c in range(3):
                dve.wait_ge(fold_done, IMAGES + c + 1)
                ln_stats(c)
                ln_out(c)
                ln_evac("yC", c)
                window_bias(c)
                window_logits(c)
                window_gate(c)
                combine2(c + 1)
                if c < 2:
                    window_add(c)
                    ln_stats(c)
                    ln_out(c)
                    ln_evac("yD", c)
                    top2("gD", c, rw[:, ROWS["bg3"]], E3)

            def output(c):
                dve.wait_ge(misc_filled, FILL["oT", c] + 1)
                nc.vector.tensor_copy(X[:, c, :], PS[:, 7, 0:2 * P]).then_inc(misc_free, 1)

            for n in range(4 * E3):
                dve.wait_ge(silu_done, n + 1)
                dve.wait_ge(hid3_ready, 2 * n + 2)
                if n >= 3:
                    dve.wait_ge(out3_done, n - 2)
                nc.vector.tensor_tensor(hid[:, n % 3], sil[:, n % 2], PS[:, (2 * n + 1) % 3, :], ALU.mult).then_inc(prod3_done, 1)
                if n == 1:
                    window_add(2)
                if n == 3:
                    ln_stats(2)
                if n == 4:
                    ln_out(2)
                if n == 5:
                    dve.wait_ge(fold_done, IMAGES + 4)
                    ln_stats(3)
                if n == 6:
                    ln_evac("yD", 2)
                if n == 7:
                    ln_out(3)
                    top2("gD", 2, rw[:, ROWS["bg3"]], E3)
                if n % E2 == 1 and n > E2:
                    combine3(n // E2 - 1)
                if n == 9:
                    ln_evac("yC", 3)
                if n == 10:
                    window_bias(3)
                if n == 12:
                    window_logits(3)
                if n == 13:
                    window_gate(3)
                if n == 14:
                    window_add(3)
                if n == 15:
                    ln_stats(3)
                if n == 17:
                    ln_out(3)
                if n == 19:
                    ln_evac("yD", 3)
                if n == 20:
                    top2("gD", 3, rw[:, ROWS["bg3"]], E3)
                if n in (28, 44, 60):
                    output(n // 16 - 1)
            combine3(7)
            output(3)

        @block.tensor
        def _(pe):
            mm = nc.tensor.matmul

            pe.wait_ge(const_loaded, 16)
            pe.wait_ge(moments_ready, 1)
            mm(PS[:, 7, 0:2 * J], c_("pair_mean"), mv[:, 0].rearrange("p j m -> p (j m)"), start=True, stop=True).then_inc(group_moments_ready, 1)
            pe.wait_ge(off_block_loaded, 32)
            for ip in range(NP):
                j, pt = divmod(ip, PT)
                pe.wait_ge(g_ready, j + 1)
                pe.wait_ge(g_shifted_ready, 2 * j + 2)
                for k in range(TAPS):
                    ky, kx = divmod(k, 3)
                    ins = mm(PS[:, 0, ip * 2 * NOFF:(ip + 1) * 2 * NOFF], G[:, kx, j, 8 * pt + ky:8 * pt + ky + 8, :],
                             w_off[:, k, :], start=(k == 0), stop=(k == TAPS - 1))
            ins.then_inc(offsets_ready, 1)
            pe.wait_ge(dl_ready, 1)
            pe.wait_ge(gl_ready, J)
            for ip in range(NP):
                j, pt = divmod(ip, PT)
                if 2 * ip + 1 >= 3:
                    pe.wait_ge(u_copied, 2 * ip + 1 - 2)
                for h in range(2):
                    n = 2 * ip + h
                    hs = slice(h * C, (h + 1) * C)
                    px = slice(pt * P, (pt + 1) * P)
                    for r, (gg, ww) in enumerate(((GH, DH), (GH, DL), (GL, DH))):
                        for a in range(2):
                            ins = mm(PS[:, 1 + 2 * (n % 3) + a, 0:288], gg[hs, j, px], ww[hs, a * 288:(a + 1) * 288],
                                     start=(r == 0), stop=(r == 2))
                ins.then_inc(u_ready, 1)

            def dT(ip):
                pe.wait_ge(d_copied, ip + 1)
                if ip >= 2:
                    pe.wait_ge(x1_tile_ready, ip - 1)
                nc.tensor.transpose(PS[:, 7 * (ip % 2), 0:P], D[:, ip % 2, :], ident).then_inc(dT_ready, 1)

            pe.wait_ge(u_copied, NT)
            for n in range(NT + 1):
                for g in range(NG):
                    if n < NT:
                        m = n * NG + g
                        if g == 0:
                            pe.wait_ge(prod_ready, n + 1)
                        if m >= 4:
                            pe.wait_ge(st_copied, m - 3)
                        for a in range(STG[g]):
                            k, qt = divmod(4 * g + a, 2)
                            ins = nc.tensor.transpose(PS[:, 1 + m % 4, a * P:(a + 1) * P], prods[n % 2][:, k, qt * P:(qt + 1) * P], ident)
                        ins.then_inc(st_ready, 1)
                    if n >= 1:
                        v = n - 1
                        ip, h = divmod(v, 2)
                        b = h * J + ip // 2
                        pe.wait_ge(st_copied, v * NG + g + 1)
                        if h == 0 and ip >= 2 and g == 0:
                            pe.wait_ge(d_copied, ip - 1)
                        for a in range(STG[g]):
                            k, qt = divmod(4 * g + a, 2)
                            ins = mm(PS[:, 5 + ip % 2, h * C:(h + 1) * C], ST[v % 2][:, 4 * g + a, :],
                                     U[:, 2 * (2 * (ip // 2) + qt) + h, k * C:(k + 1) * C],
                                     start=(g + a == 0), stop=(4 * g + a == 2 * TAPS - 1))
                        if g == NG - 1:
                            ins.then_inc(d_ready, 1)
                if n >= 4 and n % 2 == 0 and n // 2 - 2 < NP:
                    dT(n // 2 - 2)
            for ip in range(NP - 1, NP):
                dT(ip)

            pe.wait_ge(x1_tile_ready, NP)
            pe.wait_ge(moments_ready, 2)
            mm(PS[:, 7, 0:2 * J], c_("pair_mean"), mv[:, 1].rearrange("p j m -> p (j m)"), start=True, stop=True).then_inc(group_moments_ready, 1)
            pe.wait_ge(sq_ready, 1)
            mm(PS[:, 3, 0:J], c_("half_mean"), small[:, 20:20 + J], start=True, stop=True).then_inc(q_ready, 1)
            pe.wait_ge(conv_block_loaded, 32)

            def conv(r):
                pe.wait_ge(g_ready, J + 2 * r + 2)
                for k in range(TAPS):
                    ky, kx = divmod(k, 3)
                    ins = mm(PS[:, 1 + r, :], w_conv[:, k, :], G2[:, 2 * r:2 * r + 2, ky:ky + HH, kx:kx + WW],
                             start=(k == 0), stop=(k == TAPS - 1))
                ins.then_inc(conv_ready, 1)

            conv(0)
            pe.wait_ge(pb_ready, 2)
            mm(PS[0:B, 3, 0:NPHI], PB[:], weff[:], start=True, stop=True).then_inc(coef_ready, 1)
            conv(1)
            pe.wait_ge(wat_loaded, 16)
            for g in range(HEADS):
                odd, hp = divmod(g, HPAIRS)
                hs = slice(odd * C, (odd + 1) * C)
                mm(PS[:, 4 + odd, hp * P:(hp + 1) * P], wa[hs, WAT["q"]][:, hp * P:(hp + 1) * P],
                   wa[hs, WAT["k"]][:, hp * C:(hp + 1) * C].unsqueeze(1).to_broadcast([C, 2, C]), start=True, stop=True)
            for g in range(HEADS):
                odd, hp = divmod(g, HPAIRS)
                hs = slice(odd * C, (odd + 1) * C)
                ins = mm(PS[:, 6 + odd, hp * C:(hp + 1) * C], wa[hs, WAT["v"]][:, hp * P:(hp + 1) * P],
                         wa[hs, WAT["p"]][:, hp * C:(hp + 1) * C], start=True, stop=True)
            ins.then_inc(av_ready, 1)
            pe.wait_ge(v3_ready, 1)
            mm(PS[:, 3, 0:3 * J], cst[0:B, CONST["sel_half"]], V3[0:B].rearrange("p a b -> p (a b)"), start=True, stop=True).then_inc(cb_ready, 1)

            fills = [0]

            def take(*name):
                assert FILLS[fills[0]] == name, (FILLS[fills[0]], name)
                if fills[0]:
                    pe.wait_ge(misc_free, fills[0])
                else:
                    pe.wait_ge(avh_ready, 4)
                fills[0] += 1

            for j in range(J):
                pe.wait_ge(x2_ready, j + 1)
                take("xT", j)
                for pt in range(PT):
                    ins = nc.tensor.transpose(PS[:, 7, pt * P:(pt + 1) * P], X1[:, j, pt * P:(pt + 1) * P], ident)
                ins.then_inc(misc_filled, 1)

            yts = [0]

            def transpose_y(name, c):
                yts[0] += 1
                pe.wait_ge(y2_ready, yts[0])
                take(name, c)
                for q in range(CHUNK):
                    ins = nc.tensor.transpose(PS[:, 7, q * P:(q + 1) * P], Y2[:, 4 * c + q, :], ident)
                ins.then_inc(misc_filled, 1)

            def project(a, i):
                if i < HPAIRS:
                    take("q", a, i)
                    for g in (2 * i, 2 * i + 1):
                        for r, w in enumerate((AVH, AVL)):
                            ins = mm(PS[:, 7, (g % 2) * S:(g % 2 + 1) * S], w[:, g * P:(g + 1) * P], YTs[:, a * S:(a + 1) * S],
                                     start=(r == 0), stop=(r == 1))
                else:
                    t = i - HPAIRS
                    take("v", a, t)
                    for r, w in enumerate((AVH, AVL)):
                        ins = mm(PS[:, 7, :], YTs[:, (2 * a + t) * P:(2 * a + t + 1) * P], w[:, 2 * 512:3 * 512], start=(r == 0), stop=(r == 1))
                ins.then_inc(misc_filled, 1)

            def small_projection(name, c, weight, width):
                take(name, c)
                for q in range(CHUNK):
                    t = 4 * c + q
                    for r, w in enumerate((swh, swl)):
                        ins = mm(PS[:, 7, q * width:(q + 1) * width], YTs[:, t * P:(t + 1) * P], w[:, SW[weight]], start=(r == 0), stop=(r == 1))
                ins.then_inc(misc_filled, 1)

            def window(c):
                pe.wait_ge(wx_ready, c + 1)
                take("wC", c)
                n = 2 * (C + 1)
                wxv = WX[:].rearrange("p (h t) c -> p t h c", t=PT)
                mm(PS[:, 7, 0:n], c_("band"), wxv[:, 0], start=True, stop=True)
                mm(PS[:, 7, n:2 * n], c_("band"), wxv[:, 1], start=True, stop=False)
                mm(PS[:, 7, n:2 * n], c_("band_prev"), wxv[:, 0], start=False, stop=True).then_inc(misc_filled, 1)

            def result(c):
                pe.wait_ge(fold_done, IMAGES + 4 + 2 * (c + 1))
                take("oT", c)
                for h in range(2):
                    t = 4 * c + 2 * h
                    ins = nc.tensor.transpose(PS[:, 7, h * P:(h + 1) * P], T[:, t:t + 2, :].rearrange("p t c -> p (t c)"), ident)
                ins.then_inc(misc_filled, 1)

            pe.wait_ge(avl_ready, 1)
            transpose_y("yA", 0)
            pe.wait_ge(misc_free, FILL["yA", 0] + 1)
            for i in range(6):
                project(0, i)
            transpose_y("yA", 1)
            for s in range(STEPS + 2):
                if s < STEPS:
                    a, g = divmod(s, HEADS)
                    if g == 0:
                        pe.wait_ge(misc_free, FILL["v", a, 1] + 1)
                    if s >= 3:
                        pe.wait_ge(masked_ready, s - 2)
                    for qt in range(PT):
                        cols = slice(0, P) if qt == 0 else slice(P, 3 * P)
                        for r, w in enumerate((QH, QL)):
                            ins = mm(PS[:, s % 3, cols], w[:, a % 2, g, qt * P:(qt + 1) * P], YTs[:, a * S:a * S + (qt + 1) * P],
                                     start=(r == 0), stop=(r == 1))
                    ins.then_inc(scores_ready, 1)
                if 1 <= s <= STEPS:
                    v = s - 1
                    pe.wait_ge(probs_ready, v + 1)
                    if v >= 2:
                        pe.wait_ge(pT_copied, v - 1)
                    for k in range(3):
                        ins = nc.tensor.transpose(PS[:, 3 + v % 2, k * P:(k + 1) * P], PR[:, v % 3, k * P:(k + 1) * P], ident)
                    ins.then_inc(pT_ready, 1)
                if s >= 2:
                    v = s - 2
                    a, g = divmod(v, HEADS)
                    if g == 0 and a >= 1:
                        pe.wait_ge(heads_normed, a)
                    pe.wait_ge(pT_copied, v + 1)
                    vh = slice(g * C, (g + 1) * C)
                    mm(PS[:, 5, vh], PTs[:, v % 3, 0:P], VV[:, a % 2, 0, vh], start=True, stop=True)
                    mm(PS[:, 6, vh], PTs[:, v % 3, P:2 * P], VV[:, a % 2, 0, vh], start=True, stop=False)
                    mm(PS[:, 6, vh], PTs[:, v % 3, 2 * P:3 * P], VV[:, a % 2, 1, vh], start=False, stop=True).then_inc(pv_done, 1)
                if s < STEPS:
                    for what in attention_fills(s):
                        if what[0] in ("q", "v"):
                            project(what[1], what[2] + (HPAIRS if what[0] == "v" else 0))
                        elif what[0] in ("yA", "yB"):
                            transpose_y(*what)
                        else:
                            pe.wait_ge(swl_ready, 1)
                            small_projection(*what, "wg2", E2)

            def more(what):
                kind, c = what
                if kind in ("yB", "yC", "yD"):
                    transpose_y(kind, c)
                elif kind == "gB":
                    small_projection(kind, c, "wg2", E2)
                elif kind == "pC":
                    small_projection(kind, c, "wp", A3)
                elif kind == "gD":
                    small_projection(kind, c, "wg3", E3)
                elif kind == "wC":
                    window(c)
                else:
                    result(c)

            pe.wait_ge(masked_ready, STEPS)
            pe.wait_ge(stage_split, 3)
            pe.wait_ge(b2s_ready, 1)
            pe.wait_ge(w128_loaded, 16)
            N2 = 4 * E2 * 2
            for n in range(N2 + 1):
                if n < N2:
                    c, r = divmod(n, 2 * E2)
                    if n == 48:
                        pe.wait_ge(misc_free, FILL["yB", 3] + 1)
                    if n >= 3:
                        pe.wait_ge(gelu_done, n - 2)
                    for k, w in enumerate((WH, WL)):
                        ins = mm(PS[:, n % 3, :], w[:, 0, r * P:(r + 1) * P], YTs[:, c * CW:(c + 1) * CW], start=(k == 0), stop=(k == 1))
                    ins.then_inc(hid2_ready, 1)
                if n >= 1:
                    v = n - 1
                    c, r = divmod(v, 2 * E2)
                    e, ht = divmod(r, 2)
                    if v == 0:
                        pe.wait_ge(heads_normed, IMAGES)
                    for q in range(CHUNK):
                        if r == 0:
                            if c:
                                pe.wait_ge(acc_free, 4 * (c - 1) + q + 1)
                            mm(PS[:, 3 + q, :], ones[:], b2s[:], start=True, stop=False, skip_group_check=True)
                    pe.wait_ge(gelu_done, v + 1)
                    for q in range(CHUNK):
                        ins = mm(PS[:, 3 + q, e * C:(e + 1) * C], hid[:, v % 3, q * P:(q + 1) * P],
                                 wk[:, W128["w2_2"]][:, r * C:(r + 1) * C], start=False, stop=(r == 2 * E2 - 1), skip_group_check=True)
                    ins.then_inc(out2_done, 1)
                if n in FIRST_FILLS:
                    more(FIRST_FILLS[n])

            N3 = 4 * E3
            for n in range(N3 + 1):
                if n < N3:
                    c, e = divmod(n, E3)
                    if e == 0:
                        pe.wait_ge(misc_free, FILL["yD", c] + 1)
                    for a in range(2):
                        if a == 0 and n >= 2:
                            pe.wait_ge(prod3_done, n - 1)
                        if a == 1 and n >= 1:
                            pe.wait_ge(silu_done, n)
                        for k, w in enumerate((WH, WL)):
                            ins = mm(PS[:, (2 * n + a) % 3, :], w[:, 1 + a, e * P:(e + 1) * P], YTs[:, c * CW:(c + 1) * CW],
                                     start=(k == 0), stop=(k == 1))
                        ins.then_inc(hid3_ready, 1)
                if n >= 1:
                    v = n - 1
                    c, e = divmod(v, E3)
                    u = v // E2
                    pe.wait_ge(prod3_done, v + 1)
                    for q in range(CHUNK):
                        if v % E2 == 0:
                            pe.wait_ge(acc_free, 16 + 4 * (u - 1) + q + 1)
                        ins = mm(PS[:, 3 + q, (e % E2) * C:(e % E2 + 1) * C], hid[:, v % 3, q * P:(q + 1) * P],
                                 wk[:, W128["w3"]][:, e * C:(e + 1) * C], start=True, stop=True)
                    ins.then_inc(out3_done, 1)
                if n in SECOND_FILLS:
                    more(SECOND_FILLS[n])
            result(3)


def pack(widths, total, parts, height):
    a = np.zeros((height, total), np.float32)
    for name, v in parts.items():
        a[:, widths[name]] = np.asarray(v).reshape(height, -1)
    return a


def kernel(**inputs):
    import concourse.bacc as bacc
    from concourse.bass_utils import run_bass_kernel_spmd

    i = {k: np.asarray(v) for k, v in inputs.items()}

    def taps(w):
        return w.transpose(1, 2, 3, 0).reshape(C, -1)

    def heads(w, times):
        w = w.reshape(C, HPAIRS, P).transpose(2, 1, 0)
        return np.stack([w] * times, 2)

    qkv = i["L2_attn_w_qkv"].reshape(C, 3, HEADS * C)
    arrays = {
        "x": i["x"].reshape(B, C, S),
        "w64": pack(W64, NW64, {
            "w_dcn": taps(i["L0_conv_w_dcn"]), "conv_b": i["L1_conv_conv_b"], "b_dcn": i["L0_conv_b_dcn"],
            "phi": i["L1_conv_phi_w"].reshape(NPHI, STREAMS, C).transpose(2, 1, 0),
            "rms": i["L1_conv_rms_w"].reshape(STREAMS, C).T,
            "wg2": i["L2_ffn_Wg"], "wp": i["L3_attn_Wp"].T, "wg3": i["L3_ffn_gate_w"]}, C),
        "wcv": pack(WCV, NWCV, {"w_off": taps(i["L0_conv_w_off"]), "w_conv": taps(i["L1_conv_conv_w"])}, C),
        "wat": pack(WAT, NWAT, {"q": heads(qkv[:, 0], 2), "k": heads(qkv[:, 1], 1), "v": heads(qkv[:, 2], 2),
                                "p": i["L2_attn_w_proj"].reshape(HPAIRS, P, C).transpose(1, 0, 2)}, P),
        "w128": pack(W128, NW128, {
            "b1": i["L2_ffn_b1"].reshape(E2 * 2, P).T,
            "w2_2": i["L2_ffn_W2"].reshape(E2 * 2, P, C).transpose(1, 0, 2),
            "w3": i["L3_ffn_w3"].transpose(1, 0, 2)}, P),
        "wexp": np.stack([i[k].transpose(1, 0, 2).reshape(C, -1) for k in ("L2_ffn_W1", "L3_ffn_w1", "L3_ffn_w2")]),
        "rows": pack(ROWS, NROWS, {
            "b_off": i["L0_conv_b_off"], "b_proj": i["L2_attn_b_proj"], "bg2": i["L2_ffn_bg"], "bp": i["L3_attn_bp"],
            "wg": i["L3_attn_Wg"], "bg3": i["L3_ffn_gate_b"], "phi_b": i["L1_conv_phi_b"],
            "alpha": np.concatenate([i["L1_conv_alpha_pre"], i["L1_conv_alpha_post"], i["L1_conv_alpha_res"]])}, 1),
        "b2": i["L2_ffn_b2"].reshape(1, -1),
        "consts": shape_constants(),
    }
    nc = bacc.Bacc("TRN2", target_bir_lowering=False, num_devices=1)
    feeds, args = {}, []
    for name, a in arrays.items():
        feeds[f"in_{name}"] = np.ascontiguousarray(a)
        args.append(nc.dram_tensor(f"in_{name}", list(a.shape), F32, kind="ExternalInput").ap())
    result = nc.dram_tensor("out_0", [B, C, S], F32, kind="ExternalOutput").ap()
    hybrid_kernel(nc, *args, result)
    r = run_bass_kernel_spmd(nc, [feeds], core_ids=[0])
    return r.results[0]["out_0"].reshape(B, C, HH, WW)
```

```python
from contextlib import ExitStack

import numpy as np

import concourse.bass as bass
from concourse import mybir

ALU = mybir.AluOpType
ACT = mybir.ActivationFunctionType
AX = mybir.AxisListType
F32 = mybir.dt.float32
F32R = mybir.dt.float32r

B, C, HH, WW = 8, 64, 16, 16
S = HH * WW
P = 128
J = B // 2
PT = S // P
NP = J * PT
NT = 2 * NP
TAPS = 9
NOFF = 3 * TAPS
PADW = WW + 2
STREAMS = 4
NPHI = 2 * STREAMS + STREAMS * STREAMS
SINKHORN = 20
HEADS = 8
HPAIRS = HEADS // 2
SCALE = float(C) ** -0.5
E2, HID2 = 8, 256
E3, HID3 = 16, 128
A3 = 32
WINDOW = 16
NEG = -1e30
EPS5 = 1e-5


def layout(*fields):
    at, where = 0, {}
    for name, width in fields:
        where[name] = slice(at, at + width)
        at += width
    return where, at


CONST, NCONST = layout(("ident", P), ("pair_mean", P), ("half_mean", P), ("base", PT * 2 * TAPS), ("grid", WW),
                       ("causal", 2 * P), ("band", P), ("band_prev", P), ("sel_half", P), ("sel_image", J),
                       ("desc", E3), ("neg_half", 4), ("euler", 4), ("row0", 1), ("row1", 1), ("part_sum", 2 * NOFF))
W64, NW64 = layout(("w_dcn", TAPS * C), ("conv_b", 1), ("b_dcn", 1), ("phi", STREAMS * NPHI), ("rms", STREAMS),
                   ("wg2", E2), ("wp", A3), ("wg3", E3))
WCV, NWCV = layout(("w_off", TAPS * NOFF), ("w_conv", TAPS * C))
WAT, NWAT = layout(("q", HPAIRS * 2 * C), ("k", HPAIRS * C), ("v", HPAIRS * 2 * C), ("p", HPAIRS * C))
W128, NW128 = layout(("b1", 2 * E2), ("w2_2", 2 * E2 * C), ("w3", E3 * C))
ROWS, NROWS = layout(("b_off", NOFF), ("b_proj", C), ("bg2", E2), ("bp", A3), ("wg", A3), ("bg3", E3),
                     ("phi_b", NPHI), ("alpha", 3))
UNIT = 4
CHUNK = 4
CW = CHUNK * P
NEXP = E2 * HID2


def shape_constants():
    c = np.zeros((P, NCONST), np.float32)
    p = np.arange(P)
    c[:, CONST["ident"]] = np.eye(P)
    c[:, CONST["pair_mean"]] = (p[:, None] // 2 == p[None] // 2) * 0.5
    c[:, CONST["half_mean"]] = (p[:, None] // C == p[None] // C) / C
    base = np.zeros((P, PT, TAPS, 2), np.float32)
    for pt in range(PT):
        s = pt * P + p
        for k in range(TAPS):
            base[:, pt, k, 0] = s // WW - 1 + k // 3
            base[:, pt, k, 1] = s % WW - 1 + k % 3
    c[:, CONST["base"]] = base.reshape(P, -1)
    c[:, CONST["grid"]] = np.arange(WW)
    c[:, CONST["causal"]] = np.concatenate([np.zeros((P, P)), np.where(p[None] <= p[:, None], 0.0, NEG)], 1)
    c[:, CONST["band"]] = (p[:, None] <= p[None]) & (p[:, None] > p[None] - WINDOW)
    c[:, CONST["band_prev"]] = p[:, None] - P > p[None] - WINDOW
    c[:B, CONST["sel_half"]] = np.arange(B)[:, None] // J == p[None] // C
    c[:B, CONST["sel_image"]] = np.arange(B)[:, None] % J == np.arange(J)[None]
    c[:, CONST["desc"]] = E3 - np.arange(E3)
    c[:, CONST["neg_half"]] = -0.5
    c[:, CONST["euler"]] = np.e
    c[:, CONST["part_sum"]] = (p[:, None] % (2 * NOFF) == np.arange(2 * NOFF)) & (p[:, None] < 4 * NOFF)
    c[:, CONST["row0"]] = p[:, None] == 0
    c[:, CONST["row1"]] = p[:, None] == 1
    return c


IMAGES, STEPS = B, B * HEADS


def projections(a):
    return [("q", a, i) for i in range(HPAIRS)] + [("v", a, i) for i in range(PT)]


def on_side(name):
    return name[2] % 2 == 1


def attention_fills(s):
    a, i = divmod(s, HEADS)
    out = []
    if s < 2:
        out.append(("q", 0, 2 + s))
    i -= 2 * (a == 0)
    if a + 1 < IMAGES and 0 <= i < 6:
        out.append(projections(a + 1)[i])
    if s in (7, 22, 38):
        out.append(("yA", 1 + s // 16))
    if s in (14, 23):
        out.append(("xT", 2 + s // 16))
    if i == 6 and a >= 3 and a % 2 == 1:
        out.append(("yB", (a - 3) // 2))
    if i == 7 and a >= 3 and a % 2 == 1:
        out.append(("gB", (a - 3) // 2))
    return out


FIRST_FILLS = {12: ("yB", 3), 14: ("gB", 3), 27: ("yC", 0), 29: ("pC", 0), 34: ("wC", 0), 40: ("yD", 0), 42: ("gD", 0),
               51: ("yC", 1), 53: ("pC", 1), 58: ("wC", 1)}
SECOND_FILLS = {1: ("yC", 2), 4: ("pC", 2), 8: ("yD", 1), 11: ("gD", 1), 13: ("wC", 2), 20: ("yC", 3), 22: ("pC", 3),
                25: ("yD", 2), 28: ("wC", 3), 30: ("gD", 2), 36: ("oT", 0), 39: ("oT", 1), 42: ("yD", 3), 45: ("gD", 3),
                55: ("oT", 2)}
FIRST_PROJECTIONS = [("q", 0, 0), ("q", 0, 1), ("v", 0, 0), ("v", 0, 1)]
FILLS = [("xT", 0), ("yA", 0)] + FIRST_PROJECTIONS + [("xT", 1)]
for _s in range(STEPS):
    FILLS += attention_fills(_s)
FILLS += [FIRST_FILLS[n] for n in sorted(FIRST_FILLS)] + [SECOND_FILLS[n] for n in sorted(SECOND_FILLS)] + [("oT", 3)]
SIDE = {name: n for n, name in enumerate(f for f in FILLS if f[0] in ("q", "v") and on_side(f))}
FILL = {name: n for n, name in enumerate(f for f in FILLS if f not in SIDE)}
FILLS = list(FILL)


def hybrid_kernel(nc, x, w64, wcv, wat, w128, wexp, rows, b2, consts, out):
    with ExitStack() as ctx:
        def sem(name):
            return ctx.enter_context(nc.semaphore(name))

        def tensor(stack, name, *shape, dtype=F32):
            return stack.enter_context(nc.sbuf_tensor(name, [P, *shape], dtype))

        PS = ctx.enter_context(nc.psum_tensor("PS", [P, 8, 512], F32))

        def sb(name, *shape, dtype=F32):
            return tensor(ctx, name, *shape, dtype=dtype)

        cst = sb("cst", NCONST)
        wc = sb("wc", NW64)
        wk = sb("wk", NW128)
        rw = sb("rw", NROWS)
        b2row = sb("b2row", E2 * C)
        b2hi = sb("b2hi", E2 * C)
        b2s = sb("b2s", E2 * C, dtype=F32R)
        ones = sb("ones", P, dtype=F32R)
        score_arena = sb("score_arena", 9 * 384 + 774)
        w_off = score_arena[:, 2592:3078].rearrange("p (k n) -> p k n", k=TAPS)
        w_conv = score_arena[:, 3078:4230].rearrange("p (k n) -> p k n", k=TAPS)
        G2 = score_arena[:, 1296:2592].rearrange("p (j y x) -> p j y x", j=J, y=PADW)
        X = sb("X", J, S)
        X1 = sb("X1", J, S)
        stat = sb("stat", J, 6)
        mv = sb("mv", 2, J, 2)
        gmv = sb("gmv", J, 2)
        small = sb("small", 64)
        T = sb("T", NT, C)
        Y = sb("Y", NT, C)
        Y2 = sb("Y2", NT, 2 * C)
        YTs = sb("YTs", NT * P, dtype=F32R)
        lnst = sb("lnst", 3, NT)
        AVH = sb("AVH", 3 * 512, dtype=F32R)
        AVL = sb("AVL", 3 * 512, dtype=F32R)
        sw = sb("sw", 2 * (E2 + A3 + E3), dtype=F32R)
        coord = sb("coord", NT, 2 * TAPS)
        mask = sb("mask", NT, TAPS)
        D = sb("D", 2, P)
        weff = sb("weff", NPHI)
        phr = sb("phr", STREAMS, NPHI)
        PB = sb("PB", B)
        cf = sb("cf", NPHI)
        M = sb("M", STREAMS, STREAMS)
        mn = sb("mn", STREAMS)
        V = sb("V", 3)
        V3 = sb("V3", J, 3)
        gs = sb("gs", 2, 3)
        CB = sb("CB", J, 3)
        bb = sb("bb", J)
        MS, PR, PTs = (score_arena[:, o * 1152:(o + 1) * 1152].rearrange("p (u n) -> p u n", u=3) for o in range(3))
        nmx = sb("nmx", 3, 2)
        rsum = sb("rsum", 2, PT, HEADS)
        rinv = sb("rinv", 2, PT, HEADS)
        tg = sb("tg", 8, CHUNK * E3)
        gate = sb("gate", 2, NT, E3)
        PJ = sb("PJ", CHUNK, A3)
        WX = sb("WX", CHUNK, C + 1)
        wy = sb("wy", CHUNK, C)

        with ExitStack() as early:
            hats_t = tensor(early, "hats", NT, 2 * TAPS, WW)
            U = tensor(early, "U", NT, TAPS * C)
            GH = tensor(early, "GH", J, S, dtype=F32R)
            GL = tensor(early, "GL", J, S, dtype=F32R)
            DH = tensor(early, "DH", TAPS * C, dtype=F32R)
            DL = tensor(early, "DL", TAPS * C, dtype=F32R)
            wa = tensor(early, "wa", NWAT)
            with ExitStack() as first:
                G = tensor(first, "G", J, S)
                GHP = tensor(first, "GHP", J, PADW, PADW, dtype=F32R)
                GLP = tensor(first, "GLP", J, PADW, PADW, dtype=F32R)
                WO = tensor(first, "WO", TAPS, 4 * NOFF, dtype=F32R)
                OT = tensor(first, "OT", J, S)
            prods = [tensor(early, f"prod{n}", TAPS, S) for n in range(2)]
            st_mem = tensor(early, "st_mem", 4608)
            ST = [st_mem[:, o:o + 2304].rearrange("p (k q) -> p k q", q=P) for o in (0, 2304)]
        hats = hats_t[:]
        HC = U[:, 0:2].rearrange("p a b -> p (a b)")[:, 0:J * S].rearrange("p (j s) -> p j s", j=J)
        av = prods[0][:].rearrange("p k q -> p (k q)")[:, 0:3 * 512]
        QH = sb("QH", 2, HEADS, S, dtype=F32R)
        QL = sb("QL", 2, HEADS, S, dtype=F32R)
        VV = sb("VV", 2, PT, HEADS * C)
        pr8 = sb("pr8", CHUNK, E2 * C)
        stage = sb("stage", NEXP)
        WH = sb("WH", 3, NEXP, dtype=F32R)
        WL = sb("WL", 3, NEXP, dtype=F32R)
        hid = sb("hid", 3, CW)
        sil = VV[:, 0]

        def c_(name):
            return cst[:, CONST[name]]

        SW = {"wg2": (0, E2), "wp": (E2, A3), "wg3": (E2 + A3, E3)}
        SMALL64 = slice(W64["wg2"].start, W64["wg3"].stop)

        def w_(name, h=None):
            return wc[:, W64[name]] if h is None else wc[h * C:(h + 1) * C, W64[name]]

        ident = c_("ident")

        def img(t):
            return t[:].rearrange("p j (y x) -> p j y x", y=HH)

        x_loaded = sem("x_loaded")
        const_loaded = sem("const_loaded")
        rows_loaded = sem("rows_loaded")
        w64_loaded = sem("w64_loaded")
        wat_loaded = sem("wat_loaded")
        w128_loaded = sem("w128_loaded")
        b2_loaded = sem("b2_loaded")
        block_zeroed = sem("block_zeroed")
        off_block_loaded = sem("off_block_loaded")
        conv_block_loaded = sem("conv_block_loaded")
        pads_zeroed = sem("pads_zeroed")
        b2s_zeroed = sem("b2s_zeroed")
        b2s_ready = sem("b2s_ready")
        dve_step = sem("dve_step")
        act_step = sem("act_step")
        pool_step = sem("pool_step")
        moments_ready = sem("moments_ready")
        group_moments_ready = sem("group_moments_ready")
        var_ready = sem("var_ready")
        sd_ready = sem("sd_ready")
        norm_ready = sem("norm_ready")
        g_ready = sem("g_ready")
        ghp_ready = sem("ghp_ready")
        glp_ready = sem("glp_ready")
        wo_ready = sem("wo_ready")
        offset_conv_ready = sem("offset_conv_ready")
        ot_ready = sem("ot_ready")
        gh_ready = sem("gh_ready")
        gs_zeroed = sem("gs_zeroed")
        table_loaded = sem("table_loaded")
        gl_ready = sem("gl_ready")
        dh_ready = sem("dh_ready")
        dl_ready = sem("dl_ready")
        swh_ready = sem("swh_ready")
        swl_ready = sem("swl_ready")
        offsets_ready = sem("offsets_ready")
        mask_logits_ready = sem("mask_logits_ready")
        mask_ready = sem("mask_ready")
        hat_diff_ready = sem("hat_diff_ready")
        hat_ready = sem("hat_ready")
        u_ready = sem("u_ready")
        u_copied = sem("u_copied")
        u_copied_dve = sem("u_copied_dve")
        prod_ready = sem("prod_ready")
        st_ready = sem("st_ready")
        st_copied = sem("st_copied")
        d_ready = sem("d_ready")
        d_copied = sem("d_copied")
        dT_ready = sem("dT_ready")
        x1_tile_ready = sem("x1_tile_ready")
        sq_ready = sem("sq_ready")
        q_ready = sem("q_ready")
        qe_ready = sem("qe_ready")
        qs_ready = sem("qs_ready")
        pb_ready = sem("pb_ready")
        coef_ready = sem("coef_ready")
        logits_ready = sem("logits_ready")
        gates_ready = sem("gates_ready")
        v3_ready = sem("v3_ready")
        v3_diag_ready = sem("v3_diag_ready")
        cb_ready = sem("cb_ready")
        cb_copied = sem("cb_copied")
        scaled_conv_ready = sem("scaled_conv_ready")
        conv_added = sem("conv_added")
        conv_ready = sem("conv_ready")
        x2_ready = sem("x2_ready")
        av_ready = sem("av_ready")
        avh_ready = sem("avh_ready")
        avl_ready = sem("avl_ready")
        stage_loaded = sem("stage_loaded")
        stage_split = sem("stage_split")
        misc_filled = sem("misc_filled")
        misc_free = sem("misc_free")
        side_filled = sem("side_filled")
        side_free = sem("side_free")
        lnvar_ready = sem("lnvar_ready")
        lninv_ready = sem("lninv_ready")
        y2_ready = sem("y2_ready")
        centered_ready = sem("centered_ready")
        qh_copied = sem("qh_copied")
        scores_ready = sem("scores_ready")
        masked_ready = sem("masked_ready")
        probs_ready = sem("probs_ready")
        pT_ready = sem("pT_ready")
        pT_copied = sem("pT_copied")
        pv_done = sem("pv_done")
        heads_normed = sem("heads_normed")
        fold_done = sem("fold_done")
        top_diff_ready = sem("top_diff_ready")
        top_exp_ready = sem("top_exp_ready")
        hid2_ready = sem("hid2_ready")
        gelu_done = sem("gelu_done")
        out2_done = sem("out2_done")
        acc_free = sem("acc_free")
        tanh_done = sem("tanh_done")
        z_ready = sem("z_ready")
        ez_ready = sem("ez_ready")
        wx_ready = sem("wx_ready")
        hid3_ready = sem("hid3_ready")
        silu_done = sem("silu_done")
        prod3_done = sem("prod3_done")
        out3_done = sem("out3_done")
        stored = sem("stored")

        STG = (4, 4, 4, 4, 2)
        NG = len(STG)

        block = ctx.enter_context(nc.Block())

        @block.sync
        def _(sp):
            for h in range(2):
                sp.dma_start(X[h * C:(h + 1) * C], x[h * J:(h + 1) * J].rearrange("j c s -> c j s")).then_inc(x_loaded, 16)
            sp.dma_start(cst[:], consts).then_inc(const_loaded, 16)
            sp.wait_ge(block_zeroed, 1)
            for h in range(2):
                sp.dma_start(w_off[h * C:(h + 1) * C, :, h * NOFF:(h + 1) * NOFF],
                             wcv[:, WCV["w_off"]].rearrange("c (t o) -> c t o", t=TAPS)).then_inc(off_block_loaded, 16)
            for h in range(2):
                sp.dma_start(wc[h * C:(h + 1) * C, :], w64).then_inc(w64_loaded, 16)
            sp.wait_ge(block_zeroed, 2)
            for h in range(2):
                sp.dma_start(w_conv[h * C:(h + 1) * C, :, h * C:(h + 1) * C],
                             wcv[:, WCV["w_conv"]].rearrange("c (t o) -> c t o", t=TAPS)).then_inc(conv_block_loaded, 16)
            sp.dma_start(wa[:], wat).then_inc(wat_loaded, 16)
            sp.dma_start(wk[:], w128).then_inc(w128_loaded, 16)
            sp.dma_start(b2row[0:2, :], b2.to_broadcast([2, E2 * C])).then_inc(b2_loaded, 16)
            for m in range(3):
                if m == 0:
                    sp.wait_ge(x1_tile_ready, NP)
                    sp.wait_ge(avl_ready, 1)
                else:
                    sp.wait_ge(stage_split, m)
                for h in range(2):
                    sp.dma_start(stage[h * C:(h + 1) * C, :], wexp[m]).then_inc(stage_loaded, 16)
            for c in range(J):
                sp.wait_ge(misc_free, FILL["oT", c] + 1)
                for h in range(2):
                    for pt in range(PT):
                        sp.dma_start(out[h * J + c, :, pt * P:(pt + 1) * P], X[pt * C:(pt + 1) * C, c, h * P:(h + 1) * P]).then_inc(stored, 16)
            sp.wait_ge(stored, 16 * J * 2 * PT)

        @block.gpsimd
        def _(pool):
            nc.gpsimd.memset(gs[:], 0.0).then_inc(gs_zeroed, 1)
            steps = [0]

            def step(ins):
                ins.then_inc(pool_step, 1)
                steps[0] += 1

            def settle():
                pool.wait_ge(pool_step, steps[0])

            nc.gpsimd.memset(w_off, 0.0).then_inc(block_zeroed, 1)
            nc.gpsimd.memset(GHP[:].bitcast(F32), 0.0).then_inc(pads_zeroed, 1)
            nc.gpsimd.memset(GLP[:].bitcast(F32), 0.0).then_inc(pads_zeroed, 1)
            nc.gpsimd.memset(w_conv, 0.0).then_inc(block_zeroed, 1)
            nc.gpsimd.memset(G2, 0.0).then_inc(pads_zeroed, 1)
            nc.gpsimd.memset(PB[:], 0.0).then_inc(pads_zeroed, 1)
            nc.gpsimd.memset(b2s[:].bitcast(F32), 0.0).then_inc(b2s_zeroed, 1)
            nc.gpsimd.memset(ones[:].bitcast(F32), 1.0).then_inc(b2s_zeroed, 1)
            for j in range(J):
                pool.wait_ge(gh_ready, j + 1)
                pool.wait_ge(g_ready, j + 1)
                nc.gpsimd.tensor_tensor(GL[:, j], G[:, j], GH[:, j].bitcast(F32), ALU.subtract).then_inc(gl_ready, 1)
                if j == 0:
                    pool.wait_ge(dh_ready, 1)
                    pool.wait_ge(w64_loaded, 32)
                    nc.gpsimd.tensor_tensor(DL[:], w_("w_dcn"), DH[:].bitcast(F32), ALU.subtract).then_inc(dl_ready, 1)
            pool.wait_ge(swh_ready, 3)
            for at, width in SW.values():
                nc.gpsimd.tensor_tensor(sw[:, 2 * at + width:2 * (at + width)], wc[:, SMALL64][:, at:at + width],
                                        sw[:, 2 * at:2 * at + width].bitcast(F32), ALU.subtract).then_inc(swl_ready, 1)
            pool.wait_ge(b2_loaded, 16)
            pool.wait_ge(const_loaded, 16)
            pool.wait_ge(b2s_zeroed, 2)
            step(nc.gpsimd.tensor_copy(b2hi[0:2].bitcast(F32R), b2row[0:2]))
            settle()
            step(nc.gpsimd.tensor_tensor(b2row[0:2], b2row[0:2], b2hi[0:2], ALU.subtract))
            step(nc.gpsimd.tensor_scalar(b2hi[0:2], b2hi[0:2], cst[0:2, CONST["row0"]], None, ALU.mult))
            settle()
            step(nc.gpsimd.tensor_scalar(b2row[0:2], b2row[0:2], cst[0:2, CONST["row1"]], None, ALU.mult))
            settle()
            nc.gpsimd.tensor_tensor(b2s[0:2], b2row[0:2], b2hi[0:2], ALU.add).then_inc(b2s_ready, 1)
            pool.wait_ge(gates_ready, 2)
            pool.wait_ge(table_loaded, 1)
            gates = cf[0:B, 0:2 * STREAMS].rearrange("p (g n) -> p g n", g=2)
            half = gs[0:B, :, 0:2]
            step(nc.gpsimd.tensor_tensor(half, gates[:, :, 0:2], gates[:, :, 2:4], ALU.add))
            settle()
            step(nc.gpsimd.tensor_tensor(gs[0:B, :, 2:3], half[:, :, 0:1], half[:, :, 1:2], ALU.add))
            settle()
            step(nc.gpsimd.tensor_scalar(V[0:B, 2:3], gs[0:B, 1, 2:3], 0.5, None, ALU.mult))
            settle()
            step(nc.gpsimd.tensor_tensor(V[0:B, 1:2], gs[0:B, 0, 2:3], V[0:B, 2:3], ALU.mult))
            settle()
            nc.gpsimd.tensor_tensor(V3[0:B, :, 1:3], V[0:B, 1:3].unsqueeze(1).to_broadcast([B, J, 2]),
                                    cst[0:B, CONST["sel_image"]].unsqueeze(2).to_broadcast([B, J, 2]), ALU.mult).then_inc(v3_ready, 1)
            for j in range(J):
                pool.wait_ge(scaled_conv_ready, j + 1)
                nc.gpsimd.tensor_tensor(X1[:, j], X1[:, j], HC[:, j], ALU.add).then_inc(conv_added, 1)
            pool.wait_ge(avh_ready, 4)
            nc.gpsimd.tensor_tensor(AVL[:], av, AVH[:].bitcast(F32), ALU.subtract).then_inc(avl_ready, 1)

            norms = [0]

            def ln_power(c):
                norms[0] += 1
                pool.wait_ge(lnvar_ready, norms[0])
                cols = slice(4 * c, 4 * c + 4)
                nc.gpsimd.tensor_tensor(lnst[:, 2, cols], lnst[:, 1, cols], c_("neg_half"), ALU.pow).then_inc(lninv_ready, 1)

            tops = [0]

            def top_power():
                tops[0] += 1
                pool.wait_ge(top_diff_ready, tops[0])
                nc.gpsimd.tensor_tensor(tg[:, 5, 0:CHUNK], c_("euler"), tg[:, 4, 0:CHUNK], ALU.pow).then_inc(top_exp_ready, 1)

            zs = [0]

            def z_power():
                zs[0] += 1
                pool.wait_ge(z_ready, zs[0])
                nc.gpsimd.tensor_tensor(tg[:, 6, 16:16 + CHUNK], c_("euler"), tg[:, 6, 0:CHUNK], ALU.pow).then_inc(ez_ready, 1)

            def fold(buf, width, tiles):
                settle()
                while width > C:
                    width //= 2
                    step(nc.gpsimd.tensor_tensor(buf[:, :, 0:width], buf[:, :, 0:width], buf[:, :, width:2 * width], ALU.add))
                    settle()
                tt = T[:, tiles, :]
                nc.gpsimd.tensor_tensor(tt, tt, buf[:, :, 0:C], ALU.add).then_inc(fold_done, 1)
                pool.wait_ge(fold_done, folds[0] + 1)
                folds[0] += 1

            folds = [0]

            def fold_unit(u):
                c = u // 2 if u < 8 else (u - 8) // 4
                pool.wait_ge(acc_free, 2 * (u + 1))
                fold(pr8[:, :, (u % 2) * UNIT * C:(u % 2 + 1) * UNIT * C], UNIT * C, slice(4 * c, 4 * c + 4))

            def split_stage(m):
                pool.wait_ge(stage_loaded, 32 * (m + 1))
                step(nc.gpsimd.tensor_copy(WH[:, m], stage[:]))
                settle()
                nc.gpsimd.tensor_tensor(WL[:, m], stage[:], WH[:, m].bitcast(F32), ALU.subtract).then_inc(stage_split, 1)

            pool.wait_ge(rows_loaded, 16)

            def add_proj_bias(c, n):
                pool.wait_ge(centered_ready, n)
                tt = T[:, 4 * c:4 * c + 4, :]
                step(nc.gpsimd.tensor_tensor(tt, tt, rw[:, ROWS["b_proj"]].unsqueeze(1).to_broadcast([P, CHUNK, C]), ALU.add))

            ln_power(0)
            add_proj_bias(0, 1)
            for s in range(STEPS + 2):
                a, i = divmod(s, HEADS)
                if s in (3, 17, 25):
                    c = {3: 1, 17: 2, 25: 3}[s]
                    add_proj_bias(c, {1: 2, 2: 3, 3: 5}[c])
                    ln_power(c)
                if i == 1 and a >= 1:
                    pool.wait_ge(heads_normed, 2 * a)
                    settle()
                    fold(pr8[:, 2 * ((a - 1) % 2):2 * ((a - 1) % 2) + 2], HEADS * C, slice(2 * (a - 1), 2 * a))
                if s in (5, 13, 29):
                    split_stage((5, 13, 29).index(s))
                if s in (38, 54):
                    top_power()
                if i == 7 and a in (2, 4, 6):
                    ln_power((a - 2) // 2)
            top_power()
            ln_power(3)
            fold_unit(0)
            top_power()

            fold_unit(1)
            ln_power(0)
            fold_unit(2)
            z_power()
            ln_power(0)
            fold_unit(3)
            top_power()
            ln_power(1)
            fold_unit(4)
            z_power()
            fold_unit(5)
            ln_power(2)
            fold_unit(6)
            fold_unit(7)
            for n in range(4 * E3):
                if n % UNIT == 1 and n > UNIT:
                    fold_unit(8 + n // UNIT - 1)
                if n in (2, 20, 38):
                    ln_power({2: 1, 20: 2, 38: 3}[n])
                if n == 15:
                    ln_power(3)
                if n in (14, 32, 47):
                    top_power()
                if n in (8, 24):
                    z_power()

        @block.scalar
        def _(act):
            act.dma_start(rw[:], rows.to_broadcast([P, NROWS])).then_inc(rows_loaded, 16)

            def sqrt(n, ap):
                act.wait_ge(var_ready, n)
                nc.scalar.activation(ap, ap, ACT.Sqrt).then_inc(sd_ready, 1)

            sqrt(1, small[:, 0:J])
            act.wait_ge(pads_zeroed, 1)
            for j in range(J):
                act.wait_ge(g_ready, j + 1)
                nc.scalar.activation(GHP[:, j, 1:HH + 1, 1:WW + 1], img(G)[:, j], ACT.Copy).then_inc(ghp_ready, 1)
                if j == 0:
                    act.wait_ge(off_block_loaded, 32)
                    nc.scalar.activation(WO[:, :, 0:2 * NOFF], w_off, ACT.Copy).then_inc(wo_ready, 1)
            for j in range(J):
                act.wait_ge(g_ready, j + 1)
                nc.scalar.activation(GH[:, j], G[:, j], ACT.Copy).then_inc(gh_ready, 1)
                if j == 0:
                    act.wait_ge(w64_loaded, 32)
                    nc.scalar.activation(DH[:], w_("w_dcn"), ACT.Copy).then_inc(dh_ready, 1)
            for at, width in SW.values():
                nc.scalar.activation(sw[:, 2 * at:2 * at + width], wc[:, SMALL64][:, at:at + width], ACT.Copy).then_inc(swh_ready, 1)
            act.wait_ge(gs_zeroed, 1)
            nc.scalar.activation(gs[:, 0], gs[:, 0], ACT.Sigmoid).then_inc(table_loaded, 1)
            for r in range(2):
                act.wait_ge(offset_conv_ready, r + 1)
                nc.scalar.activation(OT[0:4 * NOFF, 2 * r:2 * r + 2, :].rearrange("p j n -> p (j n)"), PS[0:4 * NOFF, 5 + r, :],
                                     ACT.Copy).then_inc(ot_ready, 1)

            def u_copy(n):
                act.wait_ge(u_ready, n + 1)
                slot = 1 + 2 * (n % 3)
                nc.scalar.activation(U[:, n, :].rearrange("p (a n) -> p a n", a=2), PS[:, slot:slot + 2, 0:288],
                                     ACT.Copy).then_inc(u_copied, 1)

            for n in range(NT):
                if n % 2 == 0 or n == 1:
                    u_copy(n)
                if n == 1:
                    act.wait_ge(mask_logits_ready, 4)
                    nc.scalar.activation(mask[:], mask[:], ACT.Sigmoid).then_inc(mask_ready, 1)
                if 3 <= n <= 2 * J + 2:
                    j = (n - 3) // 2
                    hj = hats[:, 4 * j:4 * j + 4].rearrange("p t k q -> p (t k q)")
                    if n % 2 == 1:
                        act.wait_ge(hat_diff_ready, j + 1)
                        nc.scalar.activation(hj, hj, ACT.Abs).then_inc(act_step, 1)
                    else:
                        act.wait_ge(act_step, j + 1)
                        nc.scalar.activation(hj, hj, ACT.Relu, bias=1.0, scale=-1.0).then_inc(hat_ready, 1)
            for n in range(NT):
                if n >= 2:
                    act.wait_ge(d_ready, n - 1)
                for g in range(NG):
                    m = n * NG + g
                    act.wait_ge(st_ready, m + 1)
                    nc.scalar.activation(ST[n % 2][:, 4 * g:4 * g + STG[g], :],
                                         PS[:, 1 + m % 4, 0:STG[g] * P].rearrange("p (a n) -> p a n", n=P),
                                         ACT.Copy).then_inc(st_copied, 1)
            sqrt(2, small[:, 0:J])
            act.wait_ge(qe_ready, 1)
            nc.scalar.activation(small[:, 8:8 + J], small[:, 8:8 + J], ACT.Sqrt).then_inc(qs_ready, 1)
            act.wait_ge(logits_ready, 3)
            nc.scalar.activation(M[0:B].rearrange("p a b -> p (a b)"), cf[0:B, 2 * STREAMS:NPHI], ACT.Exp).then_inc(gates_ready, 1)
            nc.scalar.activation(cf[0:B, 0:2 * STREAMS], cf[0:B, 0:2 * STREAMS], ACT.Sigmoid).then_inc(gates_ready, 1)
            act.wait_ge(cb_ready, 1)
            cbp = PS[:, 3, 32:32 + 2 * J].rearrange("p (j k) -> p j k", k=2)
            act.wait_ge(w64_loaded, 32)
            nc.scalar.activation(CB[:, :, 1:3], cbp, ACT.Copy).then_inc(cb_copied, 1)
            nc.scalar.activation(bb[:], cbp[:, :, 1], ACT.Copy, scale=w_("conv_b")).then_inc(cb_copied, 1)
            act.wait_ge(cb_copied, 2)
            for j in range(J):
                act.wait_ge(conv_ready, j // 2 + 1)
                nc.scalar.activation(HC[:, j], PS[:, 1 + j // 2, (j % 2) * S:(j % 2 + 1) * S], ACT.Identity, bias=bb[:, j:j + 1],
                                     scale=CB[:, j, 1:2]).then_inc(scaled_conv_ready, 1)
            act.wait_ge(av_ready, 1)
            for to in (AVH[:], av):
                nc.scalar.activation(to[:, 0:1024].rearrange("p (a n) -> p a n", a=2), PS[:, 4:6, :], ACT.Copy).then_inc(avh_ready, 1)
                nc.scalar.activation(to[:, 1024:1536].rearrange("p (a n) -> p a n", a=2), PS[:, 6:8, 0:256], ACT.Copy).then_inc(avh_ready, 1)

            def project(name):
                kind, a, i = name
                if on_side(name):
                    act.wait_ge(side_filled, SIDE[name] + 1)
                else:
                    act.wait_ge(misc_filled, FILL[name] + 1)
                bank = PS[:, 2 if on_side(name) else 7, :]
                if kind == "q":
                    nc.scalar.activation(QH[:, a % 2, 2 * i:2 * i + 2, :].rearrange("p g n -> p (g n)"), bank, ACT.Copy).then_inc(qh_copied, 1)
                else:
                    nc.scalar.activation(VV[:, a % 2, i, :], bank, ACT.Copy).then_inc(side_free if on_side(name) else misc_free, 1)

            def copy_probs(v):
                act.wait_ge(pT_ready, v + 1)
                if v >= 3:
                    act.wait_ge(pv_done, v - 2)
                nc.scalar.activation(PTs[:, v % 3, :], PS[:, 3 + v % 2, 0:384], ACT.Copy).then_inc(pT_copied, 1)

            for name in FIRST_PROJECTIONS:
                project(name)
            for s in range(STEPS + 1):
                if s < STEPS:
                    a, g = divmod(s, HEADS)
                    act.wait_ge(masked_ready, s + 1)
                    if s >= 3:
                        act.wait_ge(pT_ready, s - 2)
                    if g == 0 and a >= 2:
                        act.wait_ge(heads_normed, 2 * (a - 1))
                    for qt in range(PT):
                        cols = slice(0, P) if qt == 0 else slice(P, 3 * P)
                        ins = nc.scalar.activation(PR[:, s % 3, cols], MS[:, s % 3, cols], ACT.Exp, bias=nmx[:, s % 3, qt:qt + 1],
                                                   scale=-1.0, accum_out=rsum[:, a % 2, qt, g:g + 1])
                    ins.then_inc(probs_ready, 1)
                if s >= 1:
                    copy_probs(s - 1)
                if s < STEPS:
                    for name in attention_fills(s):
                        if name[0] in ("q", "v"):
                            project(name)

            act.wait_ge(w128_loaded, 16)

            def tanh(c):
                act.wait_ge(misc_free, FILL["pC", c] + 1)
                nc.scalar.activation(PJ[:], PJ[:], ACT.Tanh).then_inc(tanh_done, 1)

            for n in range(4 * E2 * 2):
                e2 = n % (2 * E2)
                act.wait_ge(hid2_ready, n + 1)
                if n >= 3:
                    act.wait_ge(out2_done, n - 2)
                nc.scalar.activation(hid[:, n % 3], PS[:, n % 3, :], ACT.Gelu,
                                     bias=wk[:, W128["b1"]][:, e2:e2 + 1]).then_inc(gelu_done, 1)
                if n in (30, 54):
                    tanh({30: 0, 54: 1}[n])

            for n in range(4 * E3):
                act.wait_ge(hid3_ready, 2 * n + 1)
                if n >= 2:
                    act.wait_ge(prod3_done, n - 1)
                nc.scalar.activation(sil[:, n % 2], PS[:, 2 * n % 3, :], ACT.Silu).then_inc(silu_done, 1)
                if n in (6, 23):
                    tanh({6: 2, 23: 3}[n])

        @block.vector
        def _(dve):
            steps = [0]

            def step(ins):
                ins.then_inc(dve_step, 1)
                steps[0] += 1

            def settle():
                dve.wait_ge(dve_step, steps[0])

            def image_stats(src, j):
                step(nc.vector.bn_stats(stat[:, j, :], src[:, j, :]))

            def group_norm(n):
                settle()
                for j in range(J):
                    step(nc.vector.bn_aggr(mv[:, n, j, :], stat[:, j, :]))
                settle()
                mean, var = mv[:, n, :, 0], mv[:, n, :, 1]
                step(nc.vector.tensor_tensor(small[:, 0:J], mean, mean, ALU.mult))
                settle()
                nc.vector.tensor_tensor(var, var, small[:, 0:J], ALU.add).then_inc(moments_ready, 1)
                dve.wait_ge(group_moments_ready, n + 1)
                step(nc.vector.tensor_copy(gmv[:].rearrange("p j m -> p (j m)"), PS[:, 7, 0:2 * J]))
                settle()
                step(nc.vector.tensor_tensor(small[:, 4:4 + J], gmv[:, :, 0], gmv[:, :, 0], ALU.mult))
                settle()
                step(nc.vector.tensor_tensor(small[:, 0:J], gmv[:, :, 1], small[:, 4:4 + J], ALU.subtract))
                settle()
                nc.vector.tensor_scalar(small[:, 0:J], small[:, 0:J], EPS5, None, ALU.add).then_inc(var_ready, 1)
                dve.wait_ge(sd_ready, n + 1)
                step(nc.vector.reciprocal(small[:, 4:4 + J], small[:, 0:J]))
                settle()
                nc.vector.scalar_tensor_tensor(small[:, 12:12 + J], gmv[:, :, 0], -1.0, small[:, 4:4 + J], ALU.mult,
                                               ALU.mult).then_inc(norm_ready, 1)
                dve.wait_ge(norm_ready, n + 1)

            def apply_norm(n, src, dst):
                for j in range(J):
                    nc.vector.tensor_scalar(dst[:, j], img(src)[:, j], small[:, 4 + j:5 + j],
                                            small[:, 12 + j:13 + j], ALU.mult, ALU.add).then_inc(g_ready, 1)

            dve.wait_ge(x_loaded, 32)
            for j in range(J):
                image_stats(X, j)
            group_norm(0)
            apply_norm(0, X, img(G))
            dve.wait_ge(pads_zeroed, 2)
            for j in range(J):
                dve.wait_ge(ghp_ready, j + 1)
                dve.wait_ge(g_ready, j + 1)
                nc.vector.tensor_tensor(GLP[:, j, 1:HH + 1, 1:WW + 1], img(G)[:, j], GHP[:, j, 1:HH + 1, 1:WW + 1].bitcast(F32),
                                        ALU.subtract).then_inc(glp_ready, 1)
                if j == 0:
                    dve.wait_ge(wo_ready, 1)
                    dve.wait_ge(off_block_loaded, 32)
                    nc.vector.tensor_tensor(WO[:, :, 2 * NOFF:4 * NOFF], w_off, WO[:, :, 0:2 * NOFF].bitcast(F32),
                                            ALU.subtract).then_inc(wo_ready, 1)

            dve.wait_ge(w64_loaded, 32)
            dve.wait_ge(rows_loaded, 16)
            dve.wait_ge(const_loaded, 16)
            step(nc.vector.tensor_tensor(phr[:], w_("phi").rearrange("p (n o) -> p n o", n=STREAMS),
                                         w_("rms").unsqueeze(2).to_broadcast([P, STREAMS, NPHI]), ALU.mult))
            step(nc.vector.tensor_tensor(c_("base").rearrange("p (a k) -> p a k", a=PT), c_("base").rearrange("p (a k) -> p a k", a=PT),
                                         rw[:, ROWS["b_off"]][:, 0:2 * TAPS].unsqueeze(1).to_broadcast([P, PT, 2 * TAPS]), ALU.add))
            settle()
            step(nc.vector.tensor_reduce(weff[:], phr[:].rearrange("p n o -> p o n"), AX.X, ALU.add))

            dve.wait_ge(offsets_ready, 1)
            om = PS[:, 0, 0:NP * 2 * NOFF].rearrange("p (j t h o) -> p t h j o", j=J, t=PT, h=2)
            co = coord[:].rearrange("p (j t h) k -> p t h j k", h=2, j=J)
            mo = mask[:].rearrange("p (j t h) k -> p t h j k", h=2, j=J)
            for t in range(PT):
                for h in range(2):
                    nc.vector.tensor_tensor(mo[:, t, h], om[:, t, h, :, 2 * TAPS:NOFF],
                                            rw[:, ROWS["b_off"]][:, 2 * TAPS:NOFF].unsqueeze(1).to_broadcast([P, J, TAPS]),
                                            ALU.add).then_inc(mask_logits_ready, 1)
            for t in range(PT):
                for h in range(2):
                    step(nc.vector.tensor_tensor(co[:, t, h], om[:, t, h, :, 0:2 * TAPS],
                                                 c_("base").rearrange("p (a k) -> p a k", a=PT)[:, t].unsqueeze(1).to_broadcast([P, J, 2 * TAPS]), ALU.add))
            settle()

            def chunk(j):
                return hats[:, 4 * j:4 * j + 4].rearrange("p t k q -> p (t k) q")

            def u_copy(n):
                dve.wait_ge(u_ready, n + 1)
                slot = 1 + 2 * (n % 3)
                nc.vector.tensor_copy(U[:, n, :].rearrange("p (a n) -> p a n", a=2), PS[:, slot:slot + 2, 0:288]).then_inc(u_copied_dve, 1)

            for j in range(J):
                nc.vector.tensor_tensor(chunk(j), coord[:, 4 * j:4 * j + 4].rearrange("p t k -> p (t k)").unsqueeze(2).to_broadcast([P, 8 * TAPS, WW]),
                                        c_("grid").unsqueeze(1).to_broadcast([P, 8 * TAPS, WW]), ALU.subtract).then_inc(hat_diff_ready, 1)
                if j >= 1:
                    u_copy(2 * j + 1)

            def x1_tile(ip):
                j, pt = divmod(ip, PT)
                dve.wait_ge(dT_ready, ip + 1)
                nc.vector.scalar_tensor_tensor(X1[:, j, pt * P:(pt + 1) * P], PS[:, 7 * (ip % 2), 0:P], w_("b_dcn"),
                                               X[:, j, pt * P:(pt + 1) * P], ALU.add, ALU.add).then_inc(x1_tile_ready, 1)

            def d_copy(ip):
                dve.wait_ge(d_ready, 2 * ip + 2)
                if ip >= 2:
                    dve.wait_ge(dT_ready, ip - 1)
                nc.vector.tensor_copy(D[:, ip % 2, :], PS[:, 5 + ip % 2, 0:P]).then_inc(d_copied, 1)

            for n in range(NT):
                if n % 4 == 0:
                    dve.wait_ge(hat_ready, n // 4 + 1)
                    dve.wait_ge(mask_ready, 1)
                    hx = chunk(n // 4).rearrange("p (k c) q -> p c k q", c=2)[:, 1]
                    step(nc.vector.tensor_tensor(hx, hx, mask[:, n:n + 4].rearrange("p t k -> p (t k)").unsqueeze(2).to_broadcast([P, 4 * TAPS, WW]),
                                                 ALU.mult))
                    settle()
                if n >= 2:
                    dve.wait_ge(st_ready, NG * (n - 1))
                hk = hats[:, n].rearrange("p (k c) q -> p c k q", c=2)
                nc.vector.tensor_tensor(prods[n % 2].rearrange("p k (a b) -> p k a b", a=HH),
                                        hk[:, 0].unsqueeze(3).to_broadcast([P, TAPS, HH, WW]),
                                        hk[:, 1].unsqueeze(2).to_broadcast([P, TAPS, HH, WW]), ALU.mult).then_inc(prod_ready, 1)
                if n == 0:
                    for m in (9, 11, 13):
                        u_copy(m)
                if n == 1:
                    u_copy(15)
                if n >= 4 and n % 2 == 0:
                    d_copy(n // 2 - 2)
                if n >= 5 and n % 2 == 1:
                    x1_tile(n // 2 - 2)
                    if n % 4 == 1 and n > 5:
                        j = n // 4 - 2
                        dve.wait_ge(x1_tile_ready, 2 * j + 2)
                        image_stats(X1, j)
            for ip in range(NP - 2, NP):
                d_copy(ip)
                x1_tile(ip)
            dve.wait_ge(x1_tile_ready, NP)

            image_stats(X1, 2)
            image_stats(X1, 3)
            group_norm(1)
            pooled = small[:, 16:16 + J]
            step(nc.vector.tensor_tensor(pooled, mv[:, 1, :, 0], gmv[:, :, 0], ALU.subtract))
            settle()
            step(nc.vector.tensor_tensor(pooled, pooled, small[:, 4:4 + J], ALU.mult))
            settle()
            nc.vector.tensor_tensor(small[:, 20:20 + J], pooled, pooled, ALU.mult).then_inc(sq_ready, 1)
            dve.wait_ge(q_ready, 1)
            nc.vector.tensor_scalar(small[:, 8:8 + J], PS[:, 3, 0:J], 1e-20, None, ALU.add).then_inc(qe_ready, 1)
            dve.wait_ge(qs_ready, 1)
            step(nc.vector.reciprocal(small[:, 24:24 + J], small[:, 8:8 + J]))
            settle()
            dve.wait_ge(pads_zeroed, 4)
            for h in range(2):
                hs = slice(h * C, (h + 1) * C)
                nc.vector.tensor_tensor(PB[hs, h * J:(h + 1) * J], pooled[hs], small[hs, 24:24 + J], ALU.mult).then_inc(pb_ready, 1)
            dve.wait_ge(pads_zeroed, 3)
            apply_norm(1, X1, G2[:, :, 1:HH + 1, 1:WW + 1])
            dve.wait_ge(coef_ready, 1)
            step(nc.vector.tensor_tensor(cf[0:B], PS[0:B, 3, 0:NPHI], rw[0:B, ROWS["phi_b"]], ALU.add))
            settle()
            al = rw[0:B, ROWS["alpha"]]
            nc.vector.tensor_scalar(cf[0:B, 0:4], cf[0:B, 0:4], al[:, 0:1], None, ALU.mult).then_inc(logits_ready, 1)
            nc.vector.tensor_scalar(cf[0:B, 4:8], cf[0:B, 4:8], al[:, 1:2], None, ALU.mult).then_inc(logits_ready, 1)
            nc.vector.tensor_scalar(cf[0:B, 8:NPHI], cf[0:B, 8:NPHI], al[:, 2:3], None, ALU.mult).then_inc(logits_ready, 1)
            dve.wait_ge(gates_ready, 1)
            MM = M[0:B]
            for _ in range(SINKHORN):
                for view in (MM, MM.rearrange("p a b -> p b a")):
                    step(nc.vector.tensor_reduce(mn[0:B], view, AX.X, ALU.add))
                    settle()
                    step(nc.vector.reciprocal(mn[0:B], mn[0:B]))
                    settle()
                    step(nc.vector.tensor_tensor(view, view, mn[0:B].unsqueeze(2).to_broadcast([B, STREAMS, STREAMS]), ALU.mult))
                    settle()
            step(nc.vector.tensor_reduce(V[0:B, 0:1], MM.rearrange("p a b -> p (a b)")[:, 0:16:5], AX.X, ALU.add))
            settle()
            nc.vector.scalar_tensor_tensor(V3[0:B, :, 0], V[0:B, 0:1].to_broadcast([B, J]), 1.0 / STREAMS,
                                           cst[0:B, CONST["sel_image"]], ALU.mult, ALU.mult).then_inc(v3_diag_ready, 1)
            dve.wait_ge(cb_ready, 2)
            step(nc.vector.tensor_copy(CB[:, :, 0], PS[:, 0, 0:J]))
            settle()

            def second_residual(j):
                dve.wait_ge(conv_added, j + 1)
                nc.vector.scalar_tensor_tensor(img(X1)[:, j], G2[:, j, 1:HH + 1, 1:WW + 1], CB[:, j, 0:1],
                                               img(X1)[:, j], ALU.mult, ALU.add).then_inc(x2_ready, 1)

            def take_tokens(j):
                dve.wait_ge(misc_filled, FILL["xT", j] + 1)
                ins = nc.vector.tensor_copy(T[:, 4 * j:4 * j + 4, :].rearrange("p (h t) c -> p h t c", h=2),
                                            PS[:, 7, 0:2 * P].rearrange("p (t h c) -> p h t c", h=2, c=C))
                ins.then_inc(misc_free, 1)
                dve.wait_ge(misc_free, FILL["xT", j] + 1)

            norms = [0]

            def ln_center(c):
                ts = slice(4 * c, 4 * c + 4)
                settle()
                step(nc.vector.tensor_reduce(lnst[:, 0, ts], T[:, ts], AX.X, ALU.add))
                settle()
                nc.vector.scalar_tensor_tensor(Y[:, ts], lnst[:, 0, ts].unsqueeze(2).to_broadcast([P, CHUNK, C]), -1.0 / C, T[:, ts],
                                               ALU.mult, ALU.add).then_inc(centered_ready, 1)

            def ln_variance(c):
                ts = slice(4 * c, 4 * c + 4)
                norms[0] += 1
                dve.wait_ge(centered_ready, norms[0])
                step(nc.vector.tensor_tensor(Y2[:, ts, 0:C], Y[:, ts], Y[:, ts], ALU.mult))
                settle()
                step(nc.vector.tensor_reduce(lnst[:, 1, ts], Y2[:, ts, 0:C], AX.X, ALU.add))
                settle()
                nc.vector.tensor_scalar(lnst[:, 1, ts], lnst[:, 1, ts], 1.0 / C, EPS5, ALU.mult, ALU.add).then_inc(lnvar_ready, 1)

            def ln_stats(c):
                ln_center(c)
                ln_variance(c)

            outs = [0]

            def ln_out(c):
                ts = slice(4 * c, 4 * c + 4)
                outs[0] += 1
                dve.wait_ge(lninv_ready, outs[0])
                step(nc.vector.tensor_tensor(Y[:, ts], Y[:, ts], lnst[:, 2, ts].unsqueeze(2).to_broadcast([P, CHUNK, C]), ALU.mult))
                settle()
                step(nc.vector.tensor_copy(Y2[:, ts, 0:C].bitcast(F32R), Y[:, ts]))
                settle()
                nc.vector.tensor_tensor(Y2[:, ts, C:2 * C], Y[:, ts], Y2[:, ts, 0:C], ALU.subtract).then_inc(y2_ready, 1)

            def ln_evac(name, c):
                dve.wait_ge(misc_filled, FILL[name, c] + 1)
                nc.vector.tensor_copy(YTs[:, c * CW:(c + 1) * CW], PS[:, 7, :]).then_inc(misc_free, 1)

            second_residual(0)
            take_tokens(0)
            ln_stats(0)
            for j in range(1, J):
                second_residual(j)
            ln_out(0)
            ln_evac("yA", 0)

            queries = [0]

            def query_remainders(name):
                _, a, i = name
                queries[0] += 1
                if on_side(name):
                    dve.wait_ge(side_filled, SIDE[name] + 1)
                else:
                    dve.wait_ge(misc_filled, FILL[name] + 1)
                dve.wait_ge(qh_copied, queries[0])
                nc.vector.tensor_tensor(QL[:, a % 2, 2 * i:2 * i + 2, :].rearrange("p g n -> p (g n)"), PS[:, 2 if on_side(name) else 7, :],
                                        QH[:, a % 2, 2 * i:2 * i + 2, :].rearrange("p g n -> p (g n)").bitcast(F32),
                                        ALU.subtract).then_inc(side_free if on_side(name) else misc_free, 1)

            def normalise(a, hq):
                hh = slice(4 * hq, 4 * hq + 4)
                dve.wait_ge(probs_ready, HEADS * a + 4 * hq + 4)
                step(nc.vector.reciprocal(rinv[:, a % 2, :, hh], rsum[:, a % 2, :, hh]))
                settle()
                dve.wait_ge(pv_done, HEADS * a + 4 * hq + 4)
                if a >= 2:
                    dve.wait_ge(fold_done, a - 1)
                nc.vector.tensor_tensor(pr8[:, 2 * (a % 2):2 * (a % 2) + 2, 4 * hq * C:4 * (hq + 1) * C].rearrange("p t (h c) -> p t h c", h=4),
                                        PS[:, 5 + hq, :].rearrange("p (h t c) -> p t h c", h=4, t=PT),
                                        rinv[:, a % 2, :, hh].unsqueeze(3).to_broadcast([P, PT, 4, C]), ALU.mult).then_inc(heads_normed, 1)

            tops = [0]

            def take_logits(name, c, bias, E):
                lg = tg[:, 0, 0:CHUNK * E].rearrange("p (t e) -> p t e", e=E)
                bank = PS[:, 7, 0:2 * CHUNK * E].rearrange("p (t r e) -> p r t e", r=2, e=E)
                dve.wait_ge(misc_filled, FILL[name, c] + 1)
                step(nc.vector.tensor_tensor(lg, bank[:, 0], bias.unsqueeze(1).to_broadcast([P, CHUNK, E]), ALU.add))
                settle()
                nc.vector.tensor_tensor(lg, bank[:, 1], lg, ALU.add).then_inc(misc_free, 1)

            def top_views(E):
                return [tg[:, r, 0:CHUNK * E].rearrange("p (t e) -> p t e", e=E) for r in range(4)] + [tg[:, 4, 4 * r:4 * r + 4] for r in range(5)]

            def wide(v, E):
                return v.unsqueeze(2).to_broadcast([P, CHUNK, E])

            def first_max(src, m, hot, E):
                _, key, _, _, _, _, _, mk, _ = top_views(E)
                step(nc.vector.tensor_reduce(m, src, AX.X, ALU.max))
                settle()
                step(nc.vector.tensor_tensor(key, src, wide(m, E), ALU.is_equal))
                settle()
                step(nc.vector.tensor_tensor(key, key, c_("desc")[:, E3 - E:E3].unsqueeze(1).to_broadcast([P, CHUNK, E]), ALU.mult))
                settle()
                step(nc.vector.tensor_reduce(mk, key, AX.X, ALU.max))
                settle()
                step(nc.vector.tensor_tensor(hot, key, wide(mk, E), ALU.is_equal))
                settle()

            def top_first(name, c, E):
                lg, _, h1, _, _, m1, _, _, _ = top_views(E)
                dve.wait_ge(misc_free, FILL[name, c] + 1)
                first_max(lg, m1, h1, E)

            def top_second(E):
                lg, _, h1, l2, df, m1, m2, _, _ = top_views(E)
                step(nc.vector.scalar_tensor_tensor(l2, h1, NEG, lg, ALU.mult, ALU.add))
                settle()
                first_max(l2, m2, l2, E)
                nc.vector.tensor_tensor(df, m2, m1, ALU.subtract).then_inc(top_diff_ready, 1)

            def top_gate(c, E):
                _, _, h1, l2, _, _, _, mk, w1 = top_views(E)
                ex = tg[:, 5, 0:CHUNK]
                tops[0] += 1
                dve.wait_ge(top_exp_ready, tops[0])
                step(nc.vector.tensor_scalar(w1, ex, 1.0, None, ALU.add))
                settle()
                step(nc.vector.reciprocal(w1, w1))
                settle()
                step(nc.vector.tensor_tensor(mk, ex, w1, ALU.mult))
                settle()
                step(nc.vector.tensor_tensor(h1, h1, wide(w1, E), ALU.mult))
                step(nc.vector.tensor_tensor(l2, l2, wide(mk, E), ALU.mult))
                settle()
                step(nc.vector.tensor_tensor(gate[:, 0 if E == E2 else 1, 4 * c:4 * c + 4, 0:E], h1, l2, ALU.add))
                settle()

            def top2(name, c, bias, E):
                take_logits(name, c, bias, E)
                top_first(name, c, E)
                top_second(E)
                top_gate(c, E)

            for name in FIRST_PROJECTIONS:
                if name[0] == "q":
                    query_remainders(name)
            take_tokens(1)

            def take_fills(s):
                for what in attention_fills(s):
                    if what[0] == "q":
                        query_remainders(what)
                    elif what[0] in ("yA", "yB"):
                        ln_evac(*what)
                    elif what[0] == "xT":
                        take_tokens(what[1])
                    elif what[0] == "gB":
                        take_logits(*what, rw[:, ROWS["bg2"]], E2)

            for s in range(STEPS):
                a, g = divmod(s, HEADS)
                dve.wait_ge(scores_ready, s + 1)
                if s >= 3:
                    dve.wait_ge(probs_ready, s - 2)
                nc.vector.tensor_tensor_reduce(MS[:, s % 3, 0:P], PS[:, s % 2, 0:P], c_("causal")[:, P:2 * P], -SCALE, 1e30,
                                               ALU.add, ALU.min, nmx[:, s % 3, 0:1])
                nc.vector.tensor_tensor_reduce(MS[:, s % 3, P:3 * P], PS[:, s % 2, P:3 * P], c_("causal"), -SCALE, 1e30,
                                               ALU.add, ALU.min, nmx[:, s % 3, 1:2]).then_inc(masked_ready, 1)
                if s >= 1:
                    take_fills(s - 1)
                if g == 3 and a >= 1:
                    normalise(a - 1, 1)
                if g == 7:
                    normalise(a, 0)
                if s in (2, 17, 25):
                    ln_center({2: 1, 17: 2, 25: 3}[s])
                if s in (3, 18, 26):
                    ln_variance({3: 1, 18: 2, 26: 3}[s])
                if s in (5, 20, 30):
                    ln_out({5: 1, 20: 2, 30: 3}[s])
                if a in (3, 5, 7):
                    if g == 0:
                        dve.wait_ge(fold_done, a - 1)
                        ln_center(a // 2 - 1)
                    if g == 1:
                        ln_variance(a // 2 - 1)
                    if g == 5:
                        ln_out(a // 2 - 1)
                if s in (37, 53):
                    top_first("gB", s // 16 - 2, E2)
                if s in (38, 54):
                    top_second(E2)
                if s in (42, 58):
                    top_gate(s // 16 - 2, E2)

            def combine(u):
                m, c, e = (0, u // 2, u % 2 * UNIT) if u < 8 else (1, (u - 8) // 4, u % 4 * UNIT)
                if m == 0:
                    dve.wait_ge(out2_done, 2 * UNIT * (u + 1))
                else:
                    dve.wait_ge(out3_done, UNIT * (u - 7))
                dve.wait_ge(fold_done, IMAGES + max(0, u - 1))
                for i in range(2):
                    nc.vector.tensor_tensor(pr8[:, 2 * i:2 * i + 2, (u % 2) * UNIT * C:(u % 2 + 1) * UNIT * C].rearrange("p q (e c) -> p q e c", c=C),
                                            PS[:, 3 + 2 * (u % 2) + i, :].rearrange("p (q e c) -> p q e c", q=2, c=C),
                                            gate[:, m, 4 * c + 2 * i:4 * c + 2 * i + 2, e:e + UNIT].unsqueeze(3).to_broadcast([P, 2, UNIT, C]),
                                            ALU.mult).then_inc(acc_free, 1)

            take_fills(STEPS - 1)
            normalise(IMAGES - 1, 1)
            top_first("gB", 2, E2)
            top_second(E2)
            top_gate(2, E2)
            dve.wait_ge(fold_done, IMAGES)
            ln_stats(3)
            ln_out(3)
            combine(0)
            ln_evac("yB", 3)
            top2("gB", 3, rw[:, ROWS["bg2"]], E2)

            def window_bias(c):
                dve.wait_ge(misc_filled, FILL["pC", c] + 1)
                bank = PS[:, 7, 0:2 * CHUNK * A3].rearrange("p (t r a) -> p r t a", r=2, a=A3)
                step(nc.vector.tensor_tensor(PJ[:], bank[:, 0], rw[:, ROWS["bp"]].unsqueeze(1).to_broadcast([P, CHUNK, A3]), ALU.add))
                settle()
                nc.vector.tensor_tensor(PJ[:], bank[:, 1], PJ[:], ALU.add).then_inc(misc_free, 1)

            def window_logits(c):
                dve.wait_ge(tanh_done, c + 1)
                step(nc.vector.tensor_tensor(PJ[:], PJ[:], rw[:, ROWS["wg"]].unsqueeze(1).to_broadcast([P, CHUNK, A3]), ALU.mult))
                settle()
                nc.vector.tensor_reduce(tg[:, 6, 0:CHUNK], PJ[:], AX.X, ALU.add, negate=True).then_inc(z_ready, 1)

            def window_gate(c):
                gg = tg[:, 6, 32:32 + CHUNK]
                dve.wait_ge(ez_ready, c + 1)
                step(nc.vector.tensor_scalar(gg, tg[:, 6, 16:16 + CHUNK], 1.0, None, ALU.add))
                settle()
                step(nc.vector.reciprocal(gg, gg))
                settle()
                step(nc.vector.tensor_copy(WX[:, :, C], gg))
                nc.vector.tensor_tensor(WX[:, :, 0:C], Y[:, 4 * c:4 * c + 4], gg.unsqueeze(2).to_broadcast([P, CHUNK, C]), ALU.mult).then_inc(wx_ready, 1)

            def window_add(c):
                bank = PS[:, 7, 0:CHUNK * (C + 1)].rearrange("p (t c) -> p t c", c=C + 1)
                rd = tg[:, 7, 0:CHUNK]
                dve.wait_ge(misc_filled, FILL["wC", c] + 1)
                step(nc.vector.reciprocal(rd, bank[:, :, C]))
                settle()
                nc.vector.tensor_tensor(wy[:], bank[:, :, 0:C], rd.unsqueeze(2).to_broadcast([P, CHUNK, C]), ALU.mult).then_inc(misc_free, 1)
                dve.wait_ge(misc_free, FILL["wC", c] + 1)
                tv = T[:, 4 * c:4 * c + 4, :].rearrange("p (h t) c -> p t h c", t=PT)
                step(nc.vector.tensor_tensor(tv, tv, wy[:].rearrange("p (t h) c -> p t h c", t=PT), ALU.add))

            def window_front(c):
                dve.wait_ge(fold_done, IMAGES + 2 * (c + 1))
                ln_stats(c)
                combine(2 * c + 2)
                ln_out(c)
                if c < 2:
                    ln_evac("yC", c)
                    window_bias(c)

            combine(1)
            window_front(0)
            window_logits(0)
            window_gate(0)
            window_add(0)
            ln_stats(0)
            combine(3)
            ln_out(0)
            ln_evac("yD", 0)
            top2("gD", 0, rw[:, ROWS["bg3"]], E3)
            window_front(1)
            window_logits(1)
            window_gate(1)
            combine(5)
            window_add(1)
            window_front(2)
            combine(7)

            def output(c):
                dve.wait_ge(misc_filled, FILL["oT", c] + 1)
                nc.vector.tensor_copy(X[:, c, :], PS[:, 7, 0:2 * P]).then_inc(misc_free, 1)

            for n in range(4 * E3):
                dve.wait_ge(silu_done, n + 1)
                dve.wait_ge(hid3_ready, 2 * n + 2)
                if n >= 3:
                    dve.wait_ge(out3_done, n - 2)
                nc.vector.tensor_tensor(hid[:, n % 3], sil[:, n % 2], PS[:, (2 * n + 1) % 3, :], ALU.mult).then_inc(prod3_done, 1)
                if n % UNIT == 1 and n > UNIT:
                    combine(8 + n // UNIT - 1)
                if n in (0, 19, 36):
                    ln_center({0: 1, 19: 2, 36: 3}[n])
                if n in (2, 20, 38):
                    ln_variance({2: 1, 20: 2, 38: 3}[n])
                if n in (4, 23, 39):
                    ln_out({4: 1, 23: 2, 39: 3}[n])
                if n in (10, 27, 43):
                    ln_evac("yD", {10: 1, 27: 2, 43: 3}[n])
                if n in (12, 31, 46):
                    c = {12: 1, 31: 2, 46: 3}[n]
                    take_logits("gD", c, rw[:, ROWS["bg3"]], E3)
                    top_first("gD", c, E3)
                if n in (14, 32, 47):
                    top_second(E3)
                if n in (18, 35, 50):
                    top_gate({18: 1, 35: 2, 50: 3}[n], E3)
                if n == 7:
                    ln_center(3)
                if n == 15:
                    ln_variance(3)
                if n == 18:
                    ln_out(3)
                if n in (2, 20):
                    ln_evac("yC", {2: 2, 20: 3}[n])
                if n in (6, 22):
                    window_bias({6: 2, 22: 3}[n])
                if n in (8, 24):
                    window_logits({8: 2, 24: 3}[n])
                if n in (11, 26):
                    window_gate({11: 2, 26: 3}[n])
                if n in (16, 28):
                    window_add({16: 2, 28: 3}[n])
                if n in (38, 40, 56):
                    output({38: 0, 40: 1, 56: 2}[n])
            combine(23)
            buf = pr8[:, :, UNIT * C:2 * UNIT * C]
            dve.wait_ge(acc_free, 48)
            for width in (2 * C, C):
                step(nc.vector.tensor_tensor(buf[:, :, 0:width], buf[:, :, 0:width], buf[:, :, width:2 * width], ALU.add))
                settle()
            dve.wait_ge(fold_done, IMAGES + 23)
            nc.vector.tensor_tensor(T[:, 12:16, :], T[:, 12:16, :], buf[:, :, 0:C], ALU.add).then_inc(fold_done, 1)
            output(3)

        @block.tensor
        def _(pe):
            mm = nc.tensor.matmul

            pe.wait_ge(const_loaded, 16)
            pe.wait_ge(moments_ready, 1)
            mm(PS[:, 7, 0:2 * J], c_("pair_mean"), mv[:, 0].rearrange("p j m -> p (j m)"), start=True, stop=True).then_inc(group_moments_ready, 1)
            pe.wait_ge(wo_ready, 2)
            for r in range(2):
                for part, ready, image in ((0, ghp_ready, GHP), (1, glp_ready, GLP)):
                    pe.wait_ge(ready, 2 * r + 2)
                    for k in range(TAPS):
                        ky, kx = divmod(k, 3)
                        ins = mm(PS[0:4 * NOFF, 5 + r, :], WO[:, k, :], image[:, 2 * r:2 * r + 2, ky:ky + HH, kx:kx + WW],
                                 start=(part + k == 0), stop=(part == 1 and k == TAPS - 1))
                ins.then_inc(offset_conv_ready, 1)
            for ip in range(NP):
                j, pt = divmod(ip, PT)
                pe.wait_ge(ot_ready, j // 2 + 1)
                ins = mm(PS[:, 0, ip * 2 * NOFF:(ip + 1) * 2 * NOFF], OT[0:4 * NOFF, j, pt * P:(pt + 1) * P],
                         cst[0:4 * NOFF, CONST["part_sum"]], start=True, stop=True)
            ins.then_inc(offsets_ready, 1)
            pe.wait_ge(dl_ready, 1)
            pe.wait_ge(gl_ready, J)
            for ip in range(NP):
                j, pt = divmod(ip, PT)
                for h in range(2):
                    n = 2 * ip + h
                    m = n - 3
                    if m in (0, 1) or m >= 0 and m % 2 == 0:
                        pe.wait_ge(u_copied, m + 1 if m < 2 else m // 2 + 2)
                    elif m >= 3:
                        pe.wait_ge(u_copied_dve, m // 2)
                    hs = slice(h * C, (h + 1) * C)
                    px = slice(pt * P, (pt + 1) * P)
                    for r, (gg, ww) in enumerate(((GH, DH), (GH, DL), (GL, DH))):
                        for a in range(2):
                            ins = mm(PS[:, 1 + 2 * (n % 3) + a, 0:288], gg[hs, j, px], ww[hs, a * 288:(a + 1) * 288],
                                     start=(r == 0), stop=(r == 2))
                    ins.then_inc(u_ready, 1)

            def dT(ip):
                pe.wait_ge(d_copied, ip + 1)
                if ip >= 2:
                    pe.wait_ge(x1_tile_ready, ip - 1)
                nc.tensor.transpose(PS[:, 7 * (ip % 2), 0:P], D[:, ip % 2, :], ident).then_inc(dT_ready, 1)

            pe.wait_ge(u_copied, NT // 2 + 1)
            pe.wait_ge(u_copied_dve, NT // 2 - 1)
            for n in range(NT + 1):
                for g in range(NG):
                    if n < NT:
                        m = n * NG + g
                        if g == 0:
                            pe.wait_ge(prod_ready, n + 1)
                        if m >= 4:
                            pe.wait_ge(st_copied, m - 3)
                        for a in range(STG[g]):
                            k, qt = divmod(4 * g + a, 2)
                            ins = nc.tensor.transpose(PS[:, 1 + m % 4, a * P:(a + 1) * P], prods[n % 2][:, k, qt * P:(qt + 1) * P], ident)
                        ins.then_inc(st_ready, 1)
                    if n >= 1:
                        v = n - 1
                        ip, h = divmod(v, 2)
                        b = h * J + ip // 2
                        pe.wait_ge(st_copied, v * NG + g + 1)
                        if h == 0 and ip >= 2 and g == 0:
                            pe.wait_ge(d_copied, ip - 1)
                        for a in range(STG[g]):
                            k, qt = divmod(4 * g + a, 2)
                            ins = mm(PS[:, 5 + ip % 2, h * C:(h + 1) * C], ST[v % 2][:, 4 * g + a, :],
                                     U[:, 2 * (2 * (ip // 2) + qt) + h, k * C:(k + 1) * C],
                                     start=(g + a == 0), stop=(4 * g + a == 2 * TAPS - 1))
                        if g == NG - 1:
                            ins.then_inc(d_ready, 1)
                if n >= 4 and n % 2 == 0:
                    dT(n // 2 - 2)
            dT(NP - 1)

            pe.wait_ge(x1_tile_ready, NP)
            pe.wait_ge(moments_ready, 2)
            mm(PS[:, 7, 0:2 * J], c_("pair_mean"), mv[:, 1].rearrange("p j m -> p (j m)"), start=True, stop=True).then_inc(group_moments_ready, 1)
            pe.wait_ge(sq_ready, 1)
            mm(PS[:, 3, 0:J], c_("half_mean"), small[:, 20:20 + J], start=True, stop=True).then_inc(q_ready, 1)
            pe.wait_ge(conv_block_loaded, 32)

            def conv(r):
                pe.wait_ge(g_ready, J + 2 * r + 2)
                for k in range(TAPS):
                    ky, kx = divmod(k, 3)
                    ins = mm(PS[:, 1 + r, :], w_conv[:, k, :], G2[:, 2 * r:2 * r + 2, ky:ky + HH, kx:kx + WW],
                             start=(k == 0), stop=(k == TAPS - 1))
                ins.then_inc(conv_ready, 1)

            pe.wait_ge(pb_ready, 2)
            mm(PS[0:B, 3, 0:NPHI], PB[:], weff[:], start=True, stop=True).then_inc(coef_ready, 1)
            conv(0)
            pe.wait_ge(v3_ready, 1)
            spread = cst[0:B, CONST["sel_half"]]
            mm(PS[:, 3, 32:32 + 2 * J].rearrange("p (j k) -> p j k", k=2), spread, V3[0:B, :, 1:3], start=True, stop=True).then_inc(cb_ready, 1)
            conv(1)
            pe.wait_ge(wat_loaded, 16)
            for g in range(HEADS):
                odd, hp = divmod(g, HPAIRS)
                hs = slice(odd * C, (odd + 1) * C)
                mm(PS[:, 4 + odd, hp * P:(hp + 1) * P], wa[hs, WAT["q"]][:, hp * P:(hp + 1) * P],
                   wa[hs, WAT["k"]][:, hp * C:(hp + 1) * C].unsqueeze(1).to_broadcast([C, 2, C]), start=True, stop=True)
            for g in range(HEADS):
                odd, hp = divmod(g, HPAIRS)
                hs = slice(odd * C, (odd + 1) * C)
                ins = mm(PS[:, 6 + odd, hp * C:(hp + 1) * C], wa[hs, WAT["v"]][:, hp * P:(hp + 1) * P],
                         wa[hs, WAT["p"]][:, hp * C:(hp + 1) * C], start=True, stop=True)
            ins.then_inc(av_ready, 1)
            pe.wait_ge(v3_diag_ready, 1)
            mm(PS[:, 0, 0:J], spread, V3[0:B, :, 0], start=True, stop=True).then_inc(cb_ready, 1)

            fills = [0]

            def take(*name):
                assert FILLS[fills[0]] == name, (FILLS[fills[0]], name)
                if fills[0]:
                    pe.wait_ge(misc_free, fills[0])
                else:
                    pe.wait_ge(avh_ready, 4)
                fills[0] += 1

            def transpose_x(j):
                pe.wait_ge(x2_ready, j + 1)
                take("xT", j)
                for pt in range(PT):
                    ins = nc.tensor.transpose(PS[:, 7, pt * P:(pt + 1) * P], X1[:, j, pt * P:(pt + 1) * P], ident)
                ins.then_inc(misc_filled, 1)

            yts = [0]

            def transpose_y(name, c):
                yts[0] += 1
                pe.wait_ge(y2_ready, yts[0])
                take(name, c)
                for q in range(CHUNK):
                    ins = nc.tensor.transpose(PS[:, 7, q * P:(q + 1) * P], Y2[:, 4 * c + q, :], ident)
                ins.then_inc(misc_filled, 1)

            def project(name):
                kind, a, i = name
                if not on_side(name):
                    take(*name)
                elif SIDE[name]:
                    pe.wait_ge(side_free, SIDE[name])
                bank = 2 if on_side(name) else 7
                if kind == "q":
                    for g in (2 * i, 2 * i + 1):
                        for r, w in enumerate((AVH, AVL)):
                            ins = mm(PS[:, bank, (g % 2) * S:(g % 2 + 1) * S], w[:, g * P:(g + 1) * P], YTs[:, a * S:(a + 1) * S],
                                     start=(r == 0), stop=(r == 1))
                else:
                    for r, w in enumerate((AVH, AVL)):
                        ins = mm(PS[:, bank, :], YTs[:, (2 * a + i) * P:(2 * a + i + 1) * P], w[:, 2 * 512:3 * 512], start=(r == 0), stop=(r == 1))
                ins.then_inc(side_filled if on_side(name) else misc_filled, 1)

            def small_projection(name, c, weight, width):
                take(name, c)
                at, n = SW[weight][0], 2 * width
                for q in range(CHUNK):
                    t = 4 * c + q
                    ins = mm(PS[:, 7, q * n:(q + 1) * n], YTs[:, t * P:(t + 1) * P], sw[:, 2 * at:2 * at + n], start=True, stop=True)
                ins.then_inc(misc_filled, 1)

            def window(c):
                pe.wait_ge(wx_ready, c + 1)
                take("wC", c)
                n = 2 * (C + 1)
                wxv = WX[:].rearrange("p (h t) c -> p t h c", t=PT)
                mm(PS[:, 7, 0:n], c_("band"), wxv[:, 0], start=True, stop=True)
                mm(PS[:, 7, n:2 * n], c_("band"), wxv[:, 1], start=True, stop=False)
                mm(PS[:, 7, n:2 * n], c_("band_prev"), wxv[:, 0], start=False, stop=True).then_inc(misc_filled, 1)

            def result(c):
                pe.wait_ge(fold_done, IMAGES + 8 + 4 * (c + 1))
                take("oT", c)
                for h in range(2):
                    t = 4 * c + 2 * h
                    ins = nc.tensor.transpose(PS[:, 7, h * P:(h + 1) * P], T[:, t:t + 2, :].rearrange("p t c -> p (t c)"), ident)
                ins.then_inc(misc_filled, 1)

            transpose_x(0)
            transpose_y("yA", 0)
            pe.wait_ge(avl_ready, 1)
            pe.wait_ge(misc_free, FILL["yA", 0] + 1)
            for name in FIRST_PROJECTIONS:
                project(name)
            transpose_x(1)

            def wait_projection(name):
                if on_side(name):
                    pe.wait_ge(side_free, SIDE[name] + 1)
                else:
                    pe.wait_ge(misc_free, FILL[name] + 1)

            def scores(s):
                a, g = divmod(s, HEADS)
                if g % 2 == 0:
                    wait_projection(("q", a, g // 2))
                if s >= 2:
                    pe.wait_ge(masked_ready, s - 1)
                for qt in range(PT):
                    cols = slice(0, P) if qt == 0 else slice(P, 3 * P)
                    for r, w in enumerate((QH, QL)):
                        ins = mm(PS[:, s % 2, cols], w[:, a % 2, g, qt * P:(qt + 1) * P], YTs[:, a * S:a * S + (qt + 1) * P],
                                 start=(r == 0), stop=(r == 1))
                ins.then_inc(scores_ready, 1)

            scores(0)
            for s in range(STEPS + 2):
                if 1 <= s <= STEPS:
                    v = s - 1
                    pe.wait_ge(probs_ready, v + 1)
                    if v >= 2:
                        pe.wait_ge(pT_copied, v - 1)
                    for k in range(3):
                        ins = nc.tensor.transpose(PS[:, 3 + v % 2, k * P:(k + 1) * P], PR[:, v % 3, k * P:(k + 1) * P], ident)
                    ins.then_inc(pT_ready, 1)
                if s + 1 < STEPS:
                    scores(s + 1)
                if s >= 2:
                    v = s - 2
                    a, g = divmod(v, HEADS)
                    if g % 4 == 0 and a >= 1:
                        pe.wait_ge(heads_normed, 2 * a - 1 + g // 4)
                    if g == 0:
                        wait_projection(("v", a, 0))
                        wait_projection(("v", a, 1))
                    pe.wait_ge(pT_copied, v + 1)
                    vh = slice(g * C, (g + 1) * C)
                    o = PS[:, 5 + g // 4, (g % 4) * P:(g % 4 + 1) * P]
                    mm(o[:, 0:C], PTs[:, v % 3, 0:P], VV[:, a % 2, 0, vh], start=True, stop=True)
                    mm(o[:, C:P], PTs[:, v % 3, P:2 * P], VV[:, a % 2, 0, vh], start=True, stop=False)
                    mm(o[:, C:P], PTs[:, v % 3, 2 * P:3 * P], VV[:, a % 2, 1, vh], start=False, stop=True).then_inc(pv_done, 1)
                if s < STEPS:
                    for what in attention_fills(s):
                        if what[0] in ("q", "v"):
                            project(what)
                        elif what[0] in ("yA", "yB"):
                            transpose_y(*what)
                        elif what[0] == "xT":
                            transpose_x(what[1])
                        else:
                            pe.wait_ge(swl_ready, 3)
                            small_projection(*what, "wg2", E2)

            def more(what):
                kind, c = what
                if kind in ("yB", "yC", "yD"):
                    transpose_y(kind, c)
                elif kind == "gB":
                    small_projection(kind, c, "wg2", E2)
                elif kind == "pC":
                    small_projection(kind, c, "wp", A3)
                elif kind == "gD":
                    small_projection(kind, c, "wg3", E3)
                elif kind == "wC":
                    window(c)
                else:
                    result(c)

            def accumulator(u, q, e):
                at = (q % 2) * UNIT * C + e * C
                return PS[:, 3 + 2 * (u % 2) + q // 2, at:at + C]

            pe.wait_ge(masked_ready, STEPS)
            pe.wait_ge(stage_split, 3)
            pe.wait_ge(b2s_ready, 1)
            pe.wait_ge(w128_loaded, 16)
            N2 = 4 * E2 * 2
            for n in range(N2 + 2):
                if n < N2:
                    c, r = divmod(n, 2 * E2)
                    if n == 48:
                        pe.wait_ge(misc_free, FILL["yB", 3] + 1)
                    if n >= 3:
                        pe.wait_ge(gelu_done, n - 2)
                    for k, w in enumerate((WH, WL)):
                        ins = mm(PS[:, n % 3, :], w[:, 0, r * P:(r + 1) * P], YTs[:, c * CW:(c + 1) * CW], start=(k == 0), stop=(k == 1))
                    ins.then_inc(hid2_ready, 1)
                if n >= 2:
                    v = n - 2
                    c, r = divmod(v, 2 * E2)
                    e, ht = divmod(r, 2)
                    u = v // (2 * UNIT)
                    if v == 2 * UNIT:
                        pe.wait_ge(heads_normed, 2 * IMAGES)
                    if v % (2 * UNIT) == 0:
                        for i in range(2):
                            if u >= 2:
                                pe.wait_ge(acc_free, 2 * (u - 2) + i + 1)
                            mm(PS[:, 3 + 2 * (u % 2) + i, :].rearrange("p (q n) -> p q n", q=2), ones[:],
                               b2s[:, (u % 2) * UNIT * C:(u % 2 + 1) * UNIT * C].unsqueeze(1).to_broadcast([P, 2, UNIT * C]),
                               start=True, stop=False, skip_group_check=True)
                    pe.wait_ge(gelu_done, v + 1)
                    for q in range(CHUNK):
                        ins = mm(accumulator(u, q, e % UNIT), hid[:, v % 3, q * P:(q + 1) * P],
                                 wk[:, W128["w2_2"]][:, r * C:(r + 1) * C], start=False, stop=(v % (2 * UNIT) == 2 * UNIT - 1), skip_group_check=True)
                    ins.then_inc(out2_done, 1)
                if n in FIRST_FILLS:
                    more(FIRST_FILLS[n])

            N3 = 4 * E3

            def second_out(v):
                c, e = divmod(v, E3)
                u = 8 + v // UNIT
                pe.wait_ge(prod3_done, v + 1)
                for q in range(CHUNK):
                    if v % UNIT == 0:
                        pe.wait_ge(acc_free, 2 * (u - 2) + q // 2 + 1)
                    ins = mm(accumulator(u, q, e % UNIT), hid[:, v % 3, q * P:(q + 1) * P],
                             wk[:, W128["w3"]][:, e * C:(e + 1) * C], start=True, stop=True)
                ins.then_inc(out3_done, 1)

            for n in range(N3 + 2):
                if n < N3:
                    c, e = divmod(n, E3)
                    if e == 0:
                        pe.wait_ge(misc_free, FILL["yD", c] + 1)
                    for a in range(2):
                        if a == 0 and n >= 2:
                            pe.wait_ge(prod3_done, n - 1)
                        if a == 1 and n >= 1:
                            pe.wait_ge(silu_done, n)
                        for k, w in enumerate((WH, WL)):
                            ins = mm(PS[:, (2 * n + a) % 3, :], w[:, 1 + a, e * P:(e + 1) * P], YTs[:, c * CW:(c + 1) * CW],
                                     start=(k == 0), stop=(k == 1))
                        ins.then_inc(hid3_ready, 1)
                        if a == 0 and n >= 2:
                            second_out(n - 2)
                else:
                    second_out(n - 2)
                if n in SECOND_FILLS:
                    more(SECOND_FILLS[n])
            result(3)


def pack(widths, total, parts, height):
    a = np.zeros((height, total), np.float32)
    for name, v in parts.items():
        a[:, widths[name]] = np.asarray(v).reshape(height, -1)
    return a


def kernel(**inputs):
    import concourse.bacc as bacc
    from concourse.bass_utils import run_bass_kernel_spmd

    i = {k: np.asarray(v) for k, v in inputs.items()}

    def taps(w):
        return w.transpose(1, 2, 3, 0).reshape(C, -1)

    def heads(w, times):
        w = w.reshape(C, HPAIRS, P).transpose(2, 1, 0)
        return np.stack([w] * times, 2)

    qkv = i["L2_attn_w_qkv"].reshape(C, 3, HEADS * C)
    arrays = {
        "x": i["x"].reshape(B, C, S),
        "w64": pack(W64, NW64, {
            "w_dcn": taps(i["L0_conv_w_dcn"]), "conv_b": i["L1_conv_conv_b"], "b_dcn": i["L0_conv_b_dcn"],
            "phi": i["L1_conv_phi_w"].reshape(NPHI, STREAMS, C).transpose(2, 1, 0),
            "rms": i["L1_conv_rms_w"].reshape(STREAMS, C).T,
            "wg2": i["L2_ffn_Wg"], "wp": i["L3_attn_Wp"].T, "wg3": i["L3_ffn_gate_w"]}, C),
        "wcv": pack(WCV, NWCV, {"w_off": taps(i["L0_conv_w_off"]), "w_conv": taps(i["L1_conv_conv_w"])}, C),
        "wat": pack(WAT, NWAT, {"q": heads(qkv[:, 0], 2), "k": heads(qkv[:, 1], 1), "v": heads(qkv[:, 2], 2),
                                "p": i["L2_attn_w_proj"].reshape(HPAIRS, P, C).transpose(1, 0, 2)}, P),
        "w128": pack(W128, NW128, {
            "b1": i["L2_ffn_b1"].reshape(E2 * 2, P).T,
            "w2_2": i["L2_ffn_W2"].reshape(E2 * 2, P, C).transpose(1, 0, 2),
            "w3": i["L3_ffn_w3"].transpose(1, 0, 2)}, P),
        "wexp": np.stack([i[k].transpose(1, 0, 2).reshape(C, -1) for k in ("L2_ffn_W1", "L3_ffn_w1", "L3_ffn_w2")]),
        "rows": pack(ROWS, NROWS, {
            "b_off": i["L0_conv_b_off"], "b_proj": i["L2_attn_b_proj"], "bg2": i["L2_ffn_bg"], "bp": i["L3_attn_bp"],
            "wg": i["L3_attn_Wg"], "bg3": i["L3_ffn_gate_b"], "phi_b": i["L1_conv_phi_b"],
            "alpha": np.concatenate([i["L1_conv_alpha_pre"], i["L1_conv_alpha_post"], i["L1_conv_alpha_res"]])}, 1),
        "b2": i["L2_ffn_b2"].reshape(1, -1),
        "consts": shape_constants(),
    }
    nc = bacc.Bacc("TRN2", target_bir_lowering=False, num_devices=1)
    feeds, args = {}, []
    for name, a in arrays.items():
        feeds[f"in_{name}"] = np.ascontiguousarray(a)
        args.append(nc.dram_tensor(f"in_{name}", list(a.shape), F32, kind="ExternalInput").ap())
    result = nc.dram_tensor("out_0", [B, C, S], F32, kind="ExternalOutput").ap()
    hybrid_kernel(nc, *args, result)
    r = run_bass_kernel_spmd(nc, [feeds], core_ids=[0])
    return r.results[0]["out_0"].reshape(B, C, HH, WW)
```
